# Optimizing a Trainium2 kernel written in Bass

```python
import numpy as np
import jax
import jax.numpy as jnp

def _softmax(x, axis=-1):
    return jax.nn.softmax(x, axis=axis)

def _gelu(x):
    return jax.nn.gelu(x, approximate=True)

def _silu(x):
    return jax.nn.silu(x)

def _sigmoid(x):
    return jax.nn.sigmoid(x)

def _layernorm(x, axis=-1, eps=1e-05):
    m = jnp.mean(x, axis=axis, keepdims=True)
    v = jnp.var(x, axis=axis, keepdims=True)
    return (x - m) / jnp.sqrt(v + eps)

def _scatter_add(tgt, idx, src, axis=0):
    return tgt.at[idx].add(src)

def _segment_sum(src, seg, n):
    return jax.ops.segment_sum(src, seg, n)
kernel_name = 'mk_gnn_resnorm_d2_gnn_r8_2af422'

def setup_inputs(seed: int=0):
    np.random.seed(seed)
    _w = jnp.asarray

    def _rec_inputs():
        import jax
        import jax.numpy as jnp
        _gk = jax.random.key(seed)
        x = -0.0003713 + 1 * jax.random.normal(jax.random.fold_in(_gk, 1), (12500, 128), jnp.float32)
        src = jax.random.randint(jax.random.fold_in(_gk, 2), (200000,), 0, 12500, jnp.int32)
        dst = jnp.minimum((12500 * jax.random.uniform(jax.random.fold_in(_gk, 3), (200000,)) ** 2.0).astype(jnp.int32), 99999)
        _o = jnp.argsort(dst, stable=True)
        src = src[_o]
        dst = dst[_o]
        edge_attr_128 = 9.41057e-06 + 1 * jax.random.normal(jax.random.fold_in(_gk, 11), (200000, 128), jnp.float32)
        return (x, src, dst, edge_attr_128)
    x, src, dst, edge_attr_128 = _rec_inputs()

    def _L0_gnn_setup():
        import jax, jax.numpy as jnp
        import numpy as np
        N_NODES = 12500
        N_EDGES = 200000
        D = 128
        BN_EPS = 1e-05
        key = jax.random.key(seed)
        ks = jax.random.split(key, 8)
        x = jax.random.normal(ks[0], (N_NODES, D), dtype=jnp.float32)
        edge_index = jax.random.randint(ks[1], (2, N_EDGES), 0, N_NODES, dtype=jnp.int64)
        glorot = (6.0 / (D + D)) ** 0.5
        W1 = jax.random.uniform(ks[2], (D, D), jnp.float32, -glorot, glorot)
        b1 = jnp.zeros((D,), jnp.float32)
        W2 = jax.random.uniform(ks[3], (D, D), jnp.float32, -glorot, glorot)
        b2 = jnp.zeros((D,), jnp.float32)
        bn_gamma = jnp.ones((D,), jnp.float32)
        bn_beta = jnp.zeros((D,), jnp.float32)
        bn_mean = 0.1 * jax.random.normal(ks[4], (D,), jnp.float32)
        bn_var = 0.5 + jax.random.uniform(ks[5], (D,), jnp.float32)
        return {'x': x, 'edge_index': edge_index, 'W1': W1, 'b1': b1, 'W2': W2, 'b2': b2, 'bn_gamma': bn_gamma, 'bn_beta': bn_beta, 'bn_mean': bn_mean, 'bn_var': bn_var}
    _L0_gnn_all = _L0_gnn_setup()
    _L0_gnn_in = {k: v for k, v in _L0_gnn_all.items() if k in ('W1', 'b1', 'W2', 'b2', 'bn_gamma', 'bn_beta', 'bn_mean', 'bn_var')}
    del _L0_gnn_all

    def _L1_gnn_setup():
        import jax, jax.numpy as jnp
        import numpy as np
        HIDDEN = 128
        HEADS = 8
        HEAD_DIM = HIDDEN // HEADS
        N_NODES = 12500
        N_EDGES = 200000
        key = jax.random.key(seed)
        ks = jax.random.split(key, 12)
        s = 1.0 / np.sqrt(HIDDEN)
        inp = {'x': jax.random.normal(ks[0], (N_NODES, HIDDEN), dtype=jnp.float32), 'edge_index': jax.random.randint(ks[1], (2, N_EDGES), 0, N_NODES, dtype=jnp.int32), 'edge_emb': jax.random.normal(ks[2], (N_EDGES, HIDDEN), dtype=jnp.float32), 'q_w': jax.random.uniform(ks[3], (HIDDEN, HIDDEN), jnp.float32, -s, s), 'q_b': jax.random.uniform(ks[4], (HIDDEN,), jnp.float32, -s, s), 'k_w': jax.random.uniform(ks[5], (HIDDEN, HIDDEN), jnp.float32, -s, s), 'k_b': jax.random.uniform(ks[6], (HIDDEN,), jnp.float32, -s, s), 'v_w': jax.random.uniform(ks[7], (HIDDEN, HIDDEN), jnp.float32, -s, s), 'v_b': jax.random.uniform(ks[8], (HIDDEN,), jnp.float32, -s, s), 'out_w': jax.random.uniform(ks[9], (HIDDEN, HIDDEN), jnp.float32, -s, s), 'out_b': jax.random.uniform(ks[10], (HIDDEN,), jnp.float32, -s, s), 'eb_w': jax.random.uniform(ks[11], (HEADS, HIDDEN), jnp.float32, -s, s), 'eb_b': jnp.zeros((HEADS,), dtype=jnp.float32)}
        return inp
    _L1_gnn_all = _L1_gnn_setup()
    _L1_gnn_in = {k: v for k, v in _L1_gnn_all.items() if k in ('q_w', 'q_b', 'k_w', 'k_b', 'v_w', 'v_b', 'out_w', 'out_b', 'eb_w', 'eb_b')}
    del _L1_gnn_all
    return {'x': x, 'src': src, 'dst': dst, 'edge_attr_128': edge_attr_128, 'L0_gnn_W1': _L0_gnn_in['W1'], 'L0_gnn_b1': _L0_gnn_in['b1'], 'L0_gnn_W2': _L0_gnn_in['W2'], 'L0_gnn_b2': _L0_gnn_in['b2'], 'L0_gnn_bn_gamma': _L0_gnn_in['bn_gamma'], 'L0_gnn_bn_beta': _L0_gnn_in['bn_beta'], 'L0_gnn_bn_mean': _L0_gnn_in['bn_mean'], 'L0_gnn_bn_var': _L0_gnn_in['bn_var'], 'L1_gnn_q_w': _L1_gnn_in['q_w'], 'L1_gnn_q_b': _L1_gnn_in['q_b'], 'L1_gnn_k_w': _L1_gnn_in['k_w'], 'L1_gnn_k_b': _L1_gnn_in['k_b'], 'L1_gnn_v_w': _L1_gnn_in['v_w'], 'L1_gnn_v_b': _L1_gnn_in['v_b'], 'L1_gnn_out_w': _L1_gnn_in['out_w'], 'L1_gnn_out_b': _L1_gnn_in['out_b'], 'L1_gnn_eb_w': _L1_gnn_in['eb_w'], 'L1_gnn_eb_b': _L1_gnn_in['eb_b']}

def reference(x, src, dst, edge_attr_128, L0_gnn_W1, L0_gnn_b1, L0_gnn_W2, L0_gnn_b2, L0_gnn_bn_gamma, L0_gnn_bn_beta, L0_gnn_bn_mean, L0_gnn_bn_var, L1_gnn_q_w, L1_gnn_q_b, L1_gnn_k_w, L1_gnn_k_b, L1_gnn_v_w, L1_gnn_v_b, L1_gnn_out_w, L1_gnn_out_b, L1_gnn_eb_w, L1_gnn_eb_b):
    import jax
    import jax.numpy as jnp

    def _L0_gnn_ref(x, edge_index, W1, b1, W2, b2, bn_gamma, bn_beta, bn_mean, bn_var):
        import jax, jax.numpy as jnp
        import numpy as np
        N_NODES = 12500
        N_EDGES = 200000
        D = 128
        BN_EPS = 1e-05
        N = x.shape[0]
        src, dst = (edge_index[0], edge_index[1])
        mask = (src != dst).astype(x.dtype)
        deg = jax.ops.segment_sum(mask, dst, num_segments=N) + 1.0
        dinv = deg ** (-0.5)
        edge_w = dinv[src] * dinv[dst] * mask
        self_w = 1.0 / deg

        def spmm(h):
            msg = h[src] * edge_w[:, None]
            agg = jax.ops.segment_sum(msg, dst, num_segments=N)
            return agg + self_w[:, None] * h
        h = x @ W1 + b1
        h = spmm(h)
        h = (h - bn_mean) * jax.lax.rsqrt(bn_var + BN_EPS) * bn_gamma + bn_beta
        h = jax.nn.relu(h)
        h = h @ W2 + b2
        h = spmm(h)
        return h

    def _L1_gnn_ref(x, edge_index, edge_emb, q_w, q_b, k_w, k_b, v_w, v_b, out_w, out_b, eb_w, eb_b):
        import jax, jax.numpy as jnp
        import numpy as np
        HIDDEN = 128
        HEADS = 8
        HEAD_DIM = HIDDEN // HEADS
        N_NODES = 12500
        N_EDGES = 200000
        n = x.shape[0]
        q = (x @ q_w.T + q_b).reshape(n, HEADS, HEAD_DIM)
        k = (x @ k_w.T + k_b).reshape(n, HEADS, HEAD_DIM)
        v = (x @ v_w.T + v_b).reshape(n, HEADS, HEAD_DIM)
        row, col = (edge_index[0], edge_index[1])
        scores = jnp.einsum('ehd,ehd->eh', q[row], k[col]) / jnp.sqrt(jnp.float32(HEAD_DIM))
        scores = scores + edge_emb @ eb_w.T + eb_b
        seg_max = jax.ops.segment_max(scores, row, num_segments=n)
        exp_scores = jnp.exp(scores - seg_max[row])
        seg_sum = jax.ops.segment_sum(exp_scores, row, num_segments=n)
        attn = exp_scores / (seg_sum[row] + 1e-10)
        weighted_v = attn[..., None] * v[col]
        out = jax.ops.segment_sum(weighted_v, row, num_segments=n)
        out = out.reshape(n, HIDDEN)
        return out @ out_w.T + out_b
    edge_index = jnp.stack([src, dst])
    x = _layernorm(x + _L0_gnn_ref(x, edge_index, L0_gnn_W1, L0_gnn_b1, L0_gnn_W2, L0_gnn_b2, L0_gnn_bn_gamma, L0_gnn_bn_beta, L0_gnn_bn_mean, L0_gnn_bn_var), axis=-1)
    x = _layernorm(x + _L1_gnn_ref(x, edge_index, edge_attr_128, L1_gnn_q_w, L1_gnn_q_b, L1_gnn_k_w, L1_gnn_k_b, L1_gnn_v_w, L1_gnn_v_b, L1_gnn_out_w, L1_gnn_out_b, L1_gnn_eb_w, L1_gnn_eb_b), axis=-1)
    return x

_drawn_inputs = setup_inputs


def setup_inputs(seed=0):
    import zlib

    import numpy as np

    out = dict(_drawn_inputs(seed))
    spreads = {'L0_gnn_b1': (0.0, 0.1),
     'L0_gnn_b2': (0.0, 0.1),
     'L0_gnn_bn_gamma': (1.0, 0.2),
     'L0_gnn_bn_beta': (0.0, 0.1),
     'L1_gnn_eb_b': (0.0, 0.8)}
    factors = {'L1_gnn_q_b': 8.0, 'L1_gnn_k_b': 8.0}
    for name, (base, spread) in spreads.items():
        noise = np.random.default_rng([zlib.crc32(name.encode()), seed]).standard_normal(out[name].shape)
        drawn = base * np.exp(spread * noise) if base else spread * noise
        out[name] = jnp.asarray(drawn.astype(out[name].dtype))
    for name, factor in factors.items():
        out[name] = (out[name] * factor).astype(out[name].dtype)
    return out
```

```python
from contextlib import ExitStack, contextmanager

import concourse.bass as bass
from concourse import mybir

F32, I32, BF16 = mybir.dt.float32, mybir.dt.int32, mybir.dt.bfloat16
ALU, ACT, AX = mybir.AluOpType, mybir.ActivationFunctionType, mybir.AxisListType

P = 128
N_NODES, N_EDGES, D = 12500, 200000, 128
HEADS = 8
HEAD_DIM = D // HEADS
NT = -(-N_NODES // P)
LAST_ROWS = N_NODES - (NT - 1) * P
PAD_NODE = NT * P - 1
HALF = 8
TURN = 2 * HALF
E_COLS = -(-N_EDGES // (P * TURN)) * TURN
E_TURNS = E_COLS // TURN
LAST_COLS = N_EDGES - (P - 1) * E_COLS
CHUNKS = P // HEADS
S_TILES = -(-(E_COLS + NT - 1) // TURN) * TURN
S_TURNS = S_TILES // TURN
CHUNK_TILES = S_TILES // CHUNKS
CHUNK_LEN = CHUNK_TILES * P
AHEAD = 4
D_FIELDS, S_FIELDS = 2, 2 + HEADS
EMPTY_KEY = -0.5
NO_KEY = -30000.0
WINDOWS = 120
W_BLOCKS = S_TILES // WINDOWS
LN_EPS = BN_EPS = 1e-5
SUM_EPS = 1e-10
BREAK = -1e30
CLAMPED = "node tiles are clamped to the last one where the table is built"

assert W_BLOCKS * WINDOWS == S_TILES and CHUNK_TILES * CHUNKS == S_TILES and LAST_COLS % TURN == 0
FULL_TURNS = LAST_COLS // TURN


def need(eng, sem, value):
    if isinstance(value, int) and value <= 0:
        return
    eng.wait_ge(sem, value)


@contextmanager
def phase_semaphores(nc):
    taken = []

    def sem(name):
        taken.append(nc.alloc_semaphore(name=name))
        return taken[-1]

    yield sem
    nc.clear_and_free_semaphores(taken)
    nc.all_engine_barrier()


class Chain:

    def __init__(self, eng, sem):
        self.eng, self.sem, self.base, self.k = eng, sem, 0, 0

    def turn(self, base):
        self.base, self.k = base, 0

    def __call__(self, ins):
        ins.then_inc(self.sem, 1)
        self.k += 1
        self.eng.wait_ge(self.sem, self.base + self.k)


def gnn(nc, x, src, dst, attr, w1, b1, w2, b2, gamma, beta, bn_mean, bn_var,
        q_w, q_b, k_w, k_b, v_w, v_b, out_w, out_b, eb_w, eb_b, out):
    dram = lambda name, shape: nc.dram_tensor(name, shape, F32).ap()
    h_table = [dram("h1_table", (NT * P, D)), dram("h2_table", (NT * P, D))]
    kv_table = dram("kv_table", (NT * P, 2 * D))
    x1_dram = dram("x1_dram", (NT * P, D))
    v_sorted = dram("v_sorted", (P, S_TILES, D))
    edge_src, edge_key = dram("edge_src", (S_TILES, P)), dram("edge_key", (S_TILES, P))
    d_slots = dram("d_slots", (P * S_TILES, D_FIELDS))
    s_slots = dram("s_slots", (P * S_TILES, S_FIELDS))

    whole = ExitStack()
    with whole:
        def sb(name, shape, dt=F32):
            return whole.enter_context(nc.sbuf_tensor(name, shape, dt))

        bank = [whole.enter_context(nc.psum_tensor(f"bank{i}", [P, 512], F32)) for i in range(8)]

        iota_bf = sb("iota_bf", [P, P], BF16)
        iota_half = sb("iota_half", [P, P], BF16)
        iota_p = sb("iota_p", [P, 1])
        ident = sb("ident", [P, P])
        ident_bf = sb("ident_bf", [P, P], BF16)
        before = sb("before", [P, P])
        before_bf = sb("before_bf", [P, P], BF16)
        next_row = sb("next_row", [P, P])
        wrap_row = sb("wrap_row", [P, P])
        ones = sb("ones", [P, P])
        zeros_bf = sb("zeros_bf", [P, P], BF16)
        eps_col = sb("eps_col", [P, 1])
        w1_sb, w2_sb = sb("w1_sb", [D, D]), sb("w2_sb", [D, D])
        qkv_t, out_t, eb_t = sb("qkv_t", [D, 3 * D]), sb("out_t", [D, D]), sb("eb_t", [D, HEADS])
        b1_bc, b2_bc, out_bc = sb("b1_bc", [P, D]), sb("b2_bc", [P, D]), sb("out_bc", [P, D])
        qkv_bc = sb("qkv_bc", [P, 3 * D])
        ebb_bc = sb("ebb_bc", [P, HALF, HEADS])
        bn_cols = sb("bn_cols", [D, 4])
        bn_scale, bn_shift = sb("bn_scale", [D, 1]), sb("bn_shift", [D, 1])
        dinv = sb("dinv", [P, NT])
        base_d, base_s = sb("base_d", [NT, P]), sb("base_s", [NT, P])
        S_ROW = 32
        node_rows = sb("node_rows", [S_ROW + 1, S_TILES], I32)
        node_d, node_s = node_rows[0:1, :], node_rows[S_ROW:S_ROW + 1, :]
        unsorted = sb("unsorted", [1, 1], I32)
        window_row, window_node = sb("window_row", [P, W_BLOCKS], I32), sb("window_node", [P, W_BLOCKS])
        node_s_bc = sb("node_s_bc", [P, S_TILES], BF16)
        lo_slots = sb("lo_slots", [P, S_TILES + AHEAD])
        lo_slots_bf = sb("lo_slots_bf", [P, S_TILES + AHEAD], BF16)
        mean_var = sb("mean_var", [P, NT, 2])
        rstd = sb("rstd", [P, NT])
        slots_words = S_TILES * S_FIELDS
        region_a = sb("region_a", [P, slots_words])
        region_b = sb("region_b", [P, max(CHUNK_LEN, NT * (D + HEADS))])
        region_c = sb("region_c", [P, max(S_TILES * D_FIELDS, CHUNK_LEN // 2 + 1)])
        EC = E_COLS + AHEAD
        at = [0]

        def part(words):
            at[0] += words
            return region_a[:, at[0] - words:at[0]]

        src_i, dst_i = part(E_COLS).bitcast(I32), part(E_COLS).bitcast(I32)
        s_hi, s_lo, d_hi, d_lo = part(EC), part(EC), part(EC), part(EC)
        d_lo_kept = part(EC)
        s_hi_bf, d_hi_bf = part(EC // 2).bitcast(BF16), part(EC // 2).bitcast(BF16)
        tmp_a, tmp_b = part(E_COLS), part(E_COLS)
        assert at[0] <= slots_words
        s_slot = region_a[:, :].rearrange("p (t f) -> p t f", f=S_FIELDS)
        seg_max = region_a[:, 0:CHUNK_LEN]
        weights = region_a[:, 0:S_TILES * HEADS].rearrange("p (t h) -> p t h", h=HEADS)
        nodes = region_b[:, 0:NT * D].rearrange("p (n d) -> p n d", d=D)
        scores_t = region_b[:, 0:CHUNK_LEN]
        sums = region_b[:, 0:NT * (D + HEADS)].rearrange("p (n d) -> p n d", d=D + HEADS)
        d_slot = region_c[:, 0:S_TILES * D_FIELDS].rearrange("p (t f) -> p t f", f=D_FIELDS)
        breaks = region_c[:, 0:CHUNK_LEN // 2 + 1].bitcast(BF16)

        fetched = [whole.enter_context(nc.semaphore(f"fetched{k}")) for k in range(TURN)]

        def column(flat):
            return flat.rearrange("(p one) -> p one", one=1)

        with ExitStack() as ph:
            sem = ph.enter_context(phase_semaphores(nc))
            tmp = lambda n, s, d=F32: ph.enter_context(nc.sbuf_tensor(n, s, d))
            keys_clear, keys_in, consts, weights_in = sem("keys_clear"), sem("keys_in"), sem("consts"), sem("weights_in")
            pattern_ready, filled, prep = sem("pattern_ready"), sem("filled"), sem("prep")
            w_moved, w_taken, biases_in = sem("w_moved"), sem("w_taken"), sem("biases_in")
            bn_var_eps, edges_made = sem("bn_var_eps"), sem("edges_made")
            viol, viol_ready, prev_hi_ready = tmp("viol", [P, 2]), sem("viol_ready"), sem("prev_hi_ready")
            no_edges = tmp("no_edges", [S_TILES - E_COLS, 2, P])
            raw_w = tmp("raw_w", [P, 4, D])
            raw_eb = tmp("raw_eb", [HEADS, D])
            d_fill = tmp("d_fill", [P, S_TILES // 4, D_FIELDS])
            s_fill = tmp("s_fill", [P, CHUNK_TILES, S_FIELDS])
            bn_std = tmp("bn_std", [D, 1])
            block = ph.enter_context(nc.Block())
            CONSTS = 19
            whole_rows = 96

            @block.sync
            def _(sp):
                sp.wait_ge(keys_clear, 2)
                for keys, flat in ((dst_i, dst), (src_i, src)):
                    rows = flat[0:(P - 1) * E_COLS].rearrange("(p c) -> p c", c=E_COLS)
                    sp.dma_start(keys[0:whole_rows, :], rows[0:whole_rows, :]).then_inc(keys_in, 16)
                    sp.dma_start(keys[whole_rows:P - 1, :], rows[whole_rows:P - 1, :]).then_inc(keys_in, 16)
                    sp.dma_start(keys[P - 1:P, 0:LAST_COLS],
                                 flat[(P - 1) * E_COLS:N_EDGES].rearrange("(a c) -> a c", a=1)).then_inc(keys_in, 16)
                for n, w in enumerate((q_w, k_w, v_w, out_w)):
                    sp.dma_start(raw_w[:, n, :], w).then_inc(weights_in, 16)
                sp.dma_start(raw_eb[:, :], eb_w).then_inc(weights_in, 16)
                sp.dma_start(w1_sb[:, :], w1).then_inc(biases_in, 16)
                sp.dma_start(w2_sb[:, :], w2).then_inc(biases_in, 16)
                row = lambda b: b.rearrange("(a d) -> a d", a=1).to_broadcast([P, D])
                sp.dma_start(b1_bc[:, :], row(b1)).then_inc(biases_in, 16)
                sp.dma_start(b2_bc[:, :], row(b2)).then_inc(biases_in, 16)
                sp.dma_start(out_bc[:, :], row(out_b)).then_inc(biases_in, 16)
                for n, b in enumerate((q_b, k_b, v_b)):
                    sp.dma_start(qkv_bc[:, n * D:(n + 1) * D], row(b)).then_inc(biases_in, 16)
                for k in range(HALF):
                    sp.dma_start(ebb_bc[:, k, :],
                                 eb_b.rearrange("(a d) -> a d", a=1).to_broadcast([P, HEADS])).then_inc(biases_in, 16)
                for n, b in enumerate((gamma, beta, bn_mean, bn_var)):
                    sp.dma_start(bn_cols[:, n:n + 1], column(b)).then_inc(biases_in, 16)
                sp.wait_ge(keys_clear, 3)
                sp.dma_start(nodes[:, 0:NT - 1, :],
                             x[0:(NT - 1) * P, :].rearrange("(n p) d -> p n d", p=P)).then_inc(biases_in, 16)
                sp.dma_start(nodes[0:LAST_ROWS, NT - 1, :], x[(NT - 1) * P:N_NODES, :]).then_inc(biases_in, 16)
                sp.wait_ge(biases_in, 16 * 22)

            @block.scalar
            def _(act):
                act.wait_ge(pattern_ready, 2)
                for n in range(4):
                    step = S_TILES // 4
                    act.dma_start(d_slots.rearrange("(p t) f -> p t f", p=P)[:, n * step:(n + 1) * step, :],
                                  d_fill[:, :, :]).then_inc(filled, 16)
                for n in range(CHUNKS):
                    act.dma_start(s_slots.rearrange("(p t) f -> p t f", p=P)[:, n * CHUNK_TILES:(n + 1) * CHUNK_TILES, :],
                                  s_fill[:, :, :]).then_inc(filled, 16)
                act.wait_ge(edges_made, 4)
                for m, (keys, table) in enumerate(((tmp_a, edge_src), (tmp_b, edge_key))):
                    act.dma_start(table[0:E_COLS, :].rearrange("a d -> (a d)").rearrange("(p c) -> p c", p=P), keys).then_inc(filled, 16)
                    act.dma_start(table[E_COLS:S_TILES, :], no_edges[:, m, :]).then_inc(filled, 16)
                act.wait_ge(biases_in, 16 * 22)
                act.wait_ge(consts, 1)
                act.activation(bn_std[:, :], bn_cols[:, 3:4], ACT.Sqrt, bias=eps_col[:, 0:1]).then_inc(bn_var_eps, 1)
                act.wait_ge(filled, 16 * (4 + CHUNKS + 4))

            @block.gpsimd
            def _(pool):
                g = nc.gpsimd
                made, order = [0], consts

                def done(ins):
                    ins.then_inc(order, 1)
                    made[0] += 1
                    return made[0]

                done(g.memset(eps_col[:, :], LN_EPS))
                done(g.iota(iota_bf[:, :], pattern=[[1, P]], base=0, channel_multiplier=0,
                            allow_small_or_imprecise_dtypes=True))
                half = done(g.iota(iota_half[:, :], pattern=[[1, P]], base=0, channel_multiplier=0,
                                   allow_small_or_imprecise_dtypes=True))
                pool.wait_ge(order, half)
                done(g.tensor_scalar(iota_half[:, :], iota_half[:, :], 0.5, None, ALU.add))
                done(g.iota(iota_p[:, :], pattern=[[0, 1]], base=0, channel_multiplier=1,
                            allow_small_or_imprecise_dtypes=True))
                for m in (ident, ident_bf, next_row, wrap_row, zeros_bf):
                    done(g.memset(m[:, :], 0.0))
                for m in (ones, before, before_bf):
                    last = done(g.memset(m[:, :], 1.0))
                pool.wait_ge(order, last)
                for m in (ident, ident_bf):
                    done(g.affine_select(out=m[:, :], in_=m[:, :], compare_op=ALU.not_equal, fill=1.0, base=0,
                                         pattern=[[-1, P]], channel_multiplier=1))
                for m in (before, before_bf):
                    done(g.affine_select(out=m[:, :], in_=m[:, :], compare_op=ALU.is_gt, fill=0.0, base=0,
                                         pattern=[[1, P]], channel_multiplier=-1))
                done(g.affine_select(out=next_row[:, :], in_=next_row[:, :], compare_op=ALU.not_equal, fill=1.0,
                                     base=-1, pattern=[[1, P]], channel_multiplier=-1))
                done(g.affine_select(out=wrap_row[:, :], in_=wrap_row[:, :], compare_op=ALU.not_equal, fill=1.0,
                                     base=-(P - 1), pattern=[[-1, P]], channel_multiplier=1))
                pool.wait_ge(order, made[0])
                assert made[0] == CONSTS

            @block.vector
            def _(dve):
                v = nc.vector
                link = Chain(dve, prep)
                v.memset(dst_i, PAD_NODE).then_inc(keys_clear, 1)
                v.memset(src_i, PAD_NODE).then_inc(keys_clear, 1)
                v.memset(nodes[:, NT - 1, :], 0.0).then_inc(keys_clear, 1)
                link(v.memset(d_fill[:, :, :], 0.0))
                v.memset(d_fill[:, :, 1:2], EMPTY_KEY).then_inc(pattern_ready, 1)
                link(v.memset(s_fill[:, :, :], 0.0))
                v.memset(s_fill[:, :, 1:2], EMPTY_KEY).then_inc(pattern_ready, 1)
                dve.wait_ge(keys_in, 16 * 6)
                src_f, dst_f = tmp_a, tmp_b
                link(v.tensor_copy(src_f, src_i))
                link(v.tensor_copy(dst_f, dst_i))
                cut = slice(0, E_COLS)
                for a in (s_hi, s_lo, d_hi, d_lo, d_lo_kept):
                    v.memset(a[:, E_COLS:], 0.0)
                v.memset(s_hi_bf[:, E_COLS:], 0.0)
                link(v.memset(d_hi_bf[:, E_COLS:], 0.0))
                v.memset(no_edges[:, 0, :], 0.0).then_inc(edges_made, 1)
                v.memset(no_edges[:, 1, :], NO_KEY).then_inc(edges_made, 1)
                for key, hi, lo, hi_bf in ((src_f, s_hi, s_lo, s_hi_bf), (dst_f, d_hi, d_lo, d_hi_bf)):
                    as_int = lo[:, cut].bitcast(I32)
                    link(v.tensor_copy(as_int, key))
                    link(v.tensor_single_scalar(as_int, as_int, P.bit_length() - 1, ALU.arith_shift_right))
                    link(v.tensor_copy(hi[:, cut], as_int))
                    link(v.tensor_copy(hi_bf[:, cut], hi[:, cut]))
                    link(v.scalar_tensor_tensor(lo[:, cut], hi[:, cut], -float(P), key, ALU.mult, ALU.add))
                kept = d_lo_kept[:, cut]
                link(v.tensor_tensor(kept, src_f, dst_f, ALU.is_equal))
                link(v.scalar_tensor_tensor(kept, dst_f, -NO_KEY, kept, ALU.add, ALU.mult))
                v.tensor_tensor(dst_f, dst_f, kept, ALU.subtract).then_inc(edges_made, 2)
                dve.wait_ge(edges_made, 4)
                later = d_lo_kept[:, 0:E_COLS - 1]
                link(v.tensor_tensor(later, d_hi[:, 1:E_COLS], d_hi[:, 0:E_COLS - 1], ALU.is_lt))
                link(v.tensor_reduce(viol[:, 0:1], later, AX.X, ALU.add))
                link(v.scalar_tensor_tensor(kept, d_hi[:, cut], -float(P), dst_f, ALU.mult, ALU.add))
                dve.wait_ge(prev_hi_ready, 1)
                link(v.tensor_tensor(viol[:, 1:2], d_hi[:, 0:1], bank[2][:, 0:1], ALU.is_lt))
                v.tensor_tensor(viol[:, 0:1], viol[:, 0:1], viol[:, 1:2], ALU.add).then_inc(viol_ready, 1)
                dve.wait_ge(prev_hi_ready, 2)
                link(v.tensor_scalar(unsorted[:, :], bank[3][0:1, 0:1], 1.0, None, ALU.min))
                dve.wait_ge(w_moved, 5)
                link(v.tensor_copy(qkv_t[:, :], bank[0][:, 0:3 * D]))
                link(v.tensor_copy(out_t[:, :], bank[0][:, 3 * D:4 * D]))
                link(v.tensor_copy(eb_t[:, :], bank[1][:, 0:HEADS]))
                dve.wait_ge(biases_in, 16 * 22)
                dve.wait_ge(bn_var_eps, 1)
                link(v.reciprocal(bn_std[:, :], bn_std[:, :]))
                link(v.tensor_tensor(bn_scale[:, :], bn_cols[:, 0:1], bn_std[:, :], ALU.mult))
                link(v.tensor_tensor(bn_shift[:, :], bn_cols[:, 2:3], bn_scale[:, :], ALU.mult))
                link(v.tensor_tensor(bn_shift[:, :], bn_cols[:, 1:2], bn_shift[:, :], ALU.subtract))
                link(v.tensor_scalar(qkv_bc[:, 0:D], qkv_bc[:, 0:D], HEAD_DIM ** -0.5, None, ALU.mult))

            @block.tensor
            def _(pe):
                pe.wait_ge(consts, CONSTS)
                pe.wait_ge(weights_in, 16 * 5)
                for n in range(4):
                    nc.tensor.transpose(bank[0][:, n * D:(n + 1) * D], raw_w[:, n, :], ident[:, :]).then_inc(w_moved, 1)
                nc.tensor.transpose(bank[1][:, 0:HEADS], raw_eb[:, :], ident[0:HEADS, 0:HEADS]).then_inc(w_moved, 1)
                pe.wait_ge(edges_made, 4)
                nc.tensor.matmul(bank[2][:, 0:1], next_row[:, :], d_hi[:, E_COLS - 1:E_COLS], start=True, stop=True).then_inc(prev_hi_ready, 1)
                pe.wait_ge(viol_ready, 1)
                nc.tensor.matmul(bank[3][:, 0:1], ones[:, :], viol[:, 0:1], start=True, stop=True).then_inc(prev_hi_ready, 1)

        with ExitStack() as ph:
            sem = ph.enter_context(phase_semaphores(nc))
            tmp = lambda n, s, d=F32: ph.enter_context(nc.sbuf_tensor(n, s, d))
            hot_ready, signs_ready, hot_used = sem("count_hot_ready"), sem("count_signs_ready"), sem("count_hot_used")
            RING = 8
            s_hot, d_hot = tmp("count_s_hot", [P, RING, NT], BF16), tmp("count_d_hot", [P, RING, NT], BF16)
            s_sign = tmp("count_s_sign", [P, RING, P], BF16)
            d_sign = tmp("count_d_sign", [P, RING, 2, P], BF16)
            block = ph.enter_context(nc.Block())

            @block.vector
            def _(dve):
                def turn(i):
                    for k in range(TURN):
                        c, slot = i * TURN + k, k % RING
                        need(dve, hot_used, c + 1 - RING)
                        for hot, keys in ((s_hot[:, slot, :], s_hi), (d_hot[:, slot, :], d_hi), (d_sign[:, slot, 1, :], d_lo_kept)):
                            last = nc.vector.tensor_scalar(hot, iota_bf[:, 0:hot.shape[1]], keys[:, bass.ds(c, 1)], None, ALU.is_equal)
                        last.then_inc(hot_ready, 1)

                turn(0)
                with dve.Fori(1, E_TURNS) as i:
                    turn(i)

            @block.scalar
            def _(act):
                def turn(i):
                    for k in range(TURN):
                        c, slot = i * TURN + k, k % RING
                        need(act, hot_used, c + 1 - RING)
                        nc.scalar.activation(s_sign[:, slot, :], iota_half[:, :], ACT.Sign, bias=s_lo[:, bass.ds(c, 1)], scale=-1.0)
                        nc.scalar.activation(d_sign[:, slot, 0, :], iota_half[:, :], ACT.Sign, bias=d_lo[:, bass.ds(c, 1)],
                                             scale=-1.0).then_inc(signs_ready, 1)

                turn(0)
                with act.Fori(1, E_TURNS) as i:
                    turn(i)

            @block.tensor
            def _(pe):
                def zeros(**at):
                    nc.tensor.matmul(bank[0][0:NT, 0:P], zeros_bf[:, 0:NT], zeros_bf[:, :], **at)
                    for half in range(2):
                        nc.tensor.matmul(bank[1 + half][0:NT, 0:P], zeros_bf[:, 0:NT], zeros_bf[:, :], **at)

                zeros(start=True, stop=False)
                with pe.Fori(0, E_TURNS) as i:
                    for k in range(TURN):
                        c, slot = i * TURN + k, k % RING
                        pe.wait_ge(hot_ready, c + 1)
                        pe.wait_ge(signs_ready, c + 1)
                        nc.tensor.matmul(bank[0][0:NT, 0:P], s_hot[:, slot, :], s_sign[:, slot, :], start=False, stop=False)
                        nc.tensor.matmul(bank[1][0:NT, 0:P], d_hot[:, slot, :], d_sign[:, slot, 0, :], start=False, stop=False)
                        nc.tensor.matmul(bank[2][0:NT, 0:P], d_hot[:, slot, :], d_sign[:, slot, 1, :], start=False, stop=False).then_inc(hot_used, 1)
                zeros(start=False, stop=True)

        with ExitStack() as ph:
            sem = ph.enter_context(phase_semaphores(nc))
            tmp = lambda n, s, d=F32: ph.enter_context(nc.sbuf_tensor(n, s, d))
            step, tiles_ready, starts_ready = sem("base_step"), sem("base_tiles_ready"), sem("base_starts_ready")
            mask_ready, nodes_ready = sem("base_mask_ready"), sem("base_nodes_ready")
            deg_ready, deg_moved, deg_root = sem("deg_ready"), sem("deg_moved"), sem("deg_root")
            first_ready, map_ready, rows_ready = sem("base_first_ready"), sem("base_map_ready"), sem("base_rows_ready")
            upto = tmp("upto", [NT, 2, P])
            deg = tmp("deg", [NT, P])
            edges, first, bounds, n_tiles, start_tile, end_tile = (
                tmp(n, [NT, 2]) for n in ("edges", "first", "bounds", "n_tiles", "start_tile", "end_tile"))
            bounds_i = tmp("bounds_i", [NT, 3], I32)
            tile_map = tmp("tile_map", [NT, 2])
            passed, inside = tmp("passed", [NT, S_TILES]), tmp("inside", [NT, S_TILES])
            deg_t = tmp("deg_t", [P, NT])
            iota_t = tmp("iota_t", [NT, S_TILES])
            tile_no = tmp("tile_no", [P, W_BLOCKS])
            iota_made = sem("iota_made")
            QUARTER = S_TILES // 4
            SHIFT = P.bit_length() - 1
            block = ph.enter_context(nc.Block())

            @block.vector
            def _(dve):
                v = nc.vector
                link = Chain(dve, step)
                v.tensor_scalar(deg[:, :], bank[2][0:NT, 0:P], 1.0, None, ALU.add).then_inc(deg_ready, 1)
                for n in range(2):
                    link(v.tensor_copy(upto[:, n, :], bank[n][0:NT, 0:P]))
                    link(v.tensor_scalar(edges[:, n:n + 1], upto[:, n, P - 1:P], -1.0, None, ALU.mult))
                    link(v.tensor_scalar(upto[:, n, :], upto[:, n, :], edges[:, n:n + 1], -0.5, ALU.subtract, ALU.mult))
                v.tensor_copy(first[:, :], edges[:, :]).then_inc(tiles_ready, 1)
                dve.wait_ge(first_ready, 1)
                link(v.tensor_copy(first[:, :], bank[3][0:NT, 0:2]))
                link(v.tensor_scalar(bounds[:, 0:1], edges[:, 0:1], float(P - 1), None, ALU.add))
                link(v.tensor_scalar(bounds[:, 1:2], first[:, 1:2], edges[:, 1:2], -1.0, ALU.add, ALU.add))
                link(v.tensor_copy(bounds_i[:, 0:2], bounds[:, :]))
                link(v.tensor_copy(bounds_i[:, 2:3], first[:, 1:2]))
                link(v.tensor_single_scalar(bounds_i[:, :], bounds_i[:, :], SHIFT, ALU.arith_shift_right))
                link(v.tensor_copy(n_tiles[:, 0:1], bounds_i[:, 0:1]))
                link(v.tensor_copy(bounds[:, 1:2], bounds_i[:, 1:2]))
                link(v.tensor_copy(first[:, 0:1], bounds_i[:, 2:3]))
                link(v.tensor_scalar(n_tiles[:, 1:2], bounds[:, 1:2], first[:, 0:1], 1.0, ALU.subtract, ALU.add))
                link(v.tensor_scalar(bounds[:, 0:1], edges[:, 1:2], 1.0, None, ALU.min))
                v.tensor_tensor(n_tiles[:, 1:2], n_tiles[:, 1:2], bounds[:, 0:1], ALU.mult).then_inc(tiles_ready, 1)
                dve.wait_ge(starts_ready, 1)
                dve.wait_ge(tiles_ready, 2)
                link(v.tensor_copy(start_tile[:, :], bank[4][0:NT, 0:2]))
                link(v.tensor_tensor(end_tile[:, :], start_tile[:, :], n_tiles[:, :], ALU.add))
                link(v.tensor_scalar(bounds[:, :], start_tile[:, :], float(P), None, ALU.mult))
                link(v.tensor_tensor(tile_map[:, 0:1], first[:, 0:1], start_tile[:, 1:2], ALU.subtract))
                link(v.tensor_scalar(tile_map[:, 1:2], iota_p[0:NT, :], float(P), None, ALU.mult))
                for n, base in ((0, base_s), (1, base_d)):
                    link(v.tensor_copy(base[:, 0:1], bounds[:, n:n + 1]))
                    link(v.tensor_scalar(base[:, 1:], upto[:, n, 0:P - 1], bounds[:, n:n + 1], None, ALU.add))
                dve.wait_ge(iota_made, 2)
                for n, node in ((0, node_s), (1, node_d)):
                    v.tensor_scalar(passed[:, :], iota_t[0:NT, :], end_tile[:, n:n + 1], None, ALU.is_ge).then_inc(mask_ready, 1)
                    if n == 1:
                        dve.wait_ge(mask_ready, 2)
                        v.scalar_tensor_tensor(inside[:, :], iota_t[0:NT, :], start_tile[:, 1:2], passed[:, :], ALU.is_ge, ALU.subtract).then_inc(map_ready, 1)
                    dve.wait_ge(nodes_ready, n + 1)
                    for j in range(4):
                        part_of = slice(j * QUARTER, (j + 1) * QUARTER)
                        if n == 0:
                            link(v.tensor_scalar(node_s_bc[:, part_of], bank[4 + j][:, 0:QUARTER], float(NT - 1), None, ALU.min))
                        row = slice(S_ROW, S_ROW + 1) if n == 0 else slice(0, 1)
                        link(v.tensor_scalar(node[:, part_of], bank[4 + j][row, 0:QUARTER], float(NT - 1), None, ALU.min))
                dve.wait_ge(rows_ready, 1)
                mapped = bank[1][0:WINDOWS, 0:2 * W_BLOCKS].rearrange("p (b a) -> p a b", a=2)
                link(v.tensor_tensor(window_row[0:WINDOWS, :], mapped[:, 0, :], tile_no[0:WINDOWS, :], ALU.add))
                link(v.tensor_copy(window_node[0:WINDOWS, :], mapped[:, 1, :]))
                dve.wait_ge(deg_root, 1)
                link(v.reciprocal(dinv[:, :], deg_t[:, :]))

            @block.tensor
            def _(pe):
                pe.wait_ge(deg_ready, 1)
                nc.tensor.transpose(bank[5][:, 0:NT], deg[:, :], ident[0:NT, 0:NT]).then_inc(deg_moved, 1)
                pe.wait_ge(tiles_ready, 1)
                nc.tensor.matmul(bank[3][0:NT, 0:2], before[0:NT, 0:NT], first[:, :], start=True, stop=True).then_inc(first_ready, 1)
                pe.wait_ge(tiles_ready, 2)
                nc.tensor.matmul(bank[4][0:NT, 0:2], before[0:NT, 0:NT], n_tiles[:, :], start=True, stop=True).then_inc(starts_ready, 1)
                pe.wait_ge(deg_root, 1)
                for n in range(2):
                    pe.wait_ge(mask_ready, n + 1)
                    for j in range(4):
                        last = nc.tensor.matmul(bank[4 + j][:, 0:QUARTER], ones[0:NT, :], passed[:, j * QUARTER:(j + 1) * QUARTER],
                                                start=True, stop=True)
                    last.then_inc(nodes_ready, 1)
                pe.wait_ge(map_ready, 1)
                for b in range(W_BLOCKS):
                    last = nc.tensor.matmul(bank[1][0:WINDOWS, 2 * b:2 * b + 2], inside[:, b * WINDOWS:(b + 1) * WINDOWS], tile_map[:, :],
                                            start=True, stop=True)
                last.then_inc(rows_ready, 1)

            @block.gpsimd
            def _(pool):
                nc.gpsimd.iota(iota_t[:, :], pattern=[[1, S_TILES]], base=0, channel_multiplier=0,
                               allow_small_or_imprecise_dtypes=True).then_inc(iota_made, 1)
                nc.gpsimd.iota(tile_no[:, :], pattern=[[WINDOWS, W_BLOCKS]], base=0, channel_multiplier=1,
                               allow_small_or_imprecise_dtypes=True).then_inc(iota_made, 1)

            @block.scalar
            def _(act):
                act.wait_ge(deg_moved, 1)
                act.activation(deg_t[:, :], bank[5][:, 0:NT], ACT.Sqrt).then_inc(deg_root, 1)

        with ExitStack() as ph:
            own = ph.enter_context(phase_semaphores(nc))
            sem = lambda n: own(f"window_{n}")
            tmp = lambda n, s, d=F32: ph.enter_context(nc.sbuf_tensor(f"window_{n}", s, d))
            rows_in, local, moved, kept = [sem(f"rows_in{m}") for m in range(2)], sem("local"), sem("moved"), sem("kept")
            edge_rows = [tmp(n, [WINDOWS, W_BLOCKS, P]) for n in ("src_rows", "key_rows")]
            PER_BANK = 4
            W_BANKS = -(-W_BLOCKS // PER_BANK)
            blocks_of = lambda n: range(n * PER_BANK, min(W_BLOCKS, (n + 1) * PER_BANK))
            block = ph.enter_context(nc.Block())

            @block.gpsimd
            def _(pool):
                for m, table in enumerate((edge_src, edge_key)):
                    for b in range(W_BLOCKS):
                        nc.gpsimd.indirect_dma_start(edge_rows[m][:, b, :], None, table,
                                                     bass.IndirectOffsetOnAxis(ap=window_row[0:WINDOWS, b:b + 1], axis=0)).then_inc(rows_in[m], 16)

            @block.tensor
            def _(pe):
                for m in range(2):
                    if m == 0:
                        pe.wait_ge(rows_in[0], 16 * W_BLOCKS)
                    else:
                        pe.wait_ge(local, 1)
                    for n in range(W_BANKS):
                        for b in blocks_of(n):
                            last = nc.tensor.transpose(bank[m * W_BANKS + n][:, (b % PER_BANK) * P:(b % PER_BANK) * P + WINDOWS],
                                                       edge_rows[m][:, b, :], ident[0:WINDOWS, 0:WINDOWS])
                        last.then_inc(moved, 1)

            @block.vector
            def _(dve):
                def keep(m):
                    for n in range(W_BANKS):
                        dve.wait_ge(moved, m * W_BANKS + n + 1)
                        held = len(blocks_of(n))
                        field = d_slot[:, n * PER_BANK * WINDOWS:(n * PER_BANK + held) * WINDOWS, m:m + 1]
                        nc.vector.tensor_copy((field.bitcast(I32) if m == 0 else field).rearrange("p (b t) a -> p b (t a)", t=WINDOWS),
                                              bank[m * W_BANKS + n][:, 0:held * P].rearrange("p (b t) -> p b t", t=P)[:, :, 0:WINDOWS]).then_inc(kept, 1)

                keep(0)
                dve.wait_ge(rows_in[1], 16 * W_BLOCKS)
                nc.vector.tensor_tensor(edge_rows[1][:, :, :], edge_rows[1][:, :, :],
                                        window_node[0:WINDOWS, :].unsqueeze(2).to_broadcast([WINDOWS, W_BLOCKS, P]), ALU.subtract).then_inc(local, 1)
                keep(1)

        @contextmanager
        def always(eng):
            yield

        @contextmanager
        def when_unsorted(eng):
            with eng.If(eng.value_load(unsorted[0:1, 0:1]) != 0):
                yield

        def sort_edges(name, hi, lo, hi_bf, lo_kept, base, index, table, fields, with_bias, when=always):
            with ExitStack() as ph:
                own = ph.enter_context(phase_semaphores(nc))
                sem = lambda n: own(f"{name}_{n}")
                tmp = lambda n, s, d=F32: ph.enter_context(nc.sbuf_tensor(f"{name}_{n}", s, d))
                hot_ready, tile_row_ready, masks_ready = sem("hot_ready"), sem("tile_row_ready"), sem("masks_ready")
                counted, next_ready, found, picked = sem("counted"), sem("next_ready"), sem("found"), sem("picked")
                slot_step, payload_ready, go, slots_in = sem("slot_step"), sem("payload_ready"), sem("go"), sem("slots_in")
                scattered = [sem(f"scattered{h}") for h in range(2)]
                attr_in = [sem(f"attr_in{h}") for h in range(2)]
                attr_moved, attr_kept, bias_ready = sem("attr_moved"), sem("attr_kept"), sem("bias_ready")
                RING = 4
                hot_hi, hot_lo = tmp("hot_hi", [P, RING, NT], BF16), tmp("hot_lo", [P, RING, P], BF16)
                earlier = tmp("earlier", [P, RING, P], BF16)
                hi_t = tmp("hi_t", [NT, RING, P])
                next_slot = tmp("next_slot", [NT, 2, P])
                junk = tmp("junk", [P, P])
                slot = tmp("slot", [P, 2, HALF])
                slot_i, row_i, tile_i = (tmp(n, [P, HALF], I32) for n in ("slot_i", "row_i", "tile_i"))
                where = tmp("where", [P, 2, HALF], I32)
                payload = tmp("payload", [P, 2, HALF, fields])
                tile_row, found_in, running = [bank[0], bank[1]], [bank[2], bank[3]], bank[4]
                if with_bias:
                    attr_sb = tmp("attr_sb", [P, 2, HALF, D])
                    attr_t = tmp("attr_t", [D, 2, 4 * P])
                    bias_out = bank[7]
                    attr_bank = [bank[5], bank[6]]
                    attr_rows = attr[0:(P - 1) * E_COLS, :].rearrange("(p c) d -> p c d", c=E_COLS)
                    attr_last = attr[(P - 1) * E_COLS:N_EDGES, :].rearrange("(p c) d -> p c d", p=1)
                block = ph.enter_context(nc.Block())
                CHAINED = 2 * (4 if not with_bias else 4)

                @block.vector
                def _(dve):
                    with when(dve):
                        v = nc.vector
                        link = Chain(dve, slot_step)

                        def one_hots(c, k):
                            s = k % RING
                            need(dve, found, c + 1 - RING)
                            v.tensor_scalar(hot_hi[:, s, :], iota_bf[:, 0:NT], hi[:, bass.ds(c, 1)], None, ALU.is_equal)
                            v.tensor_scalar(hot_lo[:, s, :], iota_bf[:, :], lo[:, bass.ds(c, 1)], None, ALU.is_equal).then_inc(hot_ready, 1)

                        def masks(c, k):
                            s, b = k % RING, k % 2
                            need(dve, tile_row_ready, c + 1)
                            v.tensor_scalar(hi_t[:, s, :], tile_row[b][0:NT, 0:P], iota_p[0:NT, 0:1], None, ALU.is_equal)
                            v.scalar_tensor_tensor(earlier[:, s, :], tile_row[b][:, 0:P], hi[:, bass.ds(c, 1)], before_bf[:, :],
                                                   ALU.is_equal, ALU.mult).then_inc(masks_ready, 1)

                        def turn(i):
                            link.turn(i * CHAINED)
                            for k in range(TURN):
                                c, h = i * TURN + k, k // HALF
                                one_hots(c + 2, k + 2)
                                masks(c + 1, k + 1)
                                dve.wait_ge(found, c + 1)
                                need(dve, picked, c)
                                v.tensor_tensor_reduce(out=junk[:, :], in0=found_in[k % 2][:, 0:P], in1=hot_lo[:, k % RING, :],
                                                       scale=1.0, scalar=0.0, op0=ALU.mult, op1=ALU.add,
                                                       accum_out=slot[:, h, k % HALF:k % HALF + 1]).then_inc(picked, 1)
                                if k % HALF == HALF - 1:
                                    cols = bass.ds(i * TURN + h * HALF, HALF)
                                    dve.wait_ge(picked, c + 1)
                                    link(v.tensor_copy(slot_i[:, :], slot[:, h, :]))
                                    link(v.tensor_single_scalar(tile_i[:, :], slot_i[:, :], P.bit_length() - 1, ALU.arith_shift_right))
                                    link(v.tensor_single_scalar(row_i[:, :], slot_i[:, :], P - 1, ALU.bitwise_and))
                                    need(dve, scattered[h], i * HALF * 16)
                                    link(v.scalar_tensor_tensor(where[:, h, :], row_i[:, :], float(S_TILES), tile_i[:, :],
                                                                ALU.mult, ALU.add))
                                    v.tensor_copy(payload[:, h, :, 0:1].bitcast(I32).rearrange("p k a -> p (k a)"), index[:, cols])
                                    if with_bias:
                                        dve.wait_ge(bias_ready, 2 * i + h + 1)
                                        v.tensor_tensor(payload[:, h, :, 2:S_FIELDS],
                                                        bias_out[:, h * HALF * HEADS:(h + 1) * HALF * HEADS].rearrange("p (k a) -> p k a", a=HEADS),
                                                        ebb_bc[:, :, :], ALU.add)
                                    v.tensor_copy(payload[:, h, :, 1:2].rearrange("p k a -> p (k a)"), lo_kept[:, cols]).then_inc(payload_ready, 1)

                        for c in range(2):
                            one_hots(c, c)
                        masks(0, 0)
                        turn(0)
                        with dve.Fori(1, E_TURNS) as i:
                            turn(i)

                @block.tensor
                def _(pe):
                    with when(pe):
                        t = nc.tensor

                        def spread_tiles(c, k):
                            need(pe, masks_ready, c - 1)
                            t.matmul(tile_row[k % 2][:, 0:P], hi_bf[:, bass.ds(c, 1)].to_broadcast([P, P]), ident_bf[:, :],
                                     start=True, stop=True).then_inc(tile_row_ready, 1)

                        def turn(i):
                            for k in range(TURN):
                                c, s = i * TURN + k, k % RING
                                spread_tiles(c + 2, k + 2)
                                pe.wait_ge(hot_ready, c + 1)
                                pe.wait_ge(next_ready, c + 1)
                                t.matmul(running[0:NT, 0:P], hot_hi[:, s, :], hot_lo[:, s, :], start=False, stop=True,
                                         skip_group_check=True).then_inc(counted, 1)
                                pe.wait_ge(masks_ready, c + 1)
                                need(pe, picked, c - 1)
                                t.matmul(found_in[k % 2][:, 0:P], hi_t[:, s, :], next_slot[:, k % 2, :], start=True, stop=False)
                                t.matmul(found_in[k % 2][:, 0:P], earlier[:, s, :], hot_lo[:, s, :], start=False, stop=True).then_inc(found, 1)
                                if with_bias:
                                    h, j = k // HALF, k % HALF
                                    if j == 1:
                                        pe.wait_ge(attr_in[h], (i + 1) * (16 * 3))
                                        for m in range(HALF):
                                            if m % 4 == 0:
                                                need(pe, attr_kept, (2 * i + h) * 2 + m // 4 - 1)
                                            last = t.transpose(attr_bank[m // 4][:, (m % 4) * P:(m % 4 + 1) * P], attr_sb[:, h, m, :], ident[:, :])
                                            if m % 4 == 3:
                                                last.then_inc(attr_moved, 1)
                                    if j in (3, 5):
                                        g = (j - 3) // 2
                                        pe.wait_ge(attr_kept, (2 * i + h) * 2 + g + 1)
                                        if g == 0:
                                            need(pe, payload_ready, 2 * i + h - 1)
                                        for m in range(4):
                                            at_col = (h * HALF + g * 4 + m) * HEADS
                                            last = t.matmul(bias_out[:, at_col:at_col + HEADS], attr_t[:, g, m * P:(m + 1) * P], eb_t[:, :],
                                                            start=True, stop=True)
                                        if g == 1:
                                            last.then_inc(bias_ready, 1)

                        t.matmul(running[0:NT, 0:P], ident[0:NT, 0:NT], base[:, :], start=True, stop=True).then_inc(counted, 1)
                        for c in range(2):
                            spread_tiles(c, c)
                        turn(0)
                        with pe.Fori(1, E_TURNS) as i:
                            turn(i)

                @block.scalar
                def _(act):
                    with when(act):
                        def turn(i):
                            for k in range(TURN):
                                c = i * TURN + k
                                act.wait_ge(counted, c + 1)
                                need(act, found, c - 1)
                                nc.scalar.copy(next_slot[:, k % 2, :], running[0:NT, 0:P]).then_inc(next_ready, 1)
                                if with_bias and k % HALF == 2:
                                    h = k // HALF
                                    for g in range(2):
                                        act.wait_ge(attr_moved, (2 * i + h) * 2 + g + 1)
                                        need(act, bias_ready, 2 * i + h)
                                        nc.scalar.copy(attr_t[:, g, :], attr_bank[g][:, :]).then_inc(attr_kept, 1)

                        turn(0)
                        with act.Fori(1, E_TURNS) as i:
                            turn(i)

                @block.gpsimd
                def _(pool):
                    with when(pool):
                        def turn(i):
                            for h in range(2):
                                pool.wait_ge(payload_ready, 2 * i + h + 1)
                                pool.sem_inc(go, 1)
                                for k in range(HALF):
                                    nc.gpsimd.indirect_dma_start(
                                        table, bass.IndirectOffsetOnAxis(ap=where[:, h, k:k + 1], axis=0),
                                        payload[:, h, k, :], None).then_inc(scattered[h], 16)

                        with pool.Fori(0, E_TURNS) as i:
                            turn(i)
                        for h in range(2):
                            pool.wait_ge(scattered[h], E_TURNS * HALF * 16)
                        if not with_bias:
                            pool.dma_start(d_slot, d_slots.rearrange("(p t) f -> p t f", p=P)).then_inc(slots_in, 16)
                            pool.wait_ge(slots_in, 16)

                if with_bias:
                    @block.sync
                    def _(sp):
                        with when(sp):
                            def load(i, h, last_too):
                                need(sp, attr_moved, (2 * (i - 1) + h) * 2 + 2)
                                cols = bass.ds(i * TURN + h * HALF, HALF)
                                sp.dma_start(attr_sb[0:96, h, :, :], attr_rows[0:96, cols, :]).then_inc(attr_in[h], 16)
                                sp.dma_start(attr_sb[96:P - 1, h, :, :], attr_rows[96:P - 1, cols, :]).then_inc(attr_in[h], 16)
                                again = cols if last_too else bass.ds(h * HALF, HALF)
                                sp.dma_start(attr_sb[P - 1:P, h, :, :], attr_last[:, again, :]).then_inc(attr_in[h], 16)

                            for h in range(2):
                                load(0, h, True)
                            with sp.Fori(1, FULL_TURNS) as i:
                                for h in range(2):
                                    load(i, h, True)
                            with sp.Fori(FULL_TURNS, E_TURNS) as i:
                                for h in range(2):
                                    load(i, h, False)

        def linear(name, w_sb, b_bc, table, normed):
            with ExitStack() as ph:
                own = ph.enter_context(phase_semaphores(nc))
                sem = lambda n: own(f"{name}_{n}")
                tmp = lambda n, s, d=F32: ph.enter_context(nc.sbuf_tensor(f"{name}_{n}", s, d))
                staged, moved, kept, made, biased, scaled, stored = (
                    sem(n) for n in ("staged", "moved", "kept", "made", "biased", "scaled", "stored"))
                rows = tmp("rows", [P, 2, D])
                rows_t = tmp("rows_t", [D, 2, P])
                biased_rows = tmp("biased", [P, 2, D])
                block = ph.enter_context(nc.Block())

                @block.vector
                def _(dve):
                    def turn(i):
                        for b in range(2):
                            n = i * 2 + b
                            need(dve, moved, n - 1)
                            here = nodes[:, bass.ds(n, 1), :].rearrange("p a d -> p (a d)")
                            if normed:
                                nc.vector.tensor_scalar(rows[:, b, :], here, dinv[:, bass.ds(n, 1)], None, ALU.mult).then_inc(staged, 1)
                            else:
                                nc.vector.tensor_copy(rows[:, b, :], here).then_inc(staged, 1)
                            dve.wait_ge(made, n + 1)
                            need(dve, scaled, n - 1)
                            nc.vector.tensor_tensor(biased_rows[:, b, :], bank[2 + b][:, 0:D], b_bc[:, :], ALU.add).then_inc(biased, 1)
                            dve.wait_ge(biased, n + 1)
                            nc.vector.tensor_scalar(here, biased_rows[:, b, :], dinv[:, bass.ds(n, 1)], None, ALU.mult).then_inc(scaled, 1)

                    turn(0)
                    with dve.Fori(1, NT // 2) as i:
                        turn(i)

                @block.tensor
                def _(pe):
                    def turn(i):
                        for b in range(2):
                            n = i * 2 + b
                            pe.wait_ge(staged, n + 1)
                            need(pe, kept, n - 1)
                            nc.tensor.transpose(bank[b][:, 0:P], rows[:, b, :], ident[:, :]).then_inc(moved, 1)
                            pe.wait_ge(kept, n + 1)
                            need(pe, biased, n - 1)
                            nc.tensor.matmul(bank[2 + b][:, 0:D], rows_t[:, b, :], w_sb[:, :], start=True, stop=True).then_inc(made, 1)

                    turn(0)
                    with pe.Fori(1, NT // 2) as i:
                        turn(i)

                @block.scalar
                def _(act):
                    def turn(i):
                        for b in range(2):
                            n = i * 2 + b
                            act.wait_ge(moved, n + 1)
                            need(act, made, n - 1)
                            if normed:
                                act.activation(rows_t[:, b, :], bank[b][:, 0:P], ACT.Relu, bias=bn_shift[:, 0:1],
                                               scale=bn_scale[:, 0:1]).then_inc(kept, 1)
                            else:
                                act.copy(rows_t[:, b, :], bank[b][:, 0:P]).then_inc(kept, 1)

                    turn(0)
                    with act.Fori(1, NT // 2) as i:
                        turn(i)

                @block.sync
                def _(sp):
                    with sp.Fori(0, NT) as n:
                        sp.wait_ge(scaled, n + 1)
                        sp.dma_start(table[bass.ds(n * P, P), :], nodes[:, bass.ds(n, 1), :].rearrange("p a d -> p (a d)")).then_inc(stored, 16)
                    sp.wait_ge(stored, 16 * NT)

        def sparse_product(name, table, nth):
            with ExitStack() as ph:
                own = ph.enter_context(phase_semaphores(nc))
                sem = lambda n: own(f"{name}_{n}")
                tmp = lambda n, s, d=F32: ph.enter_context(nc.sbuf_tensor(f"{name}_{n}", s, d))
                local_ready, index_ready, go = sem("local_ready"), sem("index_ready"), sem("go")
                hot_ready, summed, added = sem("hot_ready"), sem("summed"), sem("added")
                RING = 4
                index_ring = tmp("index_ring", [P, TURN], I32)
                fetched_rows = tmp("fetched_rows", [P, TURN, D])
                hot = tmp("hot", [P, RING, P])
                block = ph.enter_context(nc.Block())

                @block.scalar
                def _(act):
                    act.copy(lo_slots[:, 0:S_TILES], d_slot[:, :, 1:2].rearrange("p t a -> p (t a)")).then_inc(local_ready, 1)

                    def turn(i):
                        for h in range(2):
                            need(act, summed, i * TURN + h * HALF + HALF - TURN)
                            act.copy(index_ring[:, h * HALF:(h + 1) * HALF],
                                     d_slot[:, bass.ds(i * TURN + h * HALF, HALF), 0:1].bitcast(I32).rearrange("p t a -> p (t a)")).then_inc(index_ready, 1)

                    turn(0)
                    with act.Fori(1, S_TURNS) as i:
                        turn(i)

                @block.gpsimd
                def _(pool):
                    nc.gpsimd.memset(lo_slots[:, S_TILES:], EMPTY_KEY).then_inc(local_ready, 1)
                    with pool.Fori(0, S_TURNS) as i:
                        for h in range(2):
                            pool.wait_ge(index_ready, 2 * i + h + 1)
                            pool.sem_inc(go, 1)
                            for k in range(h * HALF, (h + 1) * HALF):
                                nc.gpsimd.indirect_dma_start(
                                    fetched_rows[:, k, :], None, table,
                                    bass.IndirectOffsetOnAxis(ap=index_ring[:, k:k + 1], axis=0)).then_inc(fetched[k], 16)

                @block.vector
                def _(dve):
                    dve.wait_ge(local_ready, 2)

                    def one_hot(t, k):
                        need(dve, summed, t + 1 - RING)
                        nc.vector.tensor_scalar(hot[:, k % RING, :], iota_bf[:, :], lo_slots[:, bass.ds(t, 1)], None,
                                                ALU.is_equal).then_inc(hot_ready, 1)

                    def turn(i):
                        for h in range(2):
                            _, node = nc.values_load_multi_w_load_instructions(
                                node_d[0:1, bass.ds(i * TURN + h * HALF, HALF)], engines=[mybir.EngineType.DVE],
                                min_val=0, max_val=NT - 1, skip_runtime_bounds_check_because=CLAMPED)
                            for k in range(h * HALF, (h + 1) * HALF):
                                t = i * TURN + k
                                one_hot(t + 2, k + 2)
                                dve.wait_ge(summed, t + 1)
                                need(dve, added, t)
                                here = nodes[:, bass.ds(node[k % HALF], 1), :].rearrange("p a d -> p (a d)")
                                nc.vector.tensor_tensor(here, here, bank[k % RING][:, 0:D], ALU.add).then_inc(added, 1)

                    for t in range(2):
                        one_hot(t, t)
                    turn(0)
                    with dve.Fori(1, S_TURNS) as i:
                        turn(i)

                @block.tensor
                def _(pe):
                    def turn(i):
                        for k in range(TURN):
                            t = i * TURN + k
                            pe.wait_ge(hot_ready, t + 1)
                            need(pe, added, t + 1 - RING)
                            pe.wait_ge(fetched[k], (nth * S_TURNS + i + 1) * 16)
                            nc.tensor.matmul(bank[k % RING][:, 0:D], hot[:, k % RING, :], fetched_rows[:, k, :],
                                             start=True, stop=True).then_inc(summed, 1)

                    turn(0)
                    with pe.Fori(1, S_TURNS) as i:
                        turn(i)

        sort_edges("sort_d", d_hi, d_lo, d_hi_bf, d_lo_kept, base_d, src_i, d_slots, D_FIELDS, False, when_unsorted)
        sort_edges("sort_s", s_hi, s_lo, s_hi_bf, s_lo, base_s, dst_i, s_slots, S_FIELDS, True)
        linear("lin1", w1_sb, b1_bc, h_table[0], False)
        sparse_product("spmm1", h_table[0], 0)
        linear("lin2", w2_sb, b2_bc, h_table[1], True)
        sparse_product("spmm2", h_table[1], 1)

        with ExitStack() as ph:
            own = ph.enter_context(phase_semaphores(nc))
            sem = lambda n: own(f"qkv_{n}")
            tmp = lambda n, s, d=F32: ph.enter_context(nc.sbuf_tensor(f"qkv_{n}", s, d))
            cleared, x_used, step, var_ready, rooted = sem("cleared"), sem("x_used"), sem("step"), sem("var_ready"), sem("rooted")
            x_in = [sem(f"x_in{b}") for b in range(2)]
            x1_out = [sem(f"x1_out{b}") for b in range(2)]
            kv_out = [sem(f"kv_out{b}") for b in range(2)]
            staged, moved, kept, made, q_done, kv_done = (sem(n) for n in ("staged", "moved", "kept", "made", "q_done", "kv_done"))
            x_sb, stats = tmp("x_sb", [P, 2, D]), tmp("stats", [P, 2, 6])
            tile_mv, looked = tmp("tile_mv", [P, 2, 2]), sem("looked")
            rows, rows_t, kv_rows = tmp("rows", [P, 2, D]), tmp("rows_t", [D, 2, P]), tmp("kv_rows", [P, 2, 2 * D])
            block = ph.enter_context(nc.Block())

            @block.sync
            def _(sp):
                def load(n, b, rows_n):
                    need(sp, x_used, n - 1)
                    sp.dma_start(x_sb[0:rows_n, b, :], x[bass.ds(n * P, rows_n), :]).then_inc(x_in[b], 16)

                sp.wait_ge(cleared, 1)
                for b in range(2):
                    load(b, b, P)
                with sp.Fori(1, NT // 2 - 1) as i:
                    for b in range(2):
                        load(i * 2 + b, b, P)
                load(NT - 2, 0, P)
                load(NT - 1, 1, LAST_ROWS)
                with sp.Fori(0, NT // 2) as i:
                    for b in range(2):
                        n = i * 2 + b
                        sp.wait_ge(staged, n + 1)
                        sp.dma_start(x1_dram[bass.ds(n * P, P), :], rows[:, b, :]).then_inc(x1_out[b], 16)
                        sp.wait_ge(kv_done, n + 1)
                        sp.dma_start(kv_table[bass.ds(n * P, P), :], kv_rows[:, b, :]).then_inc(kv_out[b], 16)
                for b in range(2):
                    sp.wait_ge(x1_out[b], 16 * (NT // 2))
                    sp.wait_ge(kv_out[b], 16 * (NT // 2))

            @block.vector
            def _(dve):
                v = nc.vector
                v.memset(x_sb[:, :, :], 0.0).then_inc(cleared, 1)
                link = Chain(dve, step)

                def residual(i):
                    link.turn(i * 2 * 3)
                    for b in range(2):
                        n = i * 2 + b
                        here = nodes[:, bass.ds(n, 1), :].rearrange("p a d -> p (a d)")
                        dve.wait_ge(x_in[b], (i + 1) * 16)
                        ins = v.scalar_tensor_tensor(here, here, dinv[:, bass.ds(n, 1)], x_sb[:, b, :], ALU.mult, ALU.add)
                        ins.then_inc(x_used, 1)
                        dve.wait_ge(x_used, n + 1)
                        dve.sem_inc(looked, 1)
                        link(v.bn_stats(stats[:, b, :], here))
                        dve.sem_inc(looked, 1)
                        link(v.bn_aggr(tile_mv[:, b, :], stats[:, b, :]))
                        link(v.tensor_copy(mean_var[:, bass.ds(n, 1), :].rearrange("p a d -> p (a d)"), tile_mv[:, b, :]))

                residual(0)
                with dve.Fori(1, NT // 2) as i:
                    residual(i)
                v.tensor_copy(stats[:, 0, 0:1], eps_col[:, :]).then_inc(var_ready, 1)
                link.turn(NT * 3)
                dve.wait_ge(rooted, 1)
                link(v.reciprocal(rstd[:, :], rstd[:, :]))

                def turn(i):
                    for b in range(2):
                        n = i * 2 + b
                        here = nodes[:, bass.ds(n, 1), :].rearrange("p a d -> p (a d)")
                        need(dve, moved, n - 1)
                        need(dve, x1_out[b], i * 16)
                        v.tensor_scalar(rows[:, b, :], here, mean_var[:, bass.ds(n, 1), 0:1].rearrange("p a d -> p (a d)"),
                                        rstd[:, bass.ds(n, 1)], ALU.subtract, ALU.mult).then_inc(staged, 1)
                        dve.wait_ge(made, n + 1)
                        v.scalar_tensor_tensor(here, bank[2 + b][:, 0:D], HEAD_DIM ** -0.5, qkv_bc[:, 0:D], ALU.mult, ALU.add).then_inc(q_done, 1)
                        need(dve, kv_out[b], i * 16)
                        v.tensor_tensor(kv_rows[:, b, :], bank[2 + b][:, D:3 * D], qkv_bc[:, D:3 * D], ALU.add).then_inc(kv_done, 1)

                turn(0)
                with dve.Fori(1, NT // 2) as i:
                    turn(i)

            @block.scalar
            def _(act):
                act.wait_ge(var_ready, 1)
                act.activation(rstd[:, :], mean_var[:, :, 1:2].rearrange("p n a -> p (n a)"), ACT.Sqrt, bias=eps_col[:, 0:1]).then_inc(rooted, 1)

                def turn(i):
                    for b in range(2):
                        n = i * 2 + b
                        act.wait_ge(moved, n + 1)
                        need(act, made, n - 1)
                        act.copy(rows_t[:, b, :], bank[b][:, 0:P]).then_inc(kept, 1)

                turn(0)
                with act.Fori(1, NT // 2) as i:
                    turn(i)

            @block.tensor
            def _(pe):
                def turn(i):
                    for b in range(2):
                        n = i * 2 + b
                        pe.wait_ge(staged, n + 1)
                        need(pe, kept, n - 1)
                        nc.tensor.transpose(bank[b][:, 0:P], rows[:, b, :], ident[:, :]).then_inc(moved, 1)
                        pe.wait_ge(kept, n + 1)
                        need(pe, kv_done, n - 1)
                        nc.tensor.matmul(bank[2 + b][:, 0:3 * D], rows_t[:, b, :], qkv_t[:, :], start=True, stop=True).then_inc(made, 1)

                turn(0)
                with pe.Fori(1, NT // 2) as i:
                    turn(i)

        GROUP = 4
        GROUPS = TURN // GROUP
        with ExitStack() as ph:
            own = ph.enter_context(phase_semaphores(nc))
            sem = lambda n: own(f"score_{n}")
            tmp = lambda n, s, d=F32: ph.enter_context(nc.sbuf_tensor(f"score_{n}", s, d))
            slots_in, local_ready, index_ready, go = sem("slots_in"), sem("local_ready"), sem("index_ready"), sem("go")
            spread, hot_ready, q_ready, product, reduced, scored = (
                sem(n) for n in ("spread", "hot_ready", "q_ready", "product", "reduced", "scored"))
            v_out = [sem(f"v_out{h}") for h in range(2)]
            index_ring = tmp("index_ring", [P, TURN], I32)
            kv_rows = tmp("kv_rows", [P, TURN, 2 * D])
            hot_t = tmp("hot_t", [P, 2, GROUP * P])
            qk = tmp("qk", [P, GROUP * D])
            part_scores = tmp("part_scores", [P, GROUP, HEADS])
            block = ph.enter_context(nc.Block())

            @block.sync
            def _(sp):
                sp.dma_start(s_slot, s_slots.rearrange("(p t) f -> p t f", p=P)).then_inc(slots_in, 16)
                sp.wait_ge(slots_in, 16)
                with sp.Fori(0, S_TURNS) as i:
                    for h in range(2):
                        for k in range(h * HALF, (h + 1) * HALF):
                            sp.wait_ge(fetched[k], (2 * S_TURNS + i + 1) * 16)
                        sp.dma_start(v_sorted[:, bass.ds(i * TURN + h * HALF, HALF), :],
                                     kv_rows[:, h * HALF:(h + 1) * HALF, D:2 * D]).then_inc(v_out[h], 16)
                for h in range(2):
                    sp.wait_ge(v_out[h], 16 * S_TURNS)

            @block.scalar
            def _(act):
                act.wait_ge(slots_in, 16)
                lo = s_slot[:, :, 1:2].rearrange("p t a -> p (t a)")
                act.copy(lo_slots[:, 0:S_TILES], lo).then_inc(local_ready, 1)
                act.copy(lo_slots_bf[:, 0:S_TILES], lo).then_inc(local_ready, 1)

                def turn(i):
                    for h in range(2):
                        need(act, product, (i - 1) * GROUPS + (h + 1) * (GROUPS // 2))
                        need(act, v_out[h], i * 16)
                        act.copy(index_ring[:, h * HALF:(h + 1) * HALF],
                                 s_slot[:, bass.ds(i * TURN + h * HALF, HALF), 0:1].bitcast(I32).rearrange("p t a -> p (t a)")).then_inc(index_ready, 1)

                turn(0)
                with act.Fori(1, S_TURNS) as i:
                    turn(i)

            @block.gpsimd
            def _(pool):
                nc.gpsimd.memset(lo_slots_bf[:, S_TILES:], EMPTY_KEY).then_inc(local_ready, 1)
                with pool.Fori(0, S_TURNS) as i:
                    for h in range(2):
                        pool.wait_ge(index_ready, 2 * i + h + 1)
                        pool.sem_inc(go, 1)
                        for k in range(h * HALF, (h + 1) * HALF):
                            nc.gpsimd.indirect_dma_start(
                                kv_rows[:, k, :], None, kv_table,
                                bass.IndirectOffsetOnAxis(ap=index_ring[:, k:k + 1], axis=0)).then_inc(fetched[k], 16)

            @block.tensor
            def _(pe):
                pe.wait_ge(local_ready, 3)

                def spread_keys(g, b, t0):
                    need(pe, hot_ready, g - 1)
                    for m in range(GROUP):
                        last = nc.tensor.matmul(bank[b][:, m * P:(m + 1) * P], lo_slots_bf[:, bass.ds(t0 + m, 1)].to_broadcast([P, P]),
                                                ident_bf[:, :], start=True, stop=True)
                    last.then_inc(spread, 1)

                def turn(i):
                    for j in range(GROUPS):
                        g = i * GROUPS + j
                        spread_keys(g + 1, (j + 1) % 2, i * TURN + (j + 1) * GROUP)
                        _, node = nc.values_load_multi_w_load_instructions(
                            node_s[0:1, bass.ds(i * TURN + j * GROUP, GROUP)], engines=[mybir.EngineType.PE],
                            min_val=0, max_val=NT - 1, skip_runtime_bounds_check_because=CLAMPED)
                        pe.wait_ge(hot_ready, g + 1)
                        need(pe, product, g - 1)
                        for m in range(GROUP):
                            last = nc.tensor.matmul(bank[2 + j % 2][:, m * D:(m + 1) * D], hot_t[:, j % 2, m * P:(m + 1) * P],
                                                    nodes[:, bass.ds(node[m], 1), :].rearrange("p a d -> p (a d)"), start=True, stop=True)
                        last.then_inc(q_ready, 1)

                spread_keys(0, 0, 0)
                turn(0)
                with pe.Fori(1, S_TURNS) as i:
                    turn(i)

            @block.vector
            def _(dve):
                v = nc.vector

                def one_hots(g, b):
                    dve.wait_ge(spread, g + 1)
                    need(dve, q_ready, g - 1)
                    v.tensor_scalar(hot_t[:, b, :], bank[b][:, :], iota_p[:, 0:1], None, ALU.is_equal).then_inc(hot_ready, 1)

                def turn(i):
                    for j in range(GROUPS):
                        g = i * GROUPS + j
                        one_hots(g + 1, (j + 1) % 2)
                        for k in range(j * GROUP, (j + 1) * GROUP):
                            dve.wait_ge(fetched[k], (2 * S_TURNS + i + 1) * 16)
                        dve.wait_ge(q_ready, g + 1)
                        need(dve, reduced, g)
                        v.tensor_tensor(qk[:, :].rearrange("p (m d) -> p m d", d=D), bank[2 + j % 2][:, :].rearrange("p (m d) -> p m d", d=D),
                                        kv_rows[:, j * GROUP:(j + 1) * GROUP, 0:D], ALU.mult).then_inc(product, 1)
                        dve.wait_ge(product, g + 1)
                        need(dve, scored, g)
                        v.tensor_reduce(part_scores[:, :, :].rearrange("p m h -> p (m h)"),
                                        qk[:, :].rearrange("p (m d) -> p m d", d=HEAD_DIM), AX.X, ALU.add).then_inc(reduced, 1)
                        dve.wait_ge(reduced, g + 1)
                        biased = s_slot[:, bass.ds(i * TURN + j * GROUP, GROUP), 2:S_FIELDS]
                        v.tensor_tensor(biased, biased, part_scores[:, :, :], ALU.add).then_inc(scored, 1)

                dve.wait_ge(slots_in, 16)
                one_hots(0, 0)
                turn(0)
                with dve.Fori(1, S_TURNS) as i:
                    turn(i)

        with ExitStack() as ph:
            own = ph.enter_context(phase_semaphores(nc))
            sem = lambda n: own(f"soft_{n}")
            tmp = lambda n, s, d=F32: ph.enter_context(nc.sbuf_tensor(f"soft_{n}", s, d))
            step, key_ready, prev_ready = sem("step"), sem("key_ready"), sem("prev_ready")
            staged, moved, kept_s, kept_b = sem("staged"), sem("moved"), sem("kept_s"), sem("kept_b")
            b_staged, ends_ready, rows_ready, carry_ready, carried = (
                sem(n) for n in ("b_staged", "ends_ready", "rows_ready", "carry_ready", "carried"))
            shifted, exped, w_moved, w_kept = sem("shifted"), sem("exped"), sem("w_moved"), sem("w_kept")
            QUARTER = S_TILES // 4
            key = tmp("key", [P, S_TILES + 1])
            new_seg = tmp("new_seg", [P, S_TILES])
            s_stage, b_stage = tmp("s_stage", [P, 2, P]), tmp("b_stage", [P, 2, P])
            ends = tmp("ends", [P, 6])
            carry_row = tmp("carry_row", [1, 6, P])
            carry_out = tmp("carry_out", [1, 2, P + HEADS])
            carry = tmp("carry", [P, 2])
            chunk_key = new_seg[:, :].rearrange("p (c t) -> p c t", c=CHUNKS)
            chunk_scores = s_slot.rearrange("p (c t) f -> p c t f", c=CHUNKS)
            QUARTERS = 4
            PIECE = CHUNK_LEN // QUARTERS
            block = ph.enter_context(nc.Block())

            @block.vector
            def _(dve):
                v = nc.vector
                link = Chain(dve, step)
                link(v.memset(key[:, 0:1], -float(P)))
                v.scalar_tensor_tensor(key[:, 1:], node_s_bc[:, :], float(P), lo_slots[:, 0:S_TILES], ALU.mult, ALU.add).then_inc(key_ready, 1)
                dve.wait_ge(key_ready, 1)
                dve.wait_ge(prev_ready, 1)
                for j in range(4):
                    cut = slice(j * QUARTER, (j + 1) * QUARTER)
                    link(v.tensor_tensor(new_seg[:, cut], bank[4 + j][:, 0:QUARTER], key[:, 1 + j * QUARTER:1 + (j + 1) * QUARTER], ALU.not_equal))
                link(v.tensor_scalar(new_seg[:, :], new_seg[:, :], BREAK, None, ALU.mult))
                done_before = link.k

                def turn(i):
                    for b in range(2):
                        g = i * 2 + b if not isinstance(i, tuple) else i[0]
                        need(dve, moved, g - 1)
                        v.tensor_copy(b_stage[:, b, :].rearrange("p (c h) -> p c h", h=HEADS),
                                      chunk_key[:, :, bass.ds(g, 1)].to_broadcast([P, CHUNKS, HEADS])).then_inc(b_staged, 1)
                        dve.wait_ge(moved, g + 1)
                        v.tensor_copy(breaks[:, bass.ds(g * P, P)], bank[2 + b][:, 0:P]).then_inc(kept_b, 1)
                        if isinstance(i, tuple):
                            break

                turn(0)
                with dve.Fori(1, CHUNK_TILES // 2) as i:
                    turn(i)
                if CHUNK_TILES % 2:
                    turn((CHUNK_TILES - 1,))
                dve.wait_ge(kept_b, CHUNK_TILES)
                dve.wait_ge(kept_s, CHUNK_TILES)
                link(v.memset(breaks[:, CHUNK_LEN:], 0.0))
                body, back = breaks[:, 0:CHUNK_LEN], breaks[:, 1:CHUNK_LEN + 1]
                link(v.tensor_reduce(ends[:, 0:1], body, AX.X, ALU.add))
                link(v.tensor_reduce(ends[:, 1:2], back, AX.X, ALU.add))
                link(v.tensor_copy(ends[:, 2:3], breaks[:, 0:1]))
                link(v.tensor_tensor_scan(seg_max, body, scores_t, BREAK, ALU.add, ALU.max))
                link(v.tensor_copy(ends[:, 3:4], seg_max[:, CHUNK_LEN - 1:CHUNK_LEN]))
                link(v.tensor_tensor_scan(seg_max[:, ::-1], back[:, ::-1], scores_t[:, ::-1], BREAK, ALU.add, ALU.max))
                v.tensor_copy(ends[:, 4:5], seg_max[:, 0:1]).then_inc(ends_ready, 1)
                dve.wait_ge(rows_ready, 1)
                dve.wait_ge(ends_ready, 1)
                link(v.tensor_copy(carry_row[:, 0:4, :].rearrange("p a b -> p (a b)"), bank[0][0:1, 0:4 * P]))
                link(v.tensor_copy(carry_row[:, 4, :], bank[1][0:1, 0:P]))
                link(v.memset(carry_out[:, :, :], BREAK))
                by_head = carry_row[:, :, :].rearrange("p a (c h) -> p a h c", h=HEADS)
                into = carry_out[:, :, :].rearrange("p a (c h) -> p a h c", h=HEADS)
                link(v.tensor_tensor(carry_row[:, 1, :], carry_row[:, 1, :], carry_row[:, 2, :], ALU.add))
                link(v.tensor_tensor(carry_row[:, 4, :], carry_row[:, 4, :], carry_row[:, 2, :], ALU.add))
                for h in range(HEADS):
                    v.tensor_tensor_scan(into[:, 0, h, 1:], by_head[:, 0, h, :], by_head[:, 3, h, :], BREAK, ALU.add, ALU.max)
                    link(v.tensor_tensor_scan(into[:, 1, h, 0:CHUNKS][:, ::-1], by_head[:, 1, h, ::-1], by_head[:, 4, h, ::-1],
                                              BREAK, ALU.add, ALU.max))
                v.tensor_copy(carry_row[:, 5, :], carry_row[:, 4, :]).then_inc(carry_ready, 1)
                dve.wait_ge(carried, 1)
                link(v.tensor_copy(carry[:, :], bank[2][:, 0:2]))
                link(v.tensor_tensor_scan(seg_max, body, scores_t, carry[:, 0:1], ALU.add, ALU.max))
                link(v.tensor_tensor_scan(seg_max[:, ::-1], back[:, ::-1], seg_max[:, ::-1], carry[:, 1:2], ALU.add, ALU.max))
                for j in range(QUARTERS):
                    cut = slice(j * PIECE, (j + 1) * PIECE)
                    v.tensor_tensor(scores_t[:, cut], scores_t[:, cut], seg_max[:, cut], ALU.subtract).then_inc(shifted, 1)

                dve.wait_ge(shifted, QUARTERS)

                def back_turn(i):
                    for b in range(2):
                        g = i * 2 + b if not isinstance(i, tuple) else i[0]
                        dve.wait_ge(w_moved, g + 1)
                        v.tensor_copy(weights.rearrange("p (c t) h -> p c t h", c=CHUNKS)[:, :, bass.ds(g, 1), :].rearrange("p c t h -> p c (t h)"),
                                      bank[4 + b][:, 0:P].rearrange("p (c h) -> p c h", h=HEADS)).then_inc(w_kept, 1)
                        if isinstance(i, tuple):
                            break

                back_turn(0)
                with dve.Fori(1, CHUNK_TILES // 2) as i:
                    back_turn(i)
                if CHUNK_TILES % 2:
                    back_turn((CHUNK_TILES - 1,))

            @block.tensor
            def _(pe):
                t = nc.tensor
                pe.wait_ge(key_ready, 1)
                for j in range(4):
                    t.matmul(bank[4 + j][:, 0:QUARTER], next_row[:, :], key[:, 1 + j * QUARTER:1 + (j + 1) * QUARTER], start=True, stop=False)
                    last = t.matmul(bank[4 + j][:, 0:QUARTER], wrap_row[:, :], key[:, j * QUARTER:(j + 1) * QUARTER], start=False, stop=True)
                last.then_inc(prev_ready, 1)

                def turn(i):
                    for b in range(2):
                        g = i * 2 + b if not isinstance(i, tuple) else i[0]
                        need(pe, kept_s, g - 1)
                        need(pe, kept_b, g - 1)
                        pe.wait_ge(staged, g + 1)
                        t.transpose(bank[b][:, 0:P], s_stage[:, b, :], ident[:, :])
                        pe.wait_ge(b_staged, g + 1)
                        t.transpose(bank[2 + b][:, 0:P], b_stage[:, b, :], ident[:, :]).then_inc(moved, 1)
                        if isinstance(i, tuple):
                            break

                turn(0)
                with pe.Fori(1, CHUNK_TILES // 2) as i:
                    turn(i)
                if CHUNK_TILES % 2:
                    turn((CHUNK_TILES - 1,))
                pe.wait_ge(ends_ready, 1)
                for n in range(5):
                    last = t.matmul(bank[n // 4][0:1, (n % 4) * P:(n % 4 + 1) * P], ends[:, n:n + 1], ident[:, :], start=True, stop=True)
                last.then_inc(rows_ready, 1)
                pe.wait_ge(carry_ready, 1)
                t.matmul(bank[2][:, 0:1], carry_out[0:1, 0, 0:P], ones[0:1, 0:1], start=True, stop=True)
                t.matmul(bank[2][:, 1:2], carry_out[0:1, 1, HEADS:P + HEADS], ones[0:1, 0:1], start=True, stop=True).then_inc(carried, 1)

                def back_turn(i):
                    for b in range(2):
                        g = i * 2 + b if not isinstance(i, tuple) else i[0]
                        pe.wait_ge(exped, g + 1)
                        need(pe, w_kept, g - 1)
                        t.transpose(bank[4 + b][:, 0:P], s_stage[:, b, :], ident[:, :]).then_inc(w_moved, 1)
                        if isinstance(i, tuple):
                            break

                back_turn(0)
                with pe.Fori(1, CHUNK_TILES // 2) as i:
                    back_turn(i)
                if CHUNK_TILES % 2:
                    back_turn((CHUNK_TILES - 1,))

            @block.scalar
            def _(act):
                def turn(i):
                    for b in range(2):
                        g = i * 2 + b if not isinstance(i, tuple) else i[0]
                        need(act, moved, g - 1)
                        act.copy(s_stage[:, b, :].rearrange("p (c h) -> p c h", h=HEADS),
                                 chunk_scores[:, :, bass.ds(g, 1), 2:S_FIELDS].rearrange("p c t h -> p c (t h)")).then_inc(staged, 1)
                        act.wait_ge(moved, g + 1)
                        act.copy(scores_t[:, bass.ds(g * P, P)], bank[b][:, 0:P]).then_inc(kept_s, 1)
                        if isinstance(i, tuple):
                            break

                turn(0)
                with act.Fori(1, CHUNK_TILES // 2) as i:
                    turn(i)
                if CHUNK_TILES % 2:
                    turn((CHUNK_TILES - 1,))
                act.wait_ge(shifted, QUARTERS)

                def exps(i):
                    for b in range(2):
                        g = i * 2 + b if not isinstance(i, tuple) else i[0]
                        need(act, w_moved, g - 1)
                        act.activation(s_stage[:, b, :], scores_t[:, bass.ds(g * P, P)], ACT.Exp).then_inc(exped, 1)
                        if isinstance(i, tuple):
                            break

                exps(0)
                with act.Fori(1, CHUNK_TILES // 2) as i:
                    exps(i)
                if CHUNK_TILES % 2:
                    exps((CHUNK_TILES - 1,))

        with ExitStack() as ph:
            own = ph.enter_context(phase_semaphores(nc))
            sem = lambda n: own(f"mix_{n}")
            tmp = lambda n, s, d=F32: ph.enter_context(nc.sbuf_tensor(f"mix_{n}", s, d))
            cleared, hot_ready, weighted, summed, added = (sem(n) for n in ("cleared", "hot_ready", "weighted", "summed", "added"))
            v_in = [sem(f"v_in{h}") for h in range(2)]
            RING = 4
            v_rows = tmp("v_rows", [P, 2, HALF, D])
            mixed = tmp("mixed", [P, 2, GROUP * D])
            hot = tmp("hot", [P, RING, P])
            block = ph.enter_context(nc.Block())

            @block.sync
            def _(sp):
                def turn(i):
                    for h in range(2):
                        need(sp, weighted, (i - 1) * GROUPS + (h + 1) * (GROUPS // 2))
                        sp.dma_start(v_rows[:, h, :, :], v_sorted[:, bass.ds(i * TURN + h * HALF, HALF), :]).then_inc(v_in[h], 16)

                turn(0)
                with sp.Fori(1, S_TURNS) as i:
                    turn(i)

            @block.gpsimd
            def _(pool):
                def turn(i):
                    for j in range(GROUPS):
                        g, h = i * GROUPS + j, j * GROUP // HALF
                        if j * GROUP % HALF == 0:
                            pool.wait_ge(v_in[h], (i + 1) * 16)
                        need(pool, summed, (g - 1) * GROUP)
                        first = j * GROUP % HALF
                        nc.gpsimd.tensor_tensor(
                            mixed[:, j % 2, :].rearrange("p (m d) -> p m d", d=HEAD_DIM),
                            v_rows[:, h, first:first + GROUP, :].rearrange("p m (h d) -> p (m h) d", d=HEAD_DIM),
                            weights[:, bass.ds(i * TURN + j * GROUP, GROUP), :].rearrange("p m h -> p (m h)").unsqueeze(2)
                            .to_broadcast([P, GROUP * HEADS, HEAD_DIM]), ALU.mult).then_inc(weighted, 1)

                turn(0)
                with pool.Fori(1, S_TURNS) as i:
                    turn(i)

            @block.vector
            def _(dve):
                nc.vector.memset(sums, 0.0).then_inc(cleared, 1)
                dve.wait_ge(cleared, 1)

                def one_hot(t, k):
                    need(dve, summed, t + 1 - RING)
                    nc.vector.tensor_scalar(hot[:, k % RING, :], iota_bf[:, :], lo_slots[:, bass.ds(t, 1)], None,
                                            ALU.is_equal).then_inc(hot_ready, 1)

                def turn(i):
                    for h in range(2):
                        _, node = nc.values_load_multi_w_load_instructions(
                            node_s[0:1, bass.ds(i * TURN + h * HALF, HALF)], engines=[mybir.EngineType.DVE],
                            min_val=0, max_val=NT - 1, skip_runtime_bounds_check_because=CLAMPED)
                        for k in range(h * HALF, (h + 1) * HALF):
                            t = i * TURN + k
                            one_hot(t + 2, k + 2)
                            dve.wait_ge(summed, t + 1)
                            need(dve, added, t)
                            here = sums[:, bass.ds(node[k % HALF], 1), :].rearrange("p a d -> p (a d)")
                            nc.vector.tensor_tensor(here, here, bank[k % RING][:, 0:D + HEADS], ALU.add).then_inc(added, 1)

                for t in range(2):
                    one_hot(t, t)
                turn(0)
                with dve.Fori(1, S_TURNS) as i:
                    turn(i)

            @block.tensor
            def _(pe):
                def turn(i):
                    for k in range(TURN):
                        t, j = i * TURN + k, k // GROUP
                        pe.wait_ge(hot_ready, t + 1)
                        need(pe, added, t + 1 - RING)
                        if k % GROUP == 0:
                            pe.wait_ge(weighted, i * GROUPS + j + 1)
                        m = k % GROUP
                        nc.tensor.matmul(bank[k % RING][:, 0:D], hot[:, k % RING, :], mixed[:, j % 2, m * D:(m + 1) * D], start=True, stop=True)
                        nc.tensor.matmul(bank[k % RING][:, D:D + HEADS], hot[:, k % RING, :],
                                         weights[:, bass.ds(t, 1), :].rearrange("p a h -> p (a h)"), start=True, stop=True).then_inc(summed, 1)

                turn(0)
                with pe.Fori(1, S_TURNS) as i:
                    turn(i)

        with ExitStack() as ph:
            own = ph.enter_context(phase_semaphores(nc))
            sem = lambda n: own(f"fin_{n}")
            tmp = lambda n, s, d=F32: ph.enter_context(nc.sbuf_tensor(f"fin_{n}", s, d))
            x1_in, step, staged, moved, kept, made, var_ready, rooted, normed, stored = (
                sem(n) for n in ("x1_in", "step", "staged", "moved", "kept", "made", "var_ready", "rooted", "normed", "stored"))
            x1 = region_a[:, 0:NT * D].rearrange("p (n d) -> p n d", d=D)
            rec = tmp("rec", [P, 2, HEADS])
            rows, rows_t, stats = tmp("rows", [P, 2, D]), tmp("rows_t", [D, 2, P]), tmp("stats", [P, 2, 6])
            tile_mv, looked = tmp("tile_mv", [P, 2, 2]), sem("looked")
            block = ph.enter_context(nc.Block())

            @block.sync
            def _(sp):
                sp.dma_start(x1, x1_dram.rearrange("(n p) d -> p n d", p=P)).then_inc(x1_in, 16)
                sp.wait_ge(x1_in, 16)
                with sp.Fori(0, NT - 1) as n:
                    sp.wait_ge(normed, n + 1)
                    sp.dma_start(out[bass.ds(n * P, P), :], x1[:, bass.ds(n, 1), :].rearrange("p a d -> p (a d)")).then_inc(stored, 16)
                sp.wait_ge(normed, NT)
                sp.dma_start(out[(NT - 1) * P:N_NODES, :], x1[0:LAST_ROWS, NT - 1, :]).then_inc(stored, 16)
                sp.wait_ge(stored, 16 * NT)

            @block.vector
            def _(dve):
                v = nc.vector
                link = Chain(dve, step)
                PER_TILE = 7

                def turn(i):
                    link.turn(i * 2 * PER_TILE)
                    for b in range(2):
                        n = i * 2 + b
                        here = sums[:, bass.ds(n, 1), :].rearrange("p a d -> p (a d)")
                        res = x1[:, bass.ds(n, 1), :].rearrange("p a d -> p (a d)")
                        link(v.tensor_scalar(rec[:, b, :], here[:, D:D + HEADS], SUM_EPS, None, ALU.add))
                        link(v.reciprocal(rec[:, b, :], rec[:, b, :]))
                        need(dve, moved, n - 1)
                        v.tensor_tensor(rows[:, b, :].rearrange("p (h d) -> p h d", d=HEAD_DIM),
                                        here[:, 0:D].rearrange("p (h d) -> p h d", d=HEAD_DIM),
                                        rec[:, b, :].unsqueeze(2).to_broadcast([P, HEADS, HEAD_DIM]), ALU.mult).then_inc(staged, 1)
                        link(v.tensor_tensor(res, res, out_bc[:, :], ALU.add))
                        dve.wait_ge(made, n + 1)
                        link(v.tensor_tensor(res, res, bank[2 + b][:, 0:D], ALU.add))
                        dve.sem_inc(looked, 1)
                        link(v.bn_stats(stats[:, b, :], res))
                        dve.sem_inc(looked, 1)
                        link(v.bn_aggr(tile_mv[:, b, :], stats[:, b, :]))
                        link(v.tensor_copy(mean_var[:, bass.ds(n, 1), :].rearrange("p a d -> p (a d)"), tile_mv[:, b, :]))

                dve.wait_ge(x1_in, 16)
                turn(0)
                with dve.Fori(1, NT // 2) as i:
                    turn(i)
                v.tensor_copy(stats[:, 0, 0:1], eps_col[:, :]).then_inc(var_ready, 1)
                link.turn(NT * PER_TILE)
                dve.wait_ge(rooted, 1)
                link(v.reciprocal(rstd[:, :], rstd[:, :]))
                with dve.Fori(0, NT) as n:
                    res = x1[:, bass.ds(n, 1), :].rearrange("p a d -> p (a d)")
                    v.tensor_scalar(res, res, mean_var[:, bass.ds(n, 1), 0:1].rearrange("p a d -> p (a d)"),
                                    rstd[:, bass.ds(n, 1)], ALU.subtract, ALU.mult).then_inc(normed, 1)

            @block.scalar
            def _(act):
                def turn(i):
                    for b in range(2):
                        n = i * 2 + b
                        act.wait_ge(moved, n + 1)
                        need(act, made, n - 1)
                        act.copy(rows_t[:, b, :], bank[b][:, 0:P]).then_inc(kept, 1)

                turn(0)
                with act.Fori(1, NT // 2) as i:
                    turn(i)
                act.wait_ge(var_ready, 1)
                act.activation(rstd[:, :], mean_var[:, :, 1:2].rearrange("p n a -> p (n a)"), ACT.Sqrt, bias=eps_col[:, 0:1]).then_inc(rooted, 1)

            @block.tensor
            def _(pe):
                def turn(i):
                    for b in range(2):
                        n = i * 2 + b
                        pe.wait_ge(staged, n + 1)
                        need(pe, kept, n - 1)
                        nc.tensor.transpose(bank[b][:, 0:P], rows[:, b, :], ident[:, :]).then_inc(moved, 1)
                        pe.wait_ge(kept, n + 1)
                        need(pe, step, (n - 2) * PER_TILE_DONE + PER_TILE_DONE)
                        nc.tensor.matmul(bank[2 + b][:, 0:D], rows_t[:, b, :], out_t[:, :], start=True, stop=True).then_inc(made, 1)

                PER_TILE_DONE = 7
                turn(0)
                with pe.Fori(1, NT // 2) as i:
                    turn(i)


_INS = ["x", "src", "dst", "edge_attr_128",
        "L0_gnn_W1", "L0_gnn_b1", "L0_gnn_W2", "L0_gnn_b2", "L0_gnn_bn_gamma", "L0_gnn_bn_beta", "L0_gnn_bn_mean", "L0_gnn_bn_var",
        "L1_gnn_q_w", "L1_gnn_q_b", "L1_gnn_k_w", "L1_gnn_k_b", "L1_gnn_v_w", "L1_gnn_v_b", "L1_gnn_out_w", "L1_gnn_out_b",
        "L1_gnn_eb_w", "L1_gnn_eb_b"]


def kernel(**inputs):
    import numpy as _np
    import concourse.bacc as _bacc
    from concourse import mybir as _mybir
    from concourse.bass_utils import run_bass_kernel_spmd as _run

    nc = _bacc.Bacc("TRN2", target_bir_lowering=False, num_devices=1)
    arrays, args = {}, []
    for name in _INS:
        a = _np.ascontiguousarray(inputs[name])
        arrays[f"in_{name}_dram"] = a
        args.append(nc.dram_tensor(f"in_{name}_dram", a.shape, _mybir.dt.from_np(a.dtype), kind="ExternalInput").ap())
    args.append(nc.dram_tensor("out_0_dram", (N_NODES, D), F32, kind="ExternalOutput").ap())
    gnn(nc, *args)
    r = _run(nc, [arrays], core_ids=[0])
    return r.results[0]["out_0_dram"]
```

```python
from contextlib import ExitStack, contextmanager

import concourse.bass as bass
from concourse import mybir

F32, I32, BF16 = mybir.dt.float32, mybir.dt.int32, mybir.dt.bfloat16
ALU, ACT, AX = mybir.AluOpType, mybir.ActivationFunctionType, mybir.AxisListType

P = 128
N_NODES, N_EDGES, D = 12500, 200000, 128
HEADS = 8
HEAD_DIM = D // HEADS
NT = -(-N_NODES // P)
LAST_ROWS = N_NODES - (NT - 1) * P
PAD_NODE = NT * P - 1
HALF = 8
TURN = 2 * HALF
E_COLS = -(-N_EDGES // (P * TURN)) * TURN
E_TURNS = E_COLS // TURN
LAST_COLS = N_EDGES - (P - 1) * E_COLS
CHUNKS = P // HEADS
S_TILES = -(-(E_COLS + NT - 1) // TURN) * TURN
S_TURNS = S_TILES // TURN
CHUNK_TILES = S_TILES // CHUNKS
CHUNK_LEN = CHUNK_TILES * P
AHEAD = 4
D_FIELDS, S_FIELDS = 2, 2 + HEADS
EMPTY_KEY = -0.5
NO_KEY = -30000.0
WINDOWS = 120
W_BLOCKS = S_TILES // WINDOWS
LN_EPS = BN_EPS = 1e-5
SUM_EPS = 1e-10
BREAK = -1e30
CHUNK = 7
N_CHUNKS = NT // CHUNK
CLAMPED = "node tiles are clamped to the last one where the table is built"

assert N_CHUNKS * CHUNK == NT and N_CHUNKS % 2 == 0 and NT % 2 == 0
assert W_BLOCKS * WINDOWS == S_TILES and CHUNK_TILES * CHUNKS == S_TILES and LAST_COLS % TURN == 0
FULL_TURNS = LAST_COLS // TURN


def need(eng, sem, value):
    if isinstance(value, int) and value <= 0:
        return
    eng.wait_ge(sem, value)


@contextmanager
def phase_semaphores(nc):
    taken = []

    def sem(name):
        taken.append(nc.alloc_semaphore(name=name))
        return taken[-1]

    yield sem
    nc.clear_and_free_semaphores(taken)
    nc.all_engine_barrier()


class Chain:

    def __init__(self, eng, sem):
        self.eng, self.sem, self.base, self.k = eng, sem, 0, 0

    def turn(self, base):
        self.base, self.k = base, 0

    def __call__(self, ins):
        ins.then_inc(self.sem, 1)
        self.k += 1
        self.eng.wait_ge(self.sem, self.base + self.k)


def gnn(nc, x, src, dst, attr, w1, b1, w2, b2, gamma, beta, bn_mean, bn_var,
        q_w, q_b, k_w, k_b, v_w, v_b, out_w, out_b, eb_w, eb_b, out):
    dram = lambda name, shape: nc.dram_tensor(name, shape, F32).ap()
    h_table = [dram("h1_table", (NT * P, D)), dram("h2_table", (NT * P, D))]
    kv_table = dram("kv_table", (NT * P, 2 * D))
    x1_dram = dram("x1_dram", (NT * P, D))
    v_sorted = dram("v_sorted", (P, S_TILES, D))
    edge_src, edge_key = dram("edge_src", (S_TILES, P)), dram("edge_key", (S_TILES, P))
    d_slots = dram("d_slots", (P * S_TILES, D_FIELDS))
    s_slots = dram("s_slots", (P * S_TILES, S_FIELDS))

    whole = ExitStack()
    with whole:
        def sb(name, shape, dt=F32):
            return whole.enter_context(nc.sbuf_tensor(name, shape, dt))

        bank = [whole.enter_context(nc.psum_tensor(f"bank{i}", [P, 512], F32)) for i in range(8)]

        iota_bf = sb("iota_bf", [P, P], BF16)
        iota_half = sb("iota_half", [P, P], BF16)
        iota_p = sb("iota_p", [P, 1])
        ident = sb("ident", [P, P])
        ident_bf = sb("ident_bf", [P, P], BF16)
        before = sb("before", [P, P])
        before_bf = sb("before_bf", [P, P], BF16)
        next_row = sb("next_row", [P, P])
        wrap_row = sb("wrap_row", [P, P])
        ones = sb("ones", [P, P])
        zeros_bf = sb("zeros_bf", [P, P], BF16)
        ones_bf = sb("ones_bf", [P, P], BF16)
        eps_col = sb("eps_col", [P, 1])
        w1_sb, w2_sb = sb("w1_sb", [D, D]), sb("w2_sb", [D, D])
        qkv_t, out_t, eb_t = sb("qkv_t", [D, 3 * D]), sb("out_t", [D, D]), sb("eb_t", [D, HEADS])
        bias_parts = sb("bias_parts", [P, 3, D], BF16)
        b1_parts, b2_parts, out_parts = (bias_parts[:, n, :] for n in range(3))
        qkv_bc = sb("qkv_bc", [P, 3 * D])
        ebb_bc = sb("ebb_bc", [P, HALF, HEADS])
        bn_cols = sb("bn_cols", [D, 4])
        bn_scale, bn_shift = sb("bn_scale", [D, 1]), sb("bn_shift", [D, 1])
        dinv = sb("dinv", [P, NT])
        base_d, base_s = sb("base_d", [NT, P]), sb("base_s", [NT, P])
        S_ROW = 32
        sum_place = sb("sum_place", [1, NT], I32)
        node_rows = sb("node_rows", [S_ROW + 1, S_TILES], I32)
        node_d, node_s = node_rows[0:1, :], node_rows[S_ROW:S_ROW + 1, :]
        unsorted = sb("unsorted", [1, 1], I32)
        window_row, window_node = sb("window_row", [P, W_BLOCKS], I32), sb("window_node", [P, W_BLOCKS])
        node_s_bc = sb("node_s_bc", [P, S_TILES], BF16)
        lo_slots = sb("lo_slots", [P, S_TILES + AHEAD])
        lo_slots_bf = sb("lo_slots_bf", [P, S_TILES + AHEAD], BF16)
        slots_words = S_TILES * S_FIELDS
        region_a = sb("region_a", [P, slots_words])
        region_b = sb("region_b", [P, max(CHUNK_LEN, (NT + 1) * (D + HEADS))])
        region_c = sb("region_c", [P, max(S_TILES * D_FIELDS, CHUNK_LEN // 2 + 1)])
        EC = E_COLS + AHEAD
        at = [0]

        def part(words):
            at[0] += words
            return region_a[:, at[0] - words:at[0]]

        src_i, dst_i = part(E_COLS).bitcast(I32), part(E_COLS).bitcast(I32)
        s_hi, s_lo, d_hi, d_lo = part(EC), part(EC), part(EC), part(EC)
        d_lo_kept = part(EC)
        s_hi_bf, d_hi_bf = part(EC // 2).bitcast(BF16), part(EC // 2).bitcast(BF16)
        tmp_a, tmp_b = part(E_COLS), part(E_COLS)
        assert at[0] <= slots_words
        s_slot = region_a[:, :].rearrange("p (t f) -> p t f", f=S_FIELDS)
        seg_max = region_a[:, 0:CHUNK_LEN]
        weights = region_a[:, 0:S_TILES * HEADS].rearrange("p (t h) -> p t h", h=HEADS)
        nodes = region_b[:, 0:NT * D].rearrange("p (n d) -> p n d", d=D)
        scores_t = region_b[:, 0:CHUNK_LEN]
        sums = region_b[:, 0:(NT + 1) * (D + HEADS)].rearrange("p (n d) -> p n d", d=D + HEADS)
        d_slot = region_c[:, 0:S_TILES * D_FIELDS].rearrange("p (t f) -> p t f", f=D_FIELDS)
        breaks = region_c[:, 0:CHUNK_LEN // 2 + 1].bitcast(BF16)

        fetched = [whole.enter_context(nc.semaphore(f"fetched{k}")) for k in range(TURN)]

        def column(flat):
            return flat.rearrange("(p one) -> p one", one=1)

        with ExitStack() as ph:
            sem = ph.enter_context(phase_semaphores(nc))
            tmp = lambda n, s, d=F32: ph.enter_context(nc.sbuf_tensor(n, s, d))
            keys_clear, keys_in, consts, weights_in = sem("keys_clear"), sem("keys_in"), sem("consts"), sem("weights_in")
            pattern_ready, filled, prep = sem("pattern_ready"), sem("filled"), sem("prep")
            w_moved, w_taken, biases_in = sem("w_moved"), sem("w_taken"), sem("biases_in")
            bn_var_eps, edges_made = sem("bn_var_eps"), sem("edges_made")
            viol, viol_ready, prev_hi_ready = tmp("viol", [P, 2]), sem("viol_ready"), sem("prev_hi_ready")
            bias_left, bias_part = tmp("bias_left", [P, 3, D]), tmp("bias_part", [P, 3, D], BF16)
            no_edges = tmp("no_edges", [S_TILES - E_COLS, 2, P])
            raw_w = tmp("raw_w", [P, 4, D])
            raw_eb = tmp("raw_eb", [HEADS, D])
            d_fill = tmp("d_fill", [P, S_TILES // 4, D_FIELDS])
            s_fill = tmp("s_fill", [P, CHUNK_TILES, S_FIELDS])
            bn_std = tmp("bn_std", [D, 1])
            block = ph.enter_context(nc.Block())
            CONSTS = 20
            whole_rows = 96

            @block.sync
            def _(sp):
                sp.wait_ge(keys_clear, 2)
                for keys, flat in ((dst_i, dst), (src_i, src)):
                    rows = flat[0:(P - 1) * E_COLS].rearrange("(p c) -> p c", c=E_COLS)
                    sp.dma_start(keys[0:whole_rows, :], rows[0:whole_rows, :]).then_inc(keys_in, 16)
                    sp.dma_start(keys[whole_rows:P - 1, :], rows[whole_rows:P - 1, :]).then_inc(keys_in, 16)
                    sp.dma_start(keys[P - 1:P, 0:LAST_COLS],
                                 flat[(P - 1) * E_COLS:N_EDGES].rearrange("(a c) -> a c", a=1)).then_inc(keys_in, 16)
                for n, w in enumerate((q_w, k_w, v_w, out_w)):
                    sp.dma_start(raw_w[:, n, :], w).then_inc(weights_in, 16)
                sp.dma_start(raw_eb[:, :], eb_w).then_inc(weights_in, 16)
                sp.dma_start(w1_sb[:, :], w1).then_inc(biases_in, 16)
                sp.dma_start(w2_sb[:, :], w2).then_inc(biases_in, 16)
                row = lambda b: b.rearrange("(a d) -> a d", a=1).to_broadcast([P, D])
                for n, b in enumerate((b1, b2, out_b)):
                    sp.dma_start(bias_left[:, n, :], row(b)).then_inc(biases_in, 16)
                for n, b in enumerate((q_b, k_b, v_b)):
                    sp.dma_start(qkv_bc[:, n * D:(n + 1) * D], row(b)).then_inc(biases_in, 16)
                for k in range(HALF):
                    sp.dma_start(ebb_bc[:, k, :],
                                 eb_b.rearrange("(a d) -> a d", a=1).to_broadcast([P, HEADS])).then_inc(biases_in, 16)
                for n, b in enumerate((gamma, beta, bn_mean, bn_var)):
                    sp.dma_start(bn_cols[:, n:n + 1], column(b)).then_inc(biases_in, 16)
                sp.wait_ge(keys_clear, 3)
                sp.dma_start(nodes[:, 0:NT - 1, :],
                             x[0:(NT - 1) * P, :].rearrange("(n p) d -> p n d", p=P)).then_inc(biases_in, 16)
                sp.dma_start(nodes[0:LAST_ROWS, NT - 1, :], x[(NT - 1) * P:N_NODES, :]).then_inc(biases_in, 16)
                sp.wait_ge(biases_in, 16 * 22)

            @block.scalar
            def _(act):
                act.wait_ge(pattern_ready, 2)
                for n in range(4):
                    step = S_TILES // 4
                    act.dma_start(d_slots.rearrange("(p t) f -> p t f", p=P)[:, n * step:(n + 1) * step, :],
                                  d_fill[:, :, :]).then_inc(filled, 16)
                for n in range(CHUNKS):
                    act.dma_start(s_slots.rearrange("(p t) f -> p t f", p=P)[:, n * CHUNK_TILES:(n + 1) * CHUNK_TILES, :],
                                  s_fill[:, :, :]).then_inc(filled, 16)
                act.wait_ge(edges_made, 4)
                for m, (keys, table) in enumerate(((tmp_a, edge_src), (tmp_b, edge_key))):
                    act.dma_start(table[0:E_COLS, :].rearrange("a d -> (a d)").rearrange("(p c) -> p c", p=P), keys).then_inc(filled, 16)
                    act.dma_start(table[E_COLS:S_TILES, :], no_edges[:, m, :]).then_inc(filled, 16)
                act.wait_ge(biases_in, 16 * 22)
                act.wait_ge(consts, 1)
                act.activation(bn_std[:, :], bn_cols[:, 3:4], ACT.Sqrt, bias=eps_col[:, 0:1]).then_inc(bn_var_eps, 1)
                act.wait_ge(filled, 16 * (4 + CHUNKS + 4))

            @block.gpsimd
            def _(pool):
                g = nc.gpsimd
                made, order = [0], consts

                def done(ins):
                    ins.then_inc(order, 1)
                    made[0] += 1
                    return made[0]

                done(g.memset(eps_col[:, :], LN_EPS))
                done(g.iota(iota_bf[:, :], pattern=[[1, P]], base=0, channel_multiplier=0,
                            allow_small_or_imprecise_dtypes=True))
                half = done(g.iota(iota_half[:, :], pattern=[[1, P]], base=0, channel_multiplier=0,
                                   allow_small_or_imprecise_dtypes=True))
                pool.wait_ge(order, half)
                done(g.tensor_scalar(iota_half[:, :], iota_half[:, :], 0.5, None, ALU.add))
                done(g.iota(iota_p[:, :], pattern=[[0, 1]], base=0, channel_multiplier=1,
                            allow_small_or_imprecise_dtypes=True))
                for m in (ident, ident_bf, next_row, wrap_row, zeros_bf):
                    done(g.memset(m[:, :], 0.0))
                for m in (ones, ones_bf, before, before_bf):
                    last = done(g.memset(m[:, :], 1.0))
                pool.wait_ge(order, last)
                for m in (ident, ident_bf):
                    done(g.affine_select(out=m[:, :], in_=m[:, :], compare_op=ALU.not_equal, fill=1.0, base=0,
                                         pattern=[[-1, P]], channel_multiplier=1))
                for m in (before, before_bf):
                    done(g.affine_select(out=m[:, :], in_=m[:, :], compare_op=ALU.is_gt, fill=0.0, base=0,
                                         pattern=[[1, P]], channel_multiplier=-1))
                done(g.affine_select(out=next_row[:, :], in_=next_row[:, :], compare_op=ALU.not_equal, fill=1.0,
                                     base=-1, pattern=[[1, P]], channel_multiplier=-1))
                done(g.affine_select(out=wrap_row[:, :], in_=wrap_row[:, :], compare_op=ALU.not_equal, fill=1.0,
                                     base=-(P - 1), pattern=[[-1, P]], channel_multiplier=1))
                pool.wait_ge(order, made[0])
                assert made[0] == CONSTS

            @block.vector
            def _(dve):
                v = nc.vector
                link = Chain(dve, prep)
                v.memset(dst_i, PAD_NODE).then_inc(keys_clear, 1)
                v.memset(src_i, PAD_NODE).then_inc(keys_clear, 1)
                v.memset(nodes[:, NT - 1, :], 0.0).then_inc(keys_clear, 1)
                link(v.memset(d_fill[:, :, :], 0.0))
                v.memset(d_fill[:, :, 1:2], EMPTY_KEY).then_inc(pattern_ready, 1)
                link(v.memset(s_fill[:, :, :], 0.0))
                v.memset(s_fill[:, :, 1:2], EMPTY_KEY).then_inc(pattern_ready, 1)
                dve.wait_ge(keys_in, 16 * 6)
                src_f, dst_f = tmp_a, tmp_b
                link(v.tensor_copy(src_f, src_i))
                link(v.tensor_copy(dst_f, dst_i))
                cut = slice(0, E_COLS)
                for a in (s_hi, s_lo, d_hi, d_lo, d_lo_kept):
                    v.memset(a[:, E_COLS:], 0.0)
                v.memset(s_hi_bf[:, E_COLS:], 0.0)
                link(v.memset(d_hi_bf[:, E_COLS:], 0.0))
                v.memset(no_edges[:, 0, :], 0.0).then_inc(edges_made, 1)
                v.memset(no_edges[:, 1, :], NO_KEY).then_inc(edges_made, 1)
                for key, hi, lo, hi_bf in ((src_f, s_hi, s_lo, s_hi_bf), (dst_f, d_hi, d_lo, d_hi_bf)):
                    as_int = lo[:, cut].bitcast(I32)
                    link(v.tensor_copy(as_int, key))
                    link(v.tensor_single_scalar(as_int, as_int, P.bit_length() - 1, ALU.arith_shift_right))
                    link(v.tensor_copy(hi[:, cut], as_int))
                    link(v.tensor_copy(hi_bf[:, cut], hi[:, cut]))
                    link(v.scalar_tensor_tensor(lo[:, cut], hi[:, cut], -float(P), key, ALU.mult, ALU.add))
                kept = d_lo_kept[:, cut]
                link(v.tensor_tensor(kept, src_f, dst_f, ALU.is_equal))
                link(v.scalar_tensor_tensor(kept, dst_f, -NO_KEY, kept, ALU.add, ALU.mult))
                v.tensor_tensor(dst_f, dst_f, kept, ALU.subtract).then_inc(edges_made, 2)
                dve.wait_ge(edges_made, 4)
                later = d_lo_kept[:, 0:E_COLS - 1]
                link(v.tensor_tensor(later, d_hi[:, 1:E_COLS], d_hi[:, 0:E_COLS - 1], ALU.is_lt))
                link(v.tensor_reduce(viol[:, 0:1], later, AX.X, ALU.add))
                link(v.scalar_tensor_tensor(kept, d_hi[:, cut], -float(P), dst_f, ALU.mult, ALU.add))
                dve.wait_ge(prev_hi_ready, 1)
                link(v.tensor_tensor(viol[:, 1:2], d_hi[:, 0:1], bank[2][:, 0:1], ALU.is_lt))
                v.tensor_tensor(viol[:, 0:1], viol[:, 0:1], viol[:, 1:2], ALU.add).then_inc(viol_ready, 1)
                dve.wait_ge(prev_hi_ready, 2)
                link(v.tensor_scalar(unsorted[:, :], bank[3][0:1, 0:1], 1.0, None, ALU.min))
                dve.wait_ge(w_moved, 5)
                link(v.tensor_copy(qkv_t[:, :], bank[0][:, 0:3 * D]))
                link(v.tensor_copy(out_t[:, :], bank[0][:, 3 * D:4 * D]))
                link(v.tensor_copy(eb_t[:, :], bank[1][:, 0:HEADS]))
                dve.wait_ge(biases_in, 16 * 22)
                dve.wait_ge(bn_var_eps, 1)
                link(v.reciprocal(bn_std[:, :], bn_std[:, :]))
                link(v.tensor_tensor(bn_scale[:, :], bn_cols[:, 0:1], bn_std[:, :], ALU.mult))
                link(v.tensor_tensor(bn_shift[:, :], bn_cols[:, 2:3], bn_scale[:, :], ALU.mult))
                link(v.tensor_tensor(bn_shift[:, :], bn_cols[:, 1:2], bn_shift[:, :], ALU.subtract))
                link(v.tensor_scalar(qkv_bc[:, 0:D], qkv_bc[:, 0:D], HEAD_DIM ** -0.5, None, ALU.mult))
                link(v.memset(bias_parts[:, :, :], 0.0))
                for at in (0, 32, 64):
                    link(v.tensor_copy(bias_part[:, :, :], bias_left[:, :, :]))
                    link(v.tensor_copy(bias_parts[at:at + 1, :, :], bias_part[at:at + 1, :, :]))
                    link(v.tensor_tensor(bias_left[:, :, :], bias_left[:, :, :], bias_part[:, :, :], ALU.subtract))

            @block.tensor
            def _(pe):
                pe.wait_ge(consts, CONSTS)
                pe.wait_ge(weights_in, 16 * 5)
                for n in range(4):
                    nc.tensor.transpose(bank[0][:, n * D:(n + 1) * D], raw_w[:, n, :], ident[:, :]).then_inc(w_moved, 1)
                nc.tensor.transpose(bank[1][:, 0:HEADS], raw_eb[:, :], ident[0:HEADS, 0:HEADS]).then_inc(w_moved, 1)
                pe.wait_ge(edges_made, 4)
                nc.tensor.matmul(bank[2][:, 0:1], next_row[:, :], d_hi[:, E_COLS - 1:E_COLS], start=True, stop=True).then_inc(prev_hi_ready, 1)
                pe.wait_ge(viol_ready, 1)
                nc.tensor.matmul(bank[3][:, 0:1], ones[:, :], viol[:, 0:1], start=True, stop=True).then_inc(prev_hi_ready, 1)

        class Count:
            RING = TURN
            scatters = False

            def __init__(self, sem, tmp, hi, lo, lo_kept=None, lead=0):
                self.lead = lead
                self.hi, self.lo, self.lo_kept = hi, lo, lo_kept
                self.hot_ready, self.signs_ready, self.used = sem("hot_ready"), sem("signs_ready"), sem("hot_used")
                self.hot = tmp("hot_hi", [P, self.RING, NT], BF16)
                self.sign = tmp("sign", [P, self.RING, P], BF16)
                if lo_kept is not None:
                    self.kept = tmp("hot_kept", [P, self.RING, P], BF16)
                    self.keys, self.keys_ready = tmp("keys", [P, 3, TURN]), sem("keys_ready")

            def stage(self, pool, i, h):
                need(pool, self.used, (i - 1) * TURN + (h + 1) * HALF)
                for n, keys in enumerate((self.hi, self.lo, self.lo_kept)):
                    nc.gpsimd.tensor_copy(self.keys[:, n, h * HALF:(h + 1) * HALF], keys[:, bass.ds(i * TURN + h * HALF, HALF)]).then_inc(self.keys_ready, 1)

            def key(self, n, c, k):
                if self.lo_kept is not None:
                    return self.keys[:, n, k:k + 1]
                return (self.hi, self.lo)[n][:, bass.ds(c, 1)]

            def ready(self, eng, i, c, k):
                if k % HALF == 0:
                    need(eng, self.used, c + HALF - self.RING)
                    if self.lo_kept is not None:
                        eng.wait_ge(self.keys_ready, (2 * i + k // HALF % 2 + 1) * 3)

            def one_hots(self, dve, i, k):
                c, slot = i * TURN + k, k % self.RING
                self.ready(dve, i, c, k)
                last = nc.vector.tensor_scalar(self.hot[:, slot, :], iota_bf[:, 0:NT], self.key(0, c, k), None, ALU.is_equal)
                if self.lo_kept is not None:
                    last = nc.vector.tensor_scalar(self.kept[:, slot, :], iota_bf[:, :], self.key(2, c, k), None, ALU.is_equal)
                last.then_inc(self.hot_ready, 1)

            def vector_start(self, dve):
                for k in range(self.lead):
                    self.one_hots(dve, 0, k)

            def vector_step(self, dve, i, k):
                self.one_hots(dve, i, k + self.lead)

            def vector_end_step(self, dve, i, k):
                pass

            def scalar_step(self, act, i, k):
                c, slot = i * TURN + k, k % self.RING
                self.ready(act, i, c, k)
                nc.scalar.activation(self.sign[:, slot, :], iota_half[:, :], ACT.Sign, bias=self.key(1, c, k), scale=-1.0).then_inc(self.signs_ready, 1)

            def zeros(self, **at):
                for n in range(1 if self.lo_kept is None else 2):
                    nc.tensor.matmul(bank[n][0:NT, 0:P], zeros_bf[:, 0:NT], zeros_bf[:, :], **at)

            def tensor_start(self, pe):
                self.zeros(start=True, stop=False)

            def tensor_step(self, pe, i, k):
                c, slot = i * TURN + k, k % self.RING
                pe.wait_ge(self.hot_ready, c + 1)
                pe.wait_ge(self.signs_ready, c + 1)
                last = nc.tensor.matmul(bank[0][0:NT, 0:P], self.hot[:, slot, :], self.sign[:, slot, :], start=False, stop=False)
                if self.lo_kept is not None:
                    last = nc.tensor.matmul(bank[1][0:NT, 0:P], self.hot[:, slot, :], self.kept[:, slot, :], start=False, stop=False)
                last.then_inc(self.used, 1)

            def tensor_end_step(self, pe, i, k):
                pass

            def tensor_end(self, pe):
                self.zeros(start=False, stop=True)

            def sync(self, sp):
                pass

        class Sort:
            RING = 4
            scatters = True
            CHAINED = 2 * 4

            def __init__(self, sem, tmp, hi, lo, hi_bf, lo_kept, base, index, table, fields, with_bias):
                self.hi, self.lo, self.hi_bf, self.lo_kept, self.base = hi, lo, hi_bf, lo_kept, base
                self.index, self.table, self.with_bias = index, table, with_bias
                (self.hot_ready, self.tile_row_ready, self.masks_ready, self.counted, self.next_ready, self.found, self.picked,
                 self.slot_step, self.payload_ready, self.go, self.slots_in) = (sem(n) for n in (
                     "hot_ready", "tile_row_ready", "masks_ready", "counted", "next_ready", "found", "picked",
                     "slot_step", "payload_ready", "go", "slots_in"))
                self.scattered = [sem(f"scattered{h}") for h in range(2)]
                self.hot_hi, self.hot_lo = tmp("hot_hi", [P, self.RING, NT], BF16), tmp("hot_lo", [P, self.RING, P], BF16)
                self.earlier = tmp("earlier", [P, self.RING, P], BF16)
                self.hi_t = tmp("hi_t", [NT, self.RING, P])
                self.next_slot = tmp("next_slot", [NT, 2, P])
                self.junk = tmp("junk", [P, P])
                self.slot = tmp("slot", [P, 2, HALF])
                self.slot_i, self.row_i, self.tile_i = (tmp(n, [P, HALF], I32) for n in ("slot_i", "row_i", "tile_i"))
                self.where = tmp("where", [P, 2, HALF], I32)
                self.payload = tmp("payload", [P, 2, HALF, fields])
                self.tile_row, self.found_in, self.running = bank[0], [bank[1], bank[2]], bank[3]
                if with_bias:
                    self.attr_in = [sem(f"attr_in{h}") for h in range(2)]
                    self.attr_moved, self.attr_kept, self.bias_ready = sem("attr_moved"), sem("attr_kept"), sem("bias_ready")
                    self.attr_sb = tmp("attr_sb", [P, 2, HALF, D])
                    self.attr_t = tmp("attr_t", [D, 2, 4 * P])
                    self.attr_bank, self.bias_out = bank[4], bank[5]

            def one_hots(self, c, k):
                s = k % self.RING
                need(self.dve, self.found, c + 1 - self.RING)
                nc.vector.tensor_scalar(self.hot_hi[:, s, :], iota_bf[:, 0:NT], self.hi[:, bass.ds(c, 1)], None, ALU.is_equal)
                nc.vector.tensor_scalar(self.hot_lo[:, s, :], iota_bf[:, :], self.lo[:, bass.ds(c, 1)], None, ALU.is_equal).then_inc(self.hot_ready, 1)

            def masks(self, c, k):
                s = k % self.RING
                need(self.dve, self.tile_row_ready, c + 1)
                nc.vector.tensor_scalar(self.hi_t[:, s, :], self.tile_row[0:NT, 0:P], iota_p[0:NT, 0:1], None, ALU.is_equal)
                nc.vector.scalar_tensor_tensor(self.earlier[:, s, :], self.tile_row[:, 0:P], self.hi[:, bass.ds(c, 1)], before_bf[:, :],
                                               ALU.is_equal, ALU.mult).then_inc(self.masks_ready, 1)

            def vector_start(self, dve):
                self.dve, self.link = dve, Chain(dve, self.slot_step)
                for c in range(2):
                    self.one_hots(c, c)
                self.masks(0, 0)

            def vector_step(self, dve, i, k):
                c = i * TURN + k
                self.one_hots(c + 2, k + 2)
                self.masks(c + 1, k + 1)

            def vector_end_step(self, dve, i, k):
                v, link = nc.vector, self.link
                c, h = i * TURN + k, k // HALF
                if k == 0:
                    link.turn(i * self.CHAINED)
                dve.wait_ge(self.found, c + 1)
                need(dve, self.picked, c)
                v.tensor_tensor_reduce(out=self.junk[:, :], in0=self.found_in[k % 2][:, 0:P], in1=self.hot_lo[:, k % self.RING, :],
                                       scale=1.0, scalar=0.0, op0=ALU.mult, op1=ALU.add,
                                       accum_out=self.slot[:, h, k % HALF:k % HALF + 1]).then_inc(self.picked, 1)
                if k % HALF < HALF - 1:
                    return
                cols = bass.ds(i * TURN + h * HALF, HALF)
                dve.wait_ge(self.picked, c + 1)
                link(v.tensor_copy(self.slot_i[:, :], self.slot[:, h, :]))
                link(v.tensor_single_scalar(self.tile_i[:, :], self.slot_i[:, :], P.bit_length() - 1, ALU.arith_shift_right))
                link(v.tensor_single_scalar(self.row_i[:, :], self.slot_i[:, :], P - 1, ALU.bitwise_and))
                need(dve, self.scattered[h], i * HALF * 16)
                link(v.scalar_tensor_tensor(self.where[:, h, :], self.row_i[:, :], float(S_TILES), self.tile_i[:, :], ALU.mult, ALU.add))
                v.tensor_copy(self.payload[:, h, :, 0:1].bitcast(I32).rearrange("p k a -> p (k a)"), self.index[:, cols])
                if self.with_bias:
                    dve.wait_ge(self.bias_ready, 2 * i + h + 1)
                    v.tensor_tensor(self.payload[:, h, :, 2:S_FIELDS],
                                    self.bias_out[:, h * HALF * HEADS:(h + 1) * HALF * HEADS].rearrange("p (k a) -> p k a", a=HEADS),
                                    ebb_bc[:, :, :], ALU.add)
                v.tensor_copy(self.payload[:, h, :, 1:2].rearrange("p k a -> p (k a)"), self.lo_kept[:, cols]).then_inc(self.payload_ready, 1)

            def spread_tiles(self, pe, c):
                need(pe, self.masks_ready, c)
                nc.tensor.matmul(self.tile_row[:, 0:P], self.hi_bf[:, bass.ds(c, 1)].to_broadcast([P, P]), ident_bf[:, :],
                                 start=True, stop=True).then_inc(self.tile_row_ready, 1)

            def tensor_start(self, pe):
                nc.tensor.matmul(self.running[0:NT, 0:P], ident[0:NT, 0:NT], self.base[:, :], start=True, stop=True).then_inc(self.counted, 1)
                for c in range(2):
                    self.spread_tiles(pe, c)

            def tensor_step(self, pe, i, k):
                t = nc.tensor
                c, s = i * TURN + k, k % self.RING
                pe.wait_ge(self.hot_ready, c + 1)
                pe.wait_ge(self.next_ready, c + 1)
                t.matmul(self.running[0:NT, 0:P], self.hot_hi[:, s, :], self.hot_lo[:, s, :], start=False, stop=True,
                         skip_group_check=True).then_inc(self.counted, 1)
                pe.wait_ge(self.masks_ready, c + 1)
                need(pe, self.picked, c - 1)
                t.matmul(self.found_in[k % 2][:, 0:P], self.hi_t[:, s, :], self.next_slot[:, k % 2, :], start=True, stop=False)
                t.matmul(self.found_in[k % 2][:, 0:P], self.earlier[:, s, :], self.hot_lo[:, s, :], start=False, stop=True).then_inc(self.found, 1)
                if not self.with_bias:
                    return
                q, h, j = 2 * i + k // HALF, k // HALF, k % HALF
                if j in (1, 3):
                    g = j // 2
                    if g == 0:
                        pe.wait_ge(self.attr_in[h], (i + 1) * (16 * 3))
                    need(pe, self.attr_kept, q * 2 + g)
                    for m in range(4):
                        last = t.transpose(self.attr_bank[:, m * P:(m + 1) * P], self.attr_sb[:, h, g * 4 + m, :], ident[:, :])
                    last.then_inc(self.attr_moved, 1)
                if j in (4, 6):
                    g = (j - 4) // 2
                    pe.wait_ge(self.attr_kept, q * 2 + g + 1)
                    need(pe, self.payload_ready, q)
                    for m in range(4):
                        at_col = (h * HALF + g * 4 + m) * HEADS
                        last = t.matmul(self.bias_out[:, at_col:at_col + HEADS], self.attr_t[:, g, m * P:(m + 1) * P], eb_t[:, :],
                                        start=True, stop=True)
                    if g == 1:
                        last.then_inc(self.bias_ready, 1)

            def tensor_end_step(self, pe, i, k):
                self.spread_tiles(pe, i * TURN + k + 2)

            def tensor_end(self, pe):
                pass

            def scalar_step(self, act, i, k):
                c = i * TURN + k
                act.wait_ge(self.counted, c + 1)
                need(act, self.found, c - 1)
                nc.scalar.copy(self.next_slot[:, k % 2, :], self.running[0:NT, 0:P]).then_inc(self.next_ready, 1)
                if self.with_bias and k % HALF in (2, 4):
                    q, g = 2 * i + k // HALF, k % HALF // 2 - 1
                    act.wait_ge(self.attr_moved, q * 2 + g + 1)
                    need(act, self.bias_ready, q)
                    nc.scalar.copy(self.attr_t[:, g, :], self.attr_bank[:, :]).then_inc(self.attr_kept, 1)

            def scatter(self, pool, i, h):
                pool.wait_ge(self.payload_ready, 2 * i + h + 1)
                pool.sem_inc(self.go, 1)
                for k in range(HALF):
                    nc.gpsimd.indirect_dma_start(self.table, bass.IndirectOffsetOnAxis(ap=self.where[:, h, k:k + 1], axis=0),
                                                 self.payload[:, h, k, :], None).then_inc(self.scattered[h], 16)

            def scatter_end(self, pool):
                for h in range(2):
                    pool.wait_ge(self.scattered[h], E_TURNS * HALF * 16)

            def sync(self, sp):
                if not self.with_bias:
                    return
                attr_rows = attr[0:(P - 1) * E_COLS, :].rearrange("(p c) d -> p c d", c=E_COLS)
                attr_last = attr[(P - 1) * E_COLS:N_EDGES, :].rearrange("(p c) d -> p c d", p=1)
                whole_rows = 96

                def load(i, h, last_too):
                    need(sp, self.attr_moved, (2 * (i - 1) + h) * 2 + 2)
                    cols = bass.ds(i * TURN + h * HALF, HALF)
                    sp.dma_start(self.attr_sb[0:whole_rows, h, :, :], attr_rows[0:whole_rows, cols, :]).then_inc(self.attr_in[h], 16)
                    sp.dma_start(self.attr_sb[whole_rows:P - 1, h, :, :], attr_rows[whole_rows:P - 1, cols, :]).then_inc(self.attr_in[h], 16)
                    again = cols if last_too else bass.ds(h * HALF, HALF)
                    sp.dma_start(self.attr_sb[P - 1:P, h, :, :], attr_last[:, again, :]).then_inc(self.attr_in[h], 16)

                for h in range(2):
                    load(0, h, True)
                with sp.Fori(1, FULL_TURNS) as i:
                    for h in range(2):
                        load(i, h, True)
                with sp.Fori(FULL_TURNS, E_TURNS) as i:
                    for h in range(2):
                        load(i, h, False)

        def count_destinations():
            with ExitStack() as ph:
                own = ph.enter_context(phase_semaphores(nc))
                work = Count(lambda n: own(f"count_d_{n}"),
                             lambda n, s, d=F32: ph.enter_context(nc.sbuf_tensor(f"count_d_{n}", s, d)), d_hi, d_lo, d_lo_kept)
                block = ph.enter_context(nc.Block())

                @block.gpsimd
                def _(pool):
                    def turn(i):
                        for h in range(2):
                            work.stage(pool, i, h)

                    turn(0)
                    with pool.Fori(1, E_TURNS) as i:
                        turn(i)

                @block.vector
                def _(dve):
                    def turn(i):
                        for k in range(TURN):
                            work.vector_step(dve, i, k)

                    turn(0)
                    with dve.Fori(1, E_TURNS) as i:
                        turn(i)

                @block.scalar
                def _(act):
                    def turn(i):
                        for k in range(TURN):
                            work.scalar_step(act, i, k)

                    turn(0)
                    with act.Fori(1, E_TURNS) as i:
                        turn(i)

                @block.tensor
                def _(pe):
                    work.tensor_start(pe)
                    with pe.Fori(0, E_TURNS) as i:
                        for k in range(TURN):
                            work.tensor_step(pe, i, k)
                    work.tensor_end(pe)

        def find_bases(name, base, node, row, by_dst):
            with ExitStack() as ph:
                own = ph.enter_context(phase_semaphores(nc))
                sem = lambda n: own(f"{name}_{n}")
                tmp = lambda n, s, d=F32: ph.enter_context(nc.sbuf_tensor(f"{name}_{n}", s, d))
                step, edges_ready, first_ready, tiles_ready, starts_ready, mask_ready, nodes_ready, iota_made = (
                    sem(n) for n in ("step", "edges_ready", "first_ready", "tiles_ready", "starts_ready", "mask_ready", "nodes_ready", "iota_made"))
                deg_ready, deg_moved, deg_root, map_ready, rows_ready = (
                    sem(n) for n in ("deg_ready", "deg_moved", "deg_root", "map_ready", "rows_ready"))
                upto = tmp("upto", [NT, P])
                edges, first, n_tiles, start_tile, end_tile, start_slot, some = (
                    tmp(n, [NT, 1]) for n in ("edges", "first", "n_tiles", "start_tile", "end_tile", "start_slot", "some"))
                bounds, bounds_i = tmp("bounds", [NT, 2]), tmp("bounds_i", [NT, 2], I32)
                tile_map = tmp("tile_map", [NT, 2])
                passed, iota_t = tmp("passed", [NT, S_TILES]), tmp("iota_t", [NT, S_TILES])
                if by_dst:
                    deg, deg_t = tmp("deg", [NT, P]), tmp("deg_t", [P, NT])
                    inside, tile_no = tmp("inside", [NT, S_TILES]), tmp("tile_no", [P, W_BLOCKS])
                QUARTER = S_TILES // 4
                SHIFT = P.bit_length() - 1
                block = ph.enter_context(nc.Block())

                @block.vector
                def _(dve):
                    v = nc.vector
                    link = Chain(dve, step)
                    if by_dst:
                        v.tensor_scalar(deg[:, :], bank[1][0:NT, 0:P], 1.0, None, ALU.add).then_inc(deg_ready, 1)
                    link(v.tensor_copy(upto[:, :], bank[0][0:NT, 0:P]))
                    link(v.tensor_scalar(edges[:, :], upto[:, P - 1:P], -1.0, None, ALU.mult))
                    link(v.tensor_scalar(upto[:, :], upto[:, :], edges[:, :], -0.5, ALU.subtract, ALU.mult))
                    if by_dst:
                        v.tensor_copy(first[:, :], edges[:, :]).then_inc(edges_ready, 1)
                        dve.wait_ge(first_ready, 1)
                        link(v.tensor_copy(bounds[:, 0:1], bank[3][0:NT, 0:1]))
                        link(v.tensor_scalar(bounds[:, 1:2], bounds[:, 0:1], edges[:, :], -1.0, ALU.add, ALU.add))
                        link(v.tensor_copy(bounds_i[:, :], bounds[:, :]))
                        link(v.tensor_single_scalar(bounds_i[:, :], bounds_i[:, :], SHIFT, ALU.arith_shift_right))
                        link(v.tensor_copy(bounds[:, :], bounds_i[:, :]))
                        link(v.tensor_scalar(n_tiles[:, :], bounds[:, 1:2], bounds[:, 0:1], 1.0, ALU.subtract, ALU.add))
                        link(v.tensor_scalar(some[:, :], edges[:, :], 1.0, None, ALU.min))
                        v.tensor_tensor(n_tiles[:, :], n_tiles[:, :], some[:, :], ALU.mult).then_inc(tiles_ready, 1)
                    else:
                        link(v.tensor_scalar(bounds[:, 0:1], edges[:, :], float(P - 1), None, ALU.add))
                        link(v.tensor_copy(bounds_i[:, 0:1], bounds[:, 0:1]))
                        link(v.tensor_single_scalar(bounds_i[:, 0:1], bounds_i[:, 0:1], SHIFT, ALU.arith_shift_right))
                        v.tensor_copy(n_tiles[:, :], bounds_i[:, 0:1]).then_inc(tiles_ready, 1)
                    dve.wait_ge(tiles_ready, 1)
                    dve.wait_ge(starts_ready, 1)
                    link(v.tensor_copy(start_tile[:, :], bank[4][0:NT, 0:1]))
                    link(v.tensor_tensor(end_tile[:, :], start_tile[:, :], n_tiles[:, :], ALU.add))
                    link(v.tensor_scalar(start_slot[:, :], start_tile[:, :], float(P), None, ALU.mult))
                    link(v.tensor_copy(base[:, 0:1], start_slot[:, :]))
                    link(v.tensor_scalar(base[:, 1:], upto[:, 0:P - 1], start_slot[:, :], None, ALU.add))
                    if by_dst:
                        link(v.tensor_tensor(tile_map[:, 0:1], bounds[:, 0:1], start_tile[:, :], ALU.subtract))
                        link(v.tensor_scalar(tile_map[:, 1:2], iota_p[0:NT, :], float(P), None, ALU.mult))
                    dve.wait_ge(iota_made, 2 if by_dst else 1)
                    v.tensor_scalar(passed[:, :], iota_t[0:NT, :], end_tile[:, :], None, ALU.is_ge).then_inc(mask_ready, 1)
                    if by_dst:
                        dve.wait_ge(mask_ready, 1)
                        v.scalar_tensor_tensor(inside[:, :], iota_t[0:NT, :], start_tile[:, :], passed[:, :], ALU.is_ge, ALU.subtract).then_inc(map_ready, 1)
                    dve.wait_ge(nodes_ready, 1)
                    for j in range(4):
                        part_of = slice(j * QUARTER, (j + 1) * QUARTER)
                        if not by_dst:
                            link(v.tensor_scalar(node_s_bc[:, part_of], bank[4 + j][:, 0:QUARTER], float(NT - 1), None, ALU.min))
                        link(v.tensor_scalar(node[:, part_of], bank[4 + j][row:row + 1, 0:QUARTER], float(NT - 1), None, ALU.min))
                    if by_dst:
                        dve.wait_ge(rows_ready, 1)
                        mapped = bank[1][0:WINDOWS, 0:2 * W_BLOCKS].rearrange("p (b a) -> p a b", a=2)
                        link(v.tensor_tensor(window_row[0:WINDOWS, :], mapped[:, 0, :], tile_no[0:WINDOWS, :], ALU.add))
                        link(v.tensor_copy(window_node[0:WINDOWS, :], mapped[:, 1, :]))
                        dve.wait_ge(deg_root, 1)
                        link(v.reciprocal(dinv[:, :], deg_t[:, :]))

                @block.tensor
                def _(pe):
                    if by_dst:
                        pe.wait_ge(deg_ready, 1)
                        nc.tensor.transpose(bank[5][:, 0:NT], deg[:, :], ident[0:NT, 0:NT]).then_inc(deg_moved, 1)
                        pe.wait_ge(edges_ready, 1)
                        nc.tensor.matmul(bank[3][0:NT, 0:1], before[0:NT, 0:NT], first[:, :], start=True, stop=True).then_inc(first_ready, 1)
                    pe.wait_ge(tiles_ready, 1)
                    nc.tensor.matmul(bank[4][0:NT, 0:1], before[0:NT, 0:NT], n_tiles[:, :], start=True, stop=True).then_inc(starts_ready, 1)
                    if by_dst:
                        pe.wait_ge(deg_root, 1)
                    pe.wait_ge(mask_ready, 1)
                    for j in range(4):
                        last = nc.tensor.matmul(bank[4 + j][:, 0:QUARTER], ones[0:NT, :], passed[:, j * QUARTER:(j + 1) * QUARTER],
                                                start=True, stop=True)
                    last.then_inc(nodes_ready, 1)
                    if by_dst:
                        pe.wait_ge(map_ready, 1)
                        for b in range(W_BLOCKS):
                            last = nc.tensor.matmul(bank[1][0:WINDOWS, 2 * b:2 * b + 2], inside[:, b * WINDOWS:(b + 1) * WINDOWS],
                                                    tile_map[:, :], start=True, stop=True)
                        last.then_inc(rows_ready, 1)

                @block.gpsimd
                def _(pool):
                    nc.gpsimd.iota(iota_t[:, :], pattern=[[1, S_TILES]], base=0, channel_multiplier=0,
                                   allow_small_or_imprecise_dtypes=True).then_inc(iota_made, 1)
                    if by_dst:
                        nc.gpsimd.iota(tile_no[:, :], pattern=[[WINDOWS, W_BLOCKS]], base=0, channel_multiplier=1,
                                       allow_small_or_imprecise_dtypes=True).then_inc(iota_made, 1)

                if by_dst:
                    @block.scalar
                    def _(act):
                        act.wait_ge(deg_moved, 1)
                        act.activation(deg_t[:, :], bank[5][:, 0:NT], ACT.Sqrt).then_inc(deg_root, 1)

        def window_slots():
            with ExitStack() as ph:
                own = ph.enter_context(phase_semaphores(nc))
                sem = lambda n: own(f"window_{n}")
                tmp = lambda n, s, d=F32: ph.enter_context(nc.sbuf_tensor(f"window_{n}", s, d))
                rows_in, local, moved, kept = [sem(f"rows_in{m}") for m in range(2)], sem("local"), sem("moved"), sem("kept")
                edge_rows = [tmp(n, [WINDOWS, W_BLOCKS, P]) for n in ("src_rows", "key_rows")]
                PER_BANK = 4
                W_BANKS = -(-W_BLOCKS // PER_BANK)
                blocks_of = lambda n: range(n * PER_BANK, min(W_BLOCKS, (n + 1) * PER_BANK))
                block = ph.enter_context(nc.Block())

                @block.gpsimd
                def _(pool):
                    for m, table in enumerate((edge_src, edge_key)):
                        for b in range(W_BLOCKS):
                            nc.gpsimd.indirect_dma_start(edge_rows[m][:, b, :], None, table,
                                                         bass.IndirectOffsetOnAxis(ap=window_row[0:WINDOWS, b:b + 1], axis=0)).then_inc(rows_in[m], 16)

                @block.tensor
                def _(pe):
                    for m in range(2):
                        if m == 0:
                            pe.wait_ge(rows_in[0], 16 * W_BLOCKS)
                        else:
                            pe.wait_ge(local, 1)
                        for n in range(W_BANKS):
                            for b in blocks_of(n):
                                last = nc.tensor.transpose(bank[m * W_BANKS + n][:, (b % PER_BANK) * P:(b % PER_BANK) * P + WINDOWS],
                                                           edge_rows[m][:, b, :], ident[0:WINDOWS, 0:WINDOWS])
                            last.then_inc(moved, 1)

                @block.vector
                def _(dve):
                    def keep(m):
                        for n in range(W_BANKS):
                            dve.wait_ge(moved, m * W_BANKS + n + 1)
                            held = len(blocks_of(n))
                            field = d_slot[:, n * PER_BANK * WINDOWS:(n * PER_BANK + held) * WINDOWS, m:m + 1]
                            nc.vector.tensor_copy((field.bitcast(I32) if m == 0 else field).rearrange("p (b t) a -> p b (t a)", t=WINDOWS),
                                                  bank[m * W_BANKS + n][:, 0:held * P].rearrange("p (b t) -> p b t", t=P)[:, :, 0:WINDOWS]).then_inc(kept, 1)

                    keep(0)
                    dve.wait_ge(rows_in[1], 16 * W_BLOCKS)
                    nc.vector.tensor_tensor(edge_rows[1][:, :, :], edge_rows[1][:, :, :],
                                            window_node[0:WINDOWS, :].unsqueeze(2).to_broadcast([WINDOWS, W_BLOCKS, P]), ALU.subtract).then_inc(local, 1)
                    keep(1)

        def sort_destinations():
            @contextmanager
            def when_unsorted(eng):
                with eng.If(eng.value_load(unsorted[0:1, 0:1]) != 0):
                    yield

            with ExitStack() as ph:
                own = ph.enter_context(phase_semaphores(nc))
                work = Sort(lambda n: own(f"sort_d_{n}"),
                            lambda n, s, d=F32: ph.enter_context(nc.sbuf_tensor(f"sort_d_{n}", s, d)),
                            d_hi, d_lo, d_hi_bf, d_lo_kept, base_d, src_i, d_slots, D_FIELDS, False)
                block = ph.enter_context(nc.Block())

                @block.vector
                def _(dve):
                    def turn(i):
                        for k in range(TURN):
                            work.vector_step(dve, i, k)
                            work.vector_end_step(dve, i, k)

                    with when_unsorted(dve):
                        work.vector_start(dve)
                        turn(0)
                        with dve.Fori(1, E_TURNS) as i:
                            turn(i)

                @block.tensor
                def _(pe):
                    def turn(i):
                        for k in range(TURN):
                            work.tensor_step(pe, i, k)
                            work.tensor_end_step(pe, i, k)

                    with when_unsorted(pe):
                        work.tensor_start(pe)
                        turn(0)
                        with pe.Fori(1, E_TURNS) as i:
                            turn(i)

                @block.scalar
                def _(act):
                    def turn(i):
                        for k in range(TURN):
                            work.scalar_step(act, i, k)

                    with when_unsorted(act):
                        turn(0)
                        with act.Fori(1, E_TURNS) as i:
                            turn(i)

                @block.gpsimd
                def _(pool):
                    with when_unsorted(pool):
                        with pool.Fori(0, E_TURNS) as i:
                            for h in range(2):
                                work.scatter(pool, i, h)
                        work.scatter_end(pool)
                        pool.dma_start(d_slot, d_slots.rearrange("(p t) f -> p t f", p=P)).then_inc(work.slots_in, 16)
                        pool.wait_ge(work.slots_in, 16)

        def by_two(eng, body):
            body(0)
            with eng.Fori(1, NT // 2 - 1) as i:
                body(i)
            body(NT // 2 - 1)

        def in_range(n):
            return not isinstance(n, int) or n < NT

        def tile_of(rows, n):
            return rows[:, bass.ds(n, 1), :].rearrange("p a d -> p (a d)")

        def linear(name, w_sb, b_parts, table, normed):
            with ExitStack() as ph:
                own = ph.enter_context(phase_semaphores(nc))
                sem = lambda n: own(f"{name}_{n}")
                tmp = lambda n, s, d=F32: ph.enter_context(nc.sbuf_tensor(f"{name}_{n}", s, d))
                staged, moved, kept, made, scaled, stored = (sem(n) for n in ("staged", "moved", "kept", "made", "scaled", "stored"))
                rows, rows_t = tmp("rows", [P, 2, D]), tmp("rows_t", [D, 2, P])
                block = ph.enter_context(nc.Block())

                @block.vector
                def _(dve):
                    def stage(n, b):
                        need(dve, moved, n - 1)
                        if normed:
                            nc.vector.tensor_scalar(rows[:, b, :], tile_of(nodes, n), dinv[:, bass.ds(n, 1)], None, ALU.mult).then_inc(staged, 1)
                        else:
                            nc.vector.tensor_copy(rows[:, b, :], tile_of(nodes, n)).then_inc(staged, 1)

                    def turn(i):
                        for b in range(2):
                            n = i * 2 + b
                            if in_range(n + 2):
                                stage(n + 2, b)
                            dve.wait_ge(made, n + 1)
                            nc.vector.tensor_scalar(tile_of(nodes, n), bank[2 + b][:, 0:D], dinv[:, bass.ds(n, 1)], None, ALU.mult).then_inc(scaled, 1)

                    for b in range(2):
                        stage(b, b)
                    by_two(dve, turn)

                @block.tensor
                def _(pe):
                    def transpose(n, b):
                        pe.wait_ge(staged, n + 1)
                        need(pe, kept, n - 1)
                        nc.tensor.transpose(bank[b][:, 0:P], rows[:, b, :], ident[:, :]).then_inc(moved, 1)

                    def turn(i):
                        for b in range(2):
                            n = i * 2 + b
                            if in_range(n + 1):
                                transpose(n + 1, 1 - b)
                            pe.wait_ge(kept, n + 1)
                            need(pe, scaled, n - 1)
                            nc.tensor.matmul(bank[2 + b][:, 0:D], rows_t[:, b, :], w_sb[:, :], start=True, stop=False)
                            nc.tensor.matmul(bank[2 + b][:, 0:D], ones_bf[:, :], b_parts, start=False, stop=True).then_inc(made, 1)

                    transpose(0, 0)
                    by_two(pe, turn)

                @block.scalar
                def _(act):
                    def turn(i):
                        for b in range(2):
                            n = i * 2 + b
                            act.wait_ge(moved, n + 1)
                            need(act, made, n - 1)
                            if normed:
                                act.activation(rows_t[:, b, :], bank[b][:, 0:P], ACT.Relu, bias=bn_shift[:, 0:1],
                                               scale=bn_scale[:, 0:1]).then_inc(kept, 1)
                            else:
                                act.copy(rows_t[:, b, :], bank[b][:, 0:P]).then_inc(kept, 1)

                    by_two(act, turn)

                @block.sync
                def _(sp):
                    by_chunk = table.rearrange("(n p) d -> p n d", p=P)
                    with sp.Fori(0, N_CHUNKS) as j:
                        sp.wait_ge(scaled, j * CHUNK + CHUNK)
                        sp.dma_start(by_chunk[:, bass.ds(j * CHUNK, CHUNK), :], nodes[:, bass.ds(j * CHUNK, CHUNK), :]).then_inc(stored, 16)
                    sp.wait_ge(stored, 16 * N_CHUNKS)

        def sparse_product(name, table, nth, beside):
            with ExitStack() as ph:
                own = ph.enter_context(phase_semaphores(nc))
                sem = lambda n: own(f"{name}_{n}")
                tmp = lambda n, s, d=F32: ph.enter_context(nc.sbuf_tensor(f"{name}_{n}", s, d))
                work = beside(lambda n: own(f"{name}_beside_{n}"),
                              lambda n, s, d=F32: ph.enter_context(nc.sbuf_tensor(f"{name}_beside_{n}", s, d)))
                local_ready, index_ready, row_go = sem("local_ready"), sem("index_ready"), sem("row_go")
                row_hot_ready, summed, added = sem("row_hot_ready"), sem("summed"), sem("added")
                HOTS = 4
                sum_bank = [bank[6], bank[7]]
                index_ring = tmp("index_ring", [P, TURN], I32)
                fetched_rows = tmp("fetched_rows", [P, TURN, D])
                hot = tmp("hot", [P, HOTS, P])
                block = ph.enter_context(nc.Block())

                @block.scalar
                def _(act):
                    act.copy(lo_slots[:, 0:S_TILES], d_slot[:, :, 1:2].rearrange("p t a -> p (t a)")).then_inc(local_ready, 1)

                    def indices(i, h):
                        need(act, summed, i * TURN + (h - 1) * HALF)
                        act.copy(index_ring[:, h * HALF:(h + 1) * HALF],
                                 d_slot[:, bass.ds(i * TURN + h * HALF, HALF), 0:1].bitcast(I32).rearrange("p t a -> p (t a)")).then_inc(index_ready, 1)

                    def turn(i):
                        for k in range(TURN):
                            work.scalar_step(act, i, k)
                            if k == 1:
                                indices(i, 1)
                            if k == HALF + 1:
                                indices(i + 1, 0)

                    indices(0, 0)
                    turn(0)
                    with act.Fori(1, E_TURNS) as i:
                        turn(i)
                    with act.Fori(E_TURNS, S_TURNS - 1) as i:
                        indices(i, 1)
                        indices(i + 1, 0)
                    indices(S_TURNS - 1, 1)

                @block.gpsimd
                def _(pool):
                    nc.gpsimd.memset(lo_slots[:, S_TILES:], EMPTY_KEY).then_inc(local_ready, 1)

                    def fetch(i, h):
                        pool.wait_ge(index_ready, 2 * i + h + 1)
                        pool.sem_inc(row_go, 1)
                        for k in range(h * HALF, (h + 1) * HALF):
                            nc.gpsimd.indirect_dma_start(
                                fetched_rows[:, k, :], None, table,
                                bass.IndirectOffsetOnAxis(ap=index_ring[:, k:k + 1], axis=0)).then_inc(fetched[k], 16)

                    fetch(0, 0)
                    with pool.Fori(0, E_TURNS) as i:
                        fetch(i, 1)
                        if work.scatters:
                            work.scatter(pool, i, 0)
                        fetch(i + 1, 0)
                        if work.scatters:
                            work.scatter(pool, i, 1)
                    with pool.Fori(E_TURNS, S_TURNS - 1) as i:
                        fetch(i, 1)
                        fetch(i + 1, 0)
                    fetch(S_TURNS - 1, 1)
                    if work.scatters:
                        work.scatter_end(pool)

                @block.vector
                def _(dve):
                    dve.wait_ge(local_ready, 2)

                    def one_hot(t, k):
                        need(dve, summed, t + 1 - HOTS)
                        nc.vector.tensor_scalar(hot[:, k % HOTS, :], iota_bf[:, :], lo_slots[:, bass.ds(t, 1)], None,
                                                ALU.is_equal).then_inc(row_hot_ready, 1)

                    def turn(i, edges=True):
                        for h in range(2):
                            _, node = nc.values_load_multi_w_load_instructions(
                                node_d[0:1, bass.ds(i * TURN + h * HALF, HALF)], engines=[mybir.EngineType.DVE],
                                min_val=0, max_val=NT - 1, skip_runtime_bounds_check_because=CLAMPED)
                            for k in range(h * HALF, (h + 1) * HALF):
                                t = i * TURN + k
                                if edges:
                                    work.vector_step(dve, i, k)
                                one_hot(t + 2, k + 2)
                                if edges:
                                    work.vector_end_step(dve, i, k)
                                dve.wait_ge(summed, t + 1)
                                need(dve, added, t)
                                here = tile_of(nodes, node[k % HALF])
                                nc.vector.tensor_tensor(here, here, sum_bank[k % 2][:, 0:D], ALU.add).then_inc(added, 1)

                    work.vector_start(dve)
                    for t in range(2):
                        one_hot(t, t)
                    turn(0)
                    with dve.Fori(1, E_TURNS) as i:
                        turn(i)
                    with dve.Fori(E_TURNS, S_TURNS) as i:
                        turn(i, edges=False)

                @block.tensor
                def _(pe):
                    def turn(i, edges=True):
                        for k in range(TURN):
                            t = i * TURN + k
                            if edges:
                                work.tensor_step(pe, i, k)
                            pe.wait_ge(row_hot_ready, t + 1)
                            need(pe, added, t - 1)
                            pe.wait_ge(fetched[k], (nth * S_TURNS + i + 1) * 16)
                            nc.tensor.matmul(sum_bank[k % 2][:, 0:D], hot[:, k % HOTS, :], fetched_rows[:, k, :],
                                             start=True, stop=True).then_inc(summed, 1)
                            if edges:
                                work.tensor_end_step(pe, i, k)

                    work.tensor_start(pe)
                    turn(0)
                    with pe.Fori(1, E_TURNS) as i:
                        turn(i)
                    work.tensor_end(pe)
                    with pe.Fori(E_TURNS, S_TURNS) as i:
                        turn(i, edges=False)

                @block.sync
                def _(sp):
                    work.sync(sp)

        count_destinations()
        find_bases("base_d", base_d, node_d, 0, True)
        window_slots()
        sort_destinations()
        linear("lin1", w1_sb, b1_parts, h_table[0], False)
        sparse_product("spmm1", h_table[0], 0, lambda sem, tmp: Count(sem, tmp, s_hi, s_lo, lead=2))
        find_bases("base_s", base_s, node_s, S_ROW, False)
        linear("lin2", w2_sb, b2_parts, h_table[1], True)
        sparse_product("spmm2", h_table[1], 1, lambda sem, tmp: Sort(
            sem, tmp, s_hi, s_lo, s_hi_bf, s_lo, base_s, dst_i, s_slots, S_FIELDS, True))

        class Norm:

            def __init__(self, name, sem, tmp, rows):
                self.rows = rows
                self.res_in = [sem(f"res_in{b}") for b in range(2)]
                self.summed, self.centred, self.squared, self.var_ready, self.rooted, self.normed, self.step = (
                    sem(n) for n in ("res_summed", "centred", "squared", "var_ready", "rooted", "normed", "norm_step"))
                self.res, self.sq = tmp("res", [P, 2, CHUNK, D]), tmp("sq", [P, 2, CHUNK, D])
                self.mean, self.rstd = tmp("mean", [P, 2, CHUNK]), tmp("rstd", [P, 2, CHUNK])

            def chunk(self, j):
                return self.rows[:, bass.ds(j * CHUNK, CHUNK), :]

            def load(self, sp, j, b, source):
                need(sp, self.centred, j - 1)
                sp.dma_start(self.res[:, b, :, :], source[:, bass.ds(j * CHUNK, CHUNK), :]).then_inc(self.res_in[b], 16)

            def vector(self, dve, rows_ready):
                v = nc.vector
                link = Chain(dve, self.step)
                over = lambda a: a.unsqueeze(2).to_broadcast([P, CHUNK, D])

                def centre(j, b, loads):
                    here = self.chunk(j)
                    rows_ready(j)
                    dve.wait_ge(self.res_in[b], loads * 16)
                    v.tensor_tensor(self.res[:, b, :, :], here, self.res[:, b, :, :], ALU.add).then_inc(self.summed, 1)
                    dve.wait_ge(self.summed, j + 1)
                    link(v.tensor_reduce(self.mean[:, b, :], self.res[:, b, :, :], AX.X, ALU.add))
                    link(v.tensor_scalar(self.mean[:, b, :], self.mean[:, b, :], 1.0 / D, None, ALU.mult))
                    v.tensor_tensor(here, self.res[:, b, :, :], over(self.mean[:, b, :]), ALU.subtract).then_inc(self.centred, 1)

                def scale(j, b):
                    here = self.chunk(j)
                    dve.wait_ge(self.squared, j + 1)
                    v.tensor_reduce(self.rstd[:, b, :], self.sq[:, b, :, :], AX.X, ALU.add).then_inc(self.var_ready, 1)
                    dve.wait_ge(self.rooted, j + 1)
                    link(v.reciprocal(self.rstd[:, b, :], self.rstd[:, b, :]))
                    v.tensor_tensor(here, here, over(self.rstd[:, b, :]), ALU.mult).then_inc(self.normed, 1)

                PER_TURN = 2 * 3
                turns = N_CHUNKS // 2

                def turn(i):
                    link.turn(2 + i * PER_TURN)
                    centre(i * 2 + 1, 1, i + 1)
                    scale(i * 2, 0)
                    if not isinstance(i, int) or i < turns - 1:
                        centre(i * 2 + 2, 0, i + 2)
                    scale(i * 2 + 1, 1)

                centre(0, 0, 1)
                turn(0)
                with dve.Fori(1, turns - 1) as i:
                    turn(i)
                turn(turns - 1)

            def scalar(self, act):
                with act.Fori(0, N_CHUNKS // 2) as i:
                    for b in range(2):
                        j = i * 2 + b
                        act.wait_ge(self.centred, j + 1)
                        act.activation(self.sq[:, b, :, :], self.chunk(j), ACT.Square).then_inc(self.squared, 1)
                        act.wait_ge(self.var_ready, j + 1)
                        act.activation(self.rstd[:, b, :], self.rstd[:, b, :], ACT.Sqrt, bias=eps_col[:, 0:1], scale=1.0 / D).then_inc(self.rooted, 1)

        with ExitStack() as ph:
            own = ph.enter_context(phase_semaphores(nc))
            sem = lambda n: own(f"qkv_{n}")
            tmp = lambda n, s, d=F32: ph.enter_context(nc.sbuf_tensor(f"qkv_{n}", s, d))
            norm = Norm("qkv", sem, tmp, nodes)
            x1_out, tail_in = sem("x1_out"), sem("tail_in")
            kv_out = [sem(f"kv_out{b}") for b in range(2)]
            weighed, staged, moved, kept, made, q_done, kv_done = (
                sem(n) for n in ("weighed", "staged", "moved", "kept", "made", "q_done", "kv_done"))
            rows, rows_t, kv_rows = tmp("rows", [P, 2, D]), tmp("rows_t", [D, 2, P]), tmp("kv_rows", [P, 2, 2 * D])
            block = ph.enter_context(nc.Block())

            @block.sync
            def _(sp):
                x_tiles = x[0:(NT - 1) * P, :].rearrange("(n p) d -> p n d", p=P)
                for b in range(2):
                    norm.load(sp, b, b, x_tiles)
                with sp.Fori(1, N_CHUNKS // 2 - 1) as i:
                    for b in range(2):
                        norm.load(sp, i * 2 + b, b, x_tiles)
                norm.load(sp, N_CHUNKS - 2, 0, x_tiles)
                last = (N_CHUNKS - 1) * CHUNK
                sp.wait_ge(norm.centred, N_CHUNKS - 2)
                sp.dma_start(norm.res[:, 1, 0:CHUNK - 1, :], x_tiles[:, last:NT - 1, :]).then_inc(norm.res_in[1], 16)
                sp.dma_start(norm.res[0:LAST_ROWS, 1, CHUNK - 1, :], x[(NT - 1) * P:N_NODES, :]).then_inc(tail_in, 16)
                with sp.Fori(0, NT // 2) as i:
                    for b in range(2):
                        n = i * 2 + b
                        sp.wait_ge(kv_done, n + 1)
                        sp.dma_start(kv_table[bass.ds(n * P, P), :], kv_rows[:, b, :]).then_inc(kv_out[b], 16)
                for b in range(2):
                    sp.wait_ge(kv_out[b], 16 * (NT // 2))

            @block.gpsimd
            def _(pool):
                with pool.Fori(0, N_CHUNKS) as j:
                    nc.gpsimd.tensor_tensor(norm.chunk(j), norm.chunk(j),
                                            dinv[:, bass.ds(j * CHUNK, CHUNK)].unsqueeze(2).to_broadcast([P, CHUNK, D]), ALU.mult).then_inc(weighed, 1)

                def turn(i):
                    for b in range(2):
                        n = i * 2 + b
                        need(pool, moved, n - 1)
                        nc.gpsimd.tensor_copy(rows[:, b, :], tile_of(nodes, n)).then_inc(staged, 1)

                with pool.Fori(0, N_CHUNKS) as j:
                    pool.wait_ge(norm.normed, j + 1)
                    pool.dma_start(x1_dram.rearrange("(n p) d -> p n d", p=P)[:, bass.ds(j * CHUNK, CHUNK), :], norm.chunk(j)).then_inc(x1_out, 16)
                by_two(pool, turn)

            @block.vector
            def _(dve):
                v = nc.vector

                def rows_ready(j):
                    dve.wait_ge(weighed, j + 1)
                    if isinstance(j, int) and j == N_CHUNKS - 1:
                        dve.wait_ge(tail_in, 16)

                norm.vector(dve, rows_ready)

                def turn(i):
                    for b in range(2):
                        n = i * 2 + b
                        dve.wait_ge(made, n + 1)
                        v.scalar_tensor_tensor(tile_of(nodes, n), bank[2 + b][:, 0:D], HEAD_DIM ** -0.5, qkv_bc[:, 0:D], ALU.mult, ALU.add).then_inc(q_done, 1)
                        need(dve, kv_out[b], i * 16)
                        v.tensor_tensor(kv_rows[:, b, :], bank[2 + b][:, D:3 * D], qkv_bc[:, D:3 * D], ALU.add).then_inc(kv_done, 1)

                dve.wait_ge(x1_out, 16 * N_CHUNKS)
                by_two(dve, turn)

            @block.scalar
            def _(act):
                norm.scalar(act)

                def turn(i):
                    for b in range(2):
                        n = i * 2 + b
                        act.wait_ge(moved, n + 1)
                        need(act, made, n - 1)
                        act.copy(rows_t[:, b, :], bank[b][:, 0:P]).then_inc(kept, 1)

                by_two(act, turn)

            @block.tensor
            def _(pe):
                def transpose(n, b):
                    pe.wait_ge(staged, n + 1)
                    need(pe, kept, n - 1)
                    nc.tensor.transpose(bank[b][:, 0:P], rows[:, b, :], ident[:, :]).then_inc(moved, 1)

                def turn(i):
                    for b in range(2):
                        n = i * 2 + b
                        if in_range(n + 1):
                            transpose(n + 1, 1 - b)
                        pe.wait_ge(kept, n + 1)
                        need(pe, kv_done, n - 1)
                        nc.tensor.matmul(bank[2 + b][:, 0:3 * D], rows_t[:, b, :], qkv_t[:, :], start=True, stop=True).then_inc(made, 1)

                transpose(0, 0)
                by_two(pe, turn)

        GROUP = 4
        GROUPS = TURN // GROUP
        with ExitStack() as ph:
            own = ph.enter_context(phase_semaphores(nc))
            sem = lambda n: own(f"score_{n}")
            tmp = lambda n, s, d=F32: ph.enter_context(nc.sbuf_tensor(f"score_{n}", s, d))
            slots_in, local_ready, index_ready, go = sem("slots_in"), sem("local_ready"), sem("index_ready"), sem("go")
            spread, hot_ready, q_ready, product, reduced, scored = (
                sem(n) for n in ("spread", "hot_ready", "q_ready", "product", "reduced", "scored"))
            v_out = [sem(f"v_out{h}") for h in range(2)]
            index_ring = tmp("index_ring", [P, TURN], I32)
            kv_rows = tmp("kv_rows", [P, TURN, 2 * D])
            hot_t = tmp("hot_t", [P, 2, GROUP * P])
            qk = tmp("qk", [P, GROUP * D])
            part_scores = tmp("part_scores", [P, GROUP, HEADS])
            block = ph.enter_context(nc.Block())

            @block.sync
            def _(sp):
                sp.dma_start(s_slot, s_slots.rearrange("(p t) f -> p t f", p=P)).then_inc(slots_in, 16)
                sp.wait_ge(slots_in, 16)
                with sp.Fori(0, S_TURNS) as i:
                    for h in range(2):
                        for k in range(h * HALF, (h + 1) * HALF):
                            sp.wait_ge(fetched[k], (2 * S_TURNS + i + 1) * 16)
                        sp.dma_start(v_sorted[:, bass.ds(i * TURN + h * HALF, HALF), :],
                                     kv_rows[:, h * HALF:(h + 1) * HALF, D:2 * D]).then_inc(v_out[h], 16)
                for h in range(2):
                    sp.wait_ge(v_out[h], 16 * S_TURNS)

            @block.scalar
            def _(act):
                act.wait_ge(slots_in, 16)
                lo = s_slot[:, :, 1:2].rearrange("p t a -> p (t a)")
                act.copy(lo_slots[:, 0:S_TILES], lo).then_inc(local_ready, 1)
                act.copy(lo_slots_bf[:, 0:S_TILES], lo).then_inc(local_ready, 1)

                def turn(i):
                    for h in range(2):
                        need(act, product, (i - 1) * GROUPS + (h + 1) * (GROUPS // 2))
                        need(act, v_out[h], i * 16)
                        act.copy(index_ring[:, h * HALF:(h + 1) * HALF],
                                 s_slot[:, bass.ds(i * TURN + h * HALF, HALF), 0:1].bitcast(I32).rearrange("p t a -> p (t a)")).then_inc(index_ready, 1)

                turn(0)
                with act.Fori(1, S_TURNS) as i:
                    turn(i)

            @block.gpsimd
            def _(pool):
                nc.gpsimd.memset(lo_slots_bf[:, S_TILES:], EMPTY_KEY).then_inc(local_ready, 1)
                with pool.Fori(0, S_TURNS) as i:
                    for h in range(2):
                        pool.wait_ge(index_ready, 2 * i + h + 1)
                        pool.sem_inc(go, 1)
                        for k in range(h * HALF, (h + 1) * HALF):
                            nc.gpsimd.indirect_dma_start(
                                kv_rows[:, k, :], None, kv_table,
                                bass.IndirectOffsetOnAxis(ap=index_ring[:, k:k + 1], axis=0)).then_inc(fetched[k], 16)

            @block.tensor
            def _(pe):
                pe.wait_ge(local_ready, 3)

                def spread_keys(g, b, t0):
                    need(pe, hot_ready, g - 1)
                    for m in range(GROUP):
                        last = nc.tensor.matmul(bank[b][:, m * P:(m + 1) * P], lo_slots_bf[:, bass.ds(t0 + m, 1)].to_broadcast([P, P]),
                                                ident_bf[:, :], start=True, stop=True)
                    last.then_inc(spread, 1)

                def turn(i):
                    for j in range(GROUPS):
                        g = i * GROUPS + j
                        spread_keys(g + 1, (j + 1) % 2, i * TURN + (j + 1) * GROUP)
                        _, node = nc.values_load_multi_w_load_instructions(
                            node_s[0:1, bass.ds(i * TURN + j * GROUP, GROUP)], engines=[mybir.EngineType.PE],
                            min_val=0, max_val=NT - 1, skip_runtime_bounds_check_because=CLAMPED)
                        pe.wait_ge(hot_ready, g + 1)
                        need(pe, product, g - 1)
                        for m in range(GROUP):
                            last = nc.tensor.matmul(bank[2 + j % 2][:, m * D:(m + 1) * D], hot_t[:, j % 2, m * P:(m + 1) * P],
                                                    nodes[:, bass.ds(node[m], 1), :].rearrange("p a d -> p (a d)"), start=True, stop=True)
                        last.then_inc(q_ready, 1)

                spread_keys(0, 0, 0)
                turn(0)
                with pe.Fori(1, S_TURNS) as i:
                    turn(i)

            @block.vector
            def _(dve):
                v = nc.vector

                def one_hots(g, b):
                    dve.wait_ge(spread, g + 1)
                    need(dve, q_ready, g - 1)
                    v.tensor_scalar(hot_t[:, b, :], bank[b][:, :], iota_p[:, 0:1], None, ALU.is_equal).then_inc(hot_ready, 1)

                def turn(i):
                    for j in range(GROUPS):
                        g = i * GROUPS + j
                        one_hots(g + 1, (j + 1) % 2)
                        for k in range(j * GROUP, (j + 1) * GROUP):
                            dve.wait_ge(fetched[k], (2 * S_TURNS + i + 1) * 16)
                        dve.wait_ge(q_ready, g + 1)
                        need(dve, reduced, g)
                        v.tensor_tensor(qk[:, :].rearrange("p (m d) -> p m d", d=D), bank[2 + j % 2][:, :].rearrange("p (m d) -> p m d", d=D),
                                        kv_rows[:, j * GROUP:(j + 1) * GROUP, 0:D], ALU.mult).then_inc(product, 1)
                        dve.wait_ge(product, g + 1)
                        need(dve, scored, g)
                        v.tensor_reduce(part_scores[:, :, :].rearrange("p m h -> p (m h)"),
                                        qk[:, :].rearrange("p (m d) -> p m d", d=HEAD_DIM), AX.X, ALU.add).then_inc(reduced, 1)
                        dve.wait_ge(reduced, g + 1)
                        biased = s_slot[:, bass.ds(i * TURN + j * GROUP, GROUP), 2:S_FIELDS]
                        v.tensor_tensor(biased, biased, part_scores[:, :, :], ALU.add).then_inc(scored, 1)

                dve.wait_ge(slots_in, 16)
                one_hots(0, 0)
                turn(0)
                with dve.Fori(1, S_TURNS) as i:
                    turn(i)

        with ExitStack() as ph:
            own = ph.enter_context(phase_semaphores(nc))
            sem = lambda n: own(f"soft_{n}")
            tmp = lambda n, s, d=F32: ph.enter_context(nc.sbuf_tensor(f"soft_{n}", s, d))
            step, key_ready, prev_ready = sem("step"), sem("key_ready"), sem("prev_ready")
            staged, moved, kept_s, kept_b = sem("staged"), sem("moved"), sem("kept_s"), sem("kept_b")
            b_staged, ends_ready, rows_ready, carry_ready, carried = (
                sem(n) for n in ("b_staged", "ends_ready", "rows_ready", "carry_ready", "carried"))
            shifted, exped, w_moved, w_kept = sem("shifted"), sem("exped"), sem("w_moved"), sem("w_kept")
            QUARTER = S_TILES // 4
            key = tmp("key", [P, S_TILES + 1])
            new_seg = tmp("new_seg", [P, S_TILES])
            TRIO = 3
            TRIOS = CHUNK_TILES // TRIO
            T3 = TRIO * P
            assert TRIOS * TRIO == CHUNK_TILES and TRIOS % 2 == 1
            s_stage, b_stage = tmp("s_stage", [P, 2, T3]), tmp("b_stage", [P, 2, T3])
            as_tch = lambda rows: rows.rearrange("p (t c h) -> p t c h", t=TRIO, h=HEADS)

            def by_trios(eng, body):
                def turn(i):
                    for b in range(2):
                        body(i * 2 + b, b)

                turn(0)
                with eng.Fori(1, TRIOS // 2) as i:
                    turn(i)
                body(TRIOS - 1, 0)

            ends = tmp("ends", [P, 6])
            carry_row = tmp("carry_row", [1, 6, P])
            carry_out = tmp("carry_out", [1, 2, P + HEADS])
            carry = tmp("carry", [P, 2])
            chunk_key = new_seg[:, :].rearrange("p (c t) -> p c t", c=CHUNKS)
            chunk_scores = s_slot.rearrange("p (c t) f -> p c t f", c=CHUNKS)
            QUARTERS = 4
            PIECE = CHUNK_LEN // QUARTERS
            block = ph.enter_context(nc.Block())

            @block.vector
            def _(dve):
                v = nc.vector
                link = Chain(dve, step)
                link(v.memset(key[:, 0:1], -float(P)))
                v.scalar_tensor_tensor(key[:, 1:], node_s_bc[:, :], float(P), lo_slots[:, 0:S_TILES], ALU.mult, ALU.add).then_inc(key_ready, 1)
                dve.wait_ge(key_ready, 1)
                dve.wait_ge(prev_ready, 1)
                for j in range(4):
                    cut = slice(j * QUARTER, (j + 1) * QUARTER)
                    link(v.tensor_tensor(new_seg[:, cut], bank[4 + j][:, 0:QUARTER], key[:, 1 + j * QUARTER:1 + (j + 1) * QUARTER], ALU.not_equal))
                link(v.tensor_scalar(new_seg[:, :], new_seg[:, :], BREAK, None, ALU.mult))

                def stage(g, b):
                    need(dve, moved, g - 1)
                    v.tensor_copy(as_tch(b_stage[:, b, :]), chunk_key[:, :, bass.ds(g * TRIO, TRIO)].rearrange("p c t -> p t c").unsqueeze(3)
                                  .to_broadcast([P, TRIO, CHUNKS, HEADS])).then_inc(b_staged, 1)

                def keep(g, b):
                    if not (isinstance(g, int) and g == TRIOS - 1):
                        stage(g + 1, 1 - b)
                    dve.wait_ge(moved, g + 1)
                    v.tensor_copy(breaks[:, bass.ds(g * T3, T3)], bank[2 + b][:, 0:T3]).then_inc(kept_b, 1)

                stage(0, 0)
                by_trios(dve, keep)
                dve.wait_ge(kept_b, TRIOS)
                dve.wait_ge(kept_s, TRIOS)
                link(v.memset(breaks[:, CHUNK_LEN:], 0.0))
                body, back = breaks[:, 0:CHUNK_LEN], breaks[:, 1:CHUNK_LEN + 1]
                link(v.tensor_reduce(ends[:, 0:1], body, AX.X, ALU.add))
                link(v.tensor_copy(ends[:, 2:3], breaks[:, 0:1]))
                link(v.tensor_tensor(ends[:, 1:2], ends[:, 0:1], ends[:, 2:3], ALU.subtract))
                link(v.tensor_tensor_scan(seg_max, body, scores_t, BREAK, ALU.add, ALU.max))
                link(v.tensor_copy(ends[:, 3:4], seg_max[:, CHUNK_LEN - 1:CHUNK_LEN]))
                link(v.tensor_tensor_scan(seg_max[:, ::-1], back[:, ::-1], scores_t[:, ::-1], BREAK, ALU.add, ALU.max))
                v.tensor_copy(ends[:, 4:5], seg_max[:, 0:1]).then_inc(ends_ready, 1)
                dve.wait_ge(rows_ready, 1)
                dve.wait_ge(ends_ready, 1)
                link(v.tensor_copy(carry_row[:, 0:4, :].rearrange("p a b -> p (a b)"), bank[0][0:1, 0:4 * P]))
                link(v.tensor_copy(carry_row[:, 4, :], bank[1][0:1, 0:P]))
                link(v.memset(carry_out[:, :, :], BREAK))
                by_head = carry_row[:, :, :].rearrange("p a (c h) -> p a h c", h=HEADS)
                into = carry_out[:, :, :].rearrange("p a (c h) -> p a h c", h=HEADS)
                link(v.tensor_tensor(carry_row[:, 1, :], carry_row[:, 1, :], carry_row[:, 2, :], ALU.add))
                link(v.tensor_tensor(carry_row[:, 4, :], carry_row[:, 4, :], carry_row[:, 2, :], ALU.add))
                for h in range(HEADS):
                    v.tensor_tensor_scan(into[:, 0, h, 1:], by_head[:, 0, h, :], by_head[:, 3, h, :], BREAK, ALU.add, ALU.max)
                    link(v.tensor_tensor_scan(into[:, 1, h, 0:CHUNKS][:, ::-1], by_head[:, 1, h, ::-1], by_head[:, 4, h, ::-1],
                                              BREAK, ALU.add, ALU.max))
                v.tensor_copy(carry_row[:, 5, :], carry_row[:, 4, :]).then_inc(carry_ready, 1)
                dve.wait_ge(carried, 1)
                link(v.tensor_copy(carry[:, :], bank[2][:, 0:2]))
                link(v.tensor_tensor_scan(seg_max, body, scores_t, carry[:, 0:1], ALU.add, ALU.max))
                link(v.tensor_tensor_scan(seg_max[:, ::-1], back[:, ::-1], seg_max[:, ::-1], carry[:, 1:2], ALU.add, ALU.max))
                for j in range(QUARTERS):
                    cut = slice(j * PIECE, (j + 1) * PIECE)
                    v.tensor_tensor(scores_t[:, cut], scores_t[:, cut], seg_max[:, cut], ALU.subtract).then_inc(shifted, 1)

                dve.wait_ge(shifted, QUARTERS)

                def keep_weights(g, b):
                    dve.wait_ge(w_moved, g + 1)
                    v.tensor_copy(weights.rearrange("p (c t) h -> p t c h", c=CHUNKS)[:, bass.ds(g * TRIO, TRIO), :, :],
                                  as_tch(bank[4 + b][:, 0:T3])).then_inc(w_kept, 1)

                by_trios(dve, keep_weights)

            @block.tensor
            def _(pe):
                t = nc.tensor
                pe.wait_ge(key_ready, 1)
                for j in range(4):
                    t.matmul(bank[4 + j][:, 0:QUARTER], next_row[:, :], key[:, 1 + j * QUARTER:1 + (j + 1) * QUARTER], start=True, stop=False)
                    last = t.matmul(bank[4 + j][:, 0:QUARTER], wrap_row[:, :], key[:, j * QUARTER:(j + 1) * QUARTER], start=False, stop=True)
                last.then_inc(prev_ready, 1)

                def move(g, b):
                    need(pe, kept_s, g - 1)
                    pe.wait_ge(staged, g + 1)
                    for m in range(TRIO):
                        t.transpose(bank[b][:, m * P:(m + 1) * P], s_stage[:, b, m * P:(m + 1) * P], ident[:, :])
                    need(pe, kept_b, g - 1)
                    pe.wait_ge(b_staged, g + 1)
                    for m in range(TRIO):
                        last = t.transpose(bank[2 + b][:, m * P:(m + 1) * P], b_stage[:, b, m * P:(m + 1) * P], ident[:, :])
                    last.then_inc(moved, 1)

                by_trios(pe, move)
                pe.wait_ge(ends_ready, 1)
                for n in range(5):
                    last = t.matmul(bank[n // 4][0:1, (n % 4) * P:(n % 4 + 1) * P], ends[:, n:n + 1], ident[:, :], start=True, stop=True)
                last.then_inc(rows_ready, 1)
                pe.wait_ge(carry_ready, 1)
                t.matmul(bank[2][:, 0:1], carry_out[0:1, 0, 0:P], ones[0:1, 0:1], start=True, stop=True)
                t.matmul(bank[2][:, 1:2], carry_out[0:1, 1, HEADS:P + HEADS], ones[0:1, 0:1], start=True, stop=True).then_inc(carried, 1)

                def move_back(g, b):
                    pe.wait_ge(exped, g + 1)
                    need(pe, w_kept, g - 1)
                    for m in range(TRIO):
                        last = t.transpose(bank[4 + b][:, m * P:(m + 1) * P], s_stage[:, b, m * P:(m + 1) * P], ident[:, :])
                    last.then_inc(w_moved, 1)

                by_trios(pe, move_back)

            @block.scalar
            def _(act):
                def stage(g, b):
                    need(act, moved, g - 1)
                    act.copy(as_tch(s_stage[:, b, :]),
                             chunk_scores[:, :, bass.ds(g * TRIO, TRIO), 2:S_FIELDS].rearrange("p c t h -> p t c h")).then_inc(staged, 1)

                def keep(g, b):
                    if not (isinstance(g, int) and g == TRIOS - 1):
                        stage(g + 1, 1 - b)
                    act.wait_ge(moved, g + 1)
                    act.copy(scores_t[:, bass.ds(g * T3, T3)], bank[b][:, 0:T3]).then_inc(kept_s, 1)

                stage(0, 0)
                by_trios(act, keep)
                act.wait_ge(shifted, QUARTERS)

                def exps(g, b):
                    need(act, w_moved, g - 1)
                    act.activation(s_stage[:, b, :], scores_t[:, bass.ds(g * T3, T3)], ACT.Exp).then_inc(exped, 1)

                by_trios(act, exps)

        STREAM = S_TILES // 2
        with ExitStack() as ph:
            own = ph.enter_context(phase_semaphores(nc))
            sem = lambda n: own(f"mix_{n}")
            tmp = lambda n, s, d=F32: ph.enter_context(nc.sbuf_tensor(f"mix_{n}", s, d))
            cleared, hot_ready, weighted, joined, summed, added, step = (
                sem(n) for n in ("cleared", "hot_ready", "weighted", "joined", "summed", "added", "step"))
            v_in = [sem(f"v_in{j}") for j in range(GROUPS)]
            RING = 8
            W = D + HEADS
            v_rows = tmp("v_rows", [P, GROUPS, GROUP, D])
            mixed = tmp("mixed", [P, GROUPS, GROUP, W])
            hot = tmp("hot", [P, GROUPS, GROUP, P])
            ends = tmp("ends", [P, 2])
            block = ph.enter_context(nc.Block())

            def tiles_of(i, j):
                return bass.ds(i * HALF + j // 2 * GROUP + j % 2 * STREAM, GROUP)

            def half_summed(i, j):
                return (i - 1) * TURN + (j // 2 + 1) * HALF

            @block.sync
            def _(sp):
                def turn(i):
                    for j in range(GROUPS):
                        need(sp, weighted, (i - 1) * GROUPS + j + 1)
                        sp.dma_start(v_rows[:, j, :, :], v_sorted[:, tiles_of(i, j), :]).then_inc(v_in[j], 16)

                turn(0)
                with sp.Fori(1, S_TURNS) as i:
                    turn(i)

            @block.gpsimd
            def _(pool):
                def turn(i):
                    for j in range(GROUPS):
                        pool.wait_ge(v_in[j], i * 16 + 16)
                        need(pool, summed, half_summed(i, j))
                        nc.gpsimd.tensor_tensor(
                            mixed[:, j, :, 0:D].rearrange("p m (h d) -> p m h d", d=HEAD_DIM),
                            v_rows[:, j, :, :].rearrange("p m (h d) -> p m h d", d=HEAD_DIM),
                            weights[:, tiles_of(i, j), :].unsqueeze(3).to_broadcast([P, GROUP, HEADS, HEAD_DIM]), ALU.mult).then_inc(weighted, 1)

                turn(0)
                with pool.Fori(1, S_TURNS) as i:
                    turn(i)

            @block.scalar
            def _(act):
                def turn(i):
                    for j in range(GROUPS):
                        need(act, summed, half_summed(i, j))
                        act.copy(mixed[:, j, :, D:W], weights[:, tiles_of(i, j), :]).then_inc(joined, 1)

                turn(0)
                with act.Fori(1, S_TURNS) as i:
                    turn(i)

            @block.vector
            def _(dve):
                v = nc.vector
                link = Chain(dve, step)
                v.memset(sums, 0.0).then_inc(cleared, 1)
                dve.wait_ge(cleared, 1)

                def one_hots(i, j):
                    need(dve, summed, half_summed(i, j))
                    v.tensor_tensor(hot[:, j, :, :], iota_bf[:, :].unsqueeze(1).to_broadcast([P, GROUP, P]),
                                    lo_slots[:, tiles_of(i, j)].unsqueeze(2).to_broadcast([P, GROUP, P]), ALU.is_equal).then_inc(hot_ready, 1)

                def turn(i, last=False):
                    for h in range(2):
                        nodes_of = []
                        for stream in range(2):
                            _, node = nc.values_load_multi_w_load_instructions(
                                node_s[0:1, tiles_of(i, 2 * h + stream)], engines=[mybir.EngineType.DVE],
                                min_val=0, max_val=NT - 1, skip_runtime_bounds_check_because=CLAMPED)
                            nodes_of.append(node)
                        for k in range(HALF):
                            stream, done = k % 2, i * TURN + h * HALF + k
                            if k in (0, GROUP) and not (last and h == 1):
                                one_hots(i + h, 2 * (1 - h) + k // GROUP)
                            dve.wait_ge(summed, done + 1)
                            need(dve, added, done - 1)
                            here = tile_of(sums, nodes_of[stream][k // 2] + stream)
                            v.tensor_tensor(here, here, bank[k][:, 0:W], ALU.add).then_inc(added, 1)

                for j in range(2):
                    one_hots(0, j)
                turn(0)
                with dve.Fori(1, S_TURNS - 1) as i:
                    turn(i)
                turn(S_TURNS - 1, last=True)
                _, meet = nc.values_load_multi_w_load_instructions(
                    node_s[0:1, STREAM - 1:STREAM + 1], engines=[mybir.EngineType.DVE],
                    min_val=0, max_val=NT - 1, skip_runtime_bounds_check_because=CLAMPED)
                link(v.tensor_copy(ends[:, :], node_s_bc[:, STREAM - 1:STREAM + 1]))
                link(v.tensor_tensor(ends[:, 1:2], ends[:, 0:1], ends[:, 1:2], ALU.is_equal))
                dve.wait_ge(added, S_TILES)
                here = tile_of(sums, meet[0])
                link(v.scalar_tensor_tensor(here, tile_of(sums, meet[1] + 1), ends[:, 1:2], here, ALU.mult, ALU.add))
                link(v.tensor_scalar(sum_place[:, :], iota_bf[0:1, 0:NT], ends[0:1, 0:1], None, ALU.is_gt))
                link(v.tensor_tensor(sum_place[:, :], sum_place[:, :], iota_bf[0:1, 0:NT], ALU.add))

            @block.tensor
            def _(pe):
                def turn(i):
                    for k in range(TURN):
                        t, j, m = i * TURN + k, k // HALF * 2 + k % 2, k % HALF // 2
                        if m == 0:
                            pe.wait_ge(weighted, i * GROUPS + j + 1)
                            pe.wait_ge(joined, i * GROUPS + j + 1)
                            pe.wait_ge(hot_ready, i * GROUPS + j + 1)
                        need(pe, added, t + 1 - RING)
                        nc.tensor.matmul(bank[k % RING][:, 0:W], hot[:, j, m, :], mixed[:, j, m, :], start=True, stop=True).then_inc(summed, 1)

                turn(0)
                with pe.Fori(1, S_TURNS) as i:
                    turn(i)

        with ExitStack() as ph:
            own = ph.enter_context(phase_semaphores(nc))
            sem = lambda n: own(f"fin_{n}")
            tmp = lambda n, s, d=F32: ph.enter_context(nc.sbuf_tensor(f"fin_{n}", s, d))
            rec_step, staged, moved, kept, made, projected, stored = (
                sem(n) for n in ("rec_step", "staged", "moved", "kept", "made", "projected", "stored"))
            rec = tmp("rec", [P, NT + 1, HEADS])
            rows, rows_t = tmp("rows", [P, 2, D]), tmp("rows_t", [D, 2, P])
            final = sums[:, 0:NT, 0:D]
            norm = Norm("fin", sem, tmp, final)
            block = ph.enter_context(nc.Block())

            @block.sync
            def _(sp):
                x1_tiles = x1_dram.rearrange("(n p) d -> p n d", p=P)
                for b in range(2):
                    norm.load(sp, b, b, x1_tiles)
                with sp.Fori(1, N_CHUNKS // 2) as i:
                    for b in range(2):
                        norm.load(sp, i * 2 + b, b, x1_tiles)

            @block.scalar
            def _(act):
                def turn(i):
                    for b in range(2):
                        n = i * 2 + b
                        act.wait_ge(moved, n + 1)
                        need(act, made, n - 1)
                        act.copy(rows_t[:, b, :], bank[b][:, 0:P]).then_inc(kept, 1)

                by_two(act, turn)
                norm.scalar(act)

            @block.gpsimd
            def _(pool):
                def turn(i):
                    _, place = nc.values_load_multi_w_load_instructions(
                        sum_place[0:1, bass.ds(i * 2, 2)], engines=[mybir.EngineType.Pool],
                        min_val=0, max_val=NT, skip_runtime_bounds_check_because="a node tile's number, or one more")
                    for b in range(2):
                        n = i * 2 + b
                        need(pool, moved, n - 1)
                        nc.gpsimd.tensor_tensor(rows[:, b, :].rearrange("p (h d) -> p h d", d=HEAD_DIM),
                                                tile_of(sums, place[b])[:, 0:D].rearrange("p (h d) -> p h d", d=HEAD_DIM),
                                                tile_of(rec, place[b]).unsqueeze(2).to_broadcast([P, HEADS, HEAD_DIM]), ALU.mult).then_inc(staged, 1)

                pool.wait_ge(rec_step, 2)
                by_two(pool, turn)
                out_tiles = out[0:(NT - 1) * P, :].rearrange("(n p) d -> p n d", p=P)
                with pool.Fori(0, N_CHUNKS - 1) as j:
                    pool.wait_ge(norm.normed, j + 1)
                    pool.dma_start(out_tiles[:, bass.ds(j * CHUNK, CHUNK), :], norm.chunk(j)).then_inc(stored, 16)
                pool.wait_ge(norm.normed, N_CHUNKS)
                pool.dma_start(out_tiles[:, (N_CHUNKS - 1) * CHUNK:NT - 1, :], final[:, (N_CHUNKS - 1) * CHUNK:NT - 1, :]).then_inc(stored, 16)
                pool.dma_start(out[(NT - 1) * P:N_NODES, :], final[0:LAST_ROWS, NT - 1, :]).then_inc(stored, 16)
                pool.wait_ge(stored, 16 * (N_CHUNKS + 1))

            @block.vector
            def _(dve):
                v = nc.vector
                v.tensor_scalar(rec[:, :, :], sums[:, :, D:D + HEADS], SUM_EPS, None, ALU.add).then_inc(rec_step, 1)
                dve.wait_ge(rec_step, 1)
                v.reciprocal(rec[:, :, :], rec[:, :, :]).then_inc(rec_step, 1)

                def turn(i):
                    for b in range(2):
                        n = i * 2 + b
                        dve.wait_ge(made, n + 1)
                        v.tensor_copy(tile_of(final, n), bank[2 + b][:, 0:D]).then_inc(projected, 1)

                by_two(dve, turn)
                norm.vector(dve, lambda j: dve.wait_ge(projected, j * CHUNK + CHUNK))

            @block.tensor
            def _(pe):
                def transpose(n, b):
                    pe.wait_ge(staged, n + 1)
                    need(pe, kept, n - 1)
                    nc.tensor.transpose(bank[b][:, 0:P], rows[:, b, :], ident[:, :]).then_inc(moved, 1)

                def turn(i):
                    for b in range(2):
                        n = i * 2 + b
                        if in_range(n + 1):
                            transpose(n + 1, 1 - b)
                        pe.wait_ge(kept, n + 1)
                        need(pe, projected, n - 1)
                        nc.tensor.matmul(bank[2 + b][:, 0:D], rows_t[:, b, :], out_t[:, :], start=True, stop=False)
                        nc.tensor.matmul(bank[2 + b][:, 0:D], ones_bf[:, :], out_parts, start=False, stop=True).then_inc(made, 1)

                transpose(0, 0)
                by_two(pe, turn)


_INS = ["x", "src", "dst", "edge_attr_128",
        "L0_gnn_W1", "L0_gnn_b1", "L0_gnn_W2", "L0_gnn_b2", "L0_gnn_bn_gamma", "L0_gnn_bn_beta", "L0_gnn_bn_mean", "L0_gnn_bn_var",
        "L1_gnn_q_w", "L1_gnn_q_b", "L1_gnn_k_w", "L1_gnn_k_b", "L1_gnn_v_w", "L1_gnn_v_b", "L1_gnn_out_w", "L1_gnn_out_b",
        "L1_gnn_eb_w", "L1_gnn_eb_b"]


def kernel(**inputs):
    import numpy as _np
    import concourse.bacc as _bacc
    from concourse import mybir as _mybir
    from concourse.bass_utils import run_bass_kernel_spmd as _run

    nc = _bacc.Bacc("TRN2", target_bir_lowering=False, num_devices=1)
    arrays, args = {}, []
    for name in _INS:
        a = _np.ascontiguousarray(inputs[name])
        arrays[f"in_{name}_dram"] = a
        args.append(nc.dram_tensor(f"in_{name}_dram", a.shape, _mybir.dt.from_np(a.dtype), kind="ExternalInput").ap())
    args.append(nc.dram_tensor("out_0_dram", (N_NODES, D), F32, kind="ExternalOutput").ap())
    gnn(nc, *args)
    r = _run(nc, [arrays], core_ids=[0])
    return r.results[0]["out_0_dram"]
```

```python
from contextlib import ExitStack, contextmanager

import concourse.bass as bass
from concourse import mybir

F32, I32, BF16 = mybir.dt.float32, mybir.dt.int32, mybir.dt.bfloat16
ALU, ACT, AX = mybir.AluOpType, mybir.ActivationFunctionType, mybir.AxisListType

P = 128
N_NODES, N_EDGES, D = 12500, 200000, 128
HEADS = 8
HEAD_DIM = D // HEADS
NT = -(-N_NODES // P)
LAST_ROWS = N_NODES - (NT - 1) * P
PAD_NODE = NT * P - 1
HALF = 8
TURN = 2 * HALF
E_COLS = -(-N_EDGES // (P * TURN)) * TURN
E_TURNS = E_COLS // TURN
LAST_COLS = N_EDGES - (P - 1) * E_COLS
CHUNKS = P // HEADS
S_TILES = -(-(E_COLS + NT - 1) // TURN) * TURN
S_TURNS = S_TILES // TURN
LAST_TILES = E_COLS + NT - 1 - (S_TURNS - 1) * TURN
CHUNK_TILES = S_TILES // CHUNKS
CHUNK_LEN = CHUNK_TILES * P
AHEAD = 4
D_FIELDS, S_FIELDS = 2, 2 + HEADS
EMPTY_KEY = -1.5
NO_KEY = -30000.0
WINDOWS = 120
W_BLOCKS = S_TILES // WINDOWS
LN_EPS = BN_EPS = 1e-5
SUM_EPS = 1e-10
BREAK = -1e30
CHUNK = 7
N_CHUNKS = NT // CHUNK
CLAMPED = "node tiles are clamped to the last one where the table is built"

assert N_CHUNKS * CHUNK == NT and N_CHUNKS % 2 == 0 and NT % 2 == 0
assert 0 < LAST_TILES <= HALF
assert W_BLOCKS * WINDOWS == S_TILES and CHUNK_TILES * CHUNKS == S_TILES and LAST_COLS % TURN == 0
FULL_TURNS = LAST_COLS // TURN


def need(eng, sem, value):
    if isinstance(value, int) and value <= 0:
        return
    eng.wait_ge(sem, value)


@contextmanager
def phase_semaphores(nc):
    taken = []

    def sem(name):
        taken.append(nc.alloc_semaphore(name=name))
        return taken[-1]

    yield sem
    nc.clear_and_free_semaphores(taken)
    nc.all_engine_barrier()


class Chain:

    def __init__(self, eng, sem):
        self.eng, self.sem, self.base, self.k = eng, sem, 0, 0

    def turn(self, base):
        self.base, self.k = base, 0

    def __call__(self, ins):
        ins.then_inc(self.sem, 1)
        self.k += 1
        self.eng.wait_ge(self.sem, self.base + self.k)


def gnn(nc, x, src, dst, attr, w1, b1, w2, b2, gamma, beta, bn_mean, bn_var,
        q_w, q_b, k_w, k_b, v_w, v_b, out_w, out_b, eb_w, eb_b, out):
    dram = lambda name, shape: nc.dram_tensor(name, shape, F32).ap()
    h_table = [dram("h1_table", (NT * P, D)), dram("h2_table", (NT * P, D))]
    kv_table = dram("kv_table", (NT * P, 2 * D))
    x1_dram = dram("x1_dram", (NT * P, D))
    v_sorted = dram("v_sorted", (P, S_TILES, D))
    edge_src, edge_key = dram("edge_src", (S_TILES, P)), dram("edge_key", (S_TILES, P))
    d_slots = dram("d_slots", (P * S_TILES, D_FIELDS))
    s_slots = dram("s_slots", (P * S_TILES, S_FIELDS))

    whole = ExitStack()
    with whole:
        def sb(name, shape, dt=F32):
            return whole.enter_context(nc.sbuf_tensor(name, shape, dt))

        bank = [whole.enter_context(nc.psum_tensor(f"bank{i}", [P, 512], F32)) for i in range(8)]

        iota_bf = sb("iota_bf", [P, P], BF16)
        iota_half = sb("iota_half", [P, P], BF16)
        iota_p = sb("iota_p", [P, 1])
        ident = sb("ident", [P, P])
        ident_bf = sb("ident_bf", [P, P], BF16)
        before = sb("before", [P, P])
        before_bf = sb("before_bf", [P, P], BF16)
        next_row = sb("next_row", [P, P])
        wrap_row = sb("wrap_row", [P, P])
        ones = sb("ones", [P, P])
        zeros_bf = sb("zeros_bf", [P, P], BF16)
        ones_bf = sb("ones_bf", [P, P], BF16)
        eps_col = sb("eps_col", [P, 1])
        w1_sb, w2_sb = sb("w1_sb", [D, D]), sb("w2_sb", [D, D])
        qkv_t, out_t, eb_t = sb("qkv_t", [D, 3 * D]), sb("out_t", [D, D]), sb("eb_t", [D, HEADS])
        bias_parts = sb("bias_parts", [P, 3, D], BF16)
        b1_parts, b2_parts, out_parts = (bias_parts[:, n, :] for n in range(3))
        qkv_bc = sb("qkv_bc", [P, 3 * D])
        ebb_bc = sb("ebb_bc", [P, HALF, HEADS])
        bn_cols = sb("bn_cols", [D, 4])
        bn_scale, bn_shift = sb("bn_scale", [D, 1]), sb("bn_shift", [D, 1])
        dinv = sb("dinv", [P, NT])
        base_d, base_s = sb("base_d", [NT, P]), sb("base_s", [NT, P])
        S_ROW = 32
        sum_place = sb("sum_place", [1, NT], I32)
        node_rows = sb("node_rows", [S_ROW + 1, S_TILES], I32)
        node_d, node_s = node_rows[0:1, :], node_rows[S_ROW:S_ROW + 1, :]
        unsorted = sb("unsorted", [1, 1], I32)
        window_row, window_node = sb("window_row", [P, W_BLOCKS], I32), sb("window_node", [P, W_BLOCKS])
        node_s_bc = sb("node_s_bc", [P, S_TILES], BF16)
        lo_slots = sb("lo_slots", [P, S_TILES + AHEAD])
        lo_slots_bf = sb("lo_slots_bf", [P, S_TILES + AHEAD], BF16)
        slots_words = S_TILES * S_FIELDS
        region_a = sb("region_a", [P, slots_words])
        region_b = sb("region_b", [P, max(CHUNK_LEN, (NT + 1) * (D + HEADS))])
        region_c = sb("region_c", [P, max(S_TILES * D_FIELDS, CHUNK_LEN // 2 + 1)])
        EC = E_COLS + AHEAD
        at = [0]

        def part(words):
            at[0] += words
            return region_a[:, at[0] - words:at[0]]

        src_i, dst_i = part(E_COLS).bitcast(I32), part(E_COLS).bitcast(I32)
        s_hi, s_lo, d_hi, d_lo = part(EC), part(EC), part(EC), part(EC)
        d_lo_kept = part(EC)
        s_hi_bf, d_hi_bf = part(EC // 2).bitcast(BF16), part(EC // 2).bitcast(BF16)
        tmp_a, tmp_b = part(E_COLS), part(E_COLS)
        assert at[0] <= slots_words
        s_slot = region_a[:, :].rearrange("p (t f) -> p t f", f=S_FIELDS)
        seg_max = region_a[:, 0:CHUNK_LEN]
        weights = region_a[:, 0:S_TILES * HEADS].rearrange("p (t h) -> p t h", h=HEADS)
        nodes = region_b[:, 0:NT * D].rearrange("p (n d) -> p n d", d=D)
        scores_t = region_b[:, 0:CHUNK_LEN]
        sums = region_b[:, 0:(NT + 1) * (D + HEADS)].rearrange("p (n d) -> p n d", d=D + HEADS)
        d_slot = region_c[:, 0:S_TILES * D_FIELDS].rearrange("p (t f) -> p t f", f=D_FIELDS)
        breaks = region_c[:, 0:CHUNK_LEN // 2 + 1].bitcast(BF16)

        fetched = [whole.enter_context(nc.semaphore(f"fetched{k}")) for k in range(TURN)]

        def fetched_before(products, k):
            return products * (S_TURNS - (0 if k < LAST_TILES else 1))

        def column(flat):
            return flat.rearrange("(p one) -> p one", one=1)

        early = ExitStack()
        d_fill = early.enter_context(nc.sbuf_tensor("d_fill", [P, S_TILES // 4, D_FIELDS], F32))
        s_fill = early.enter_context(nc.sbuf_tensor("s_fill", [P, CHUNK_TILES, S_FIELDS], F32))

        with ExitStack() as ph:
            sem = ph.enter_context(phase_semaphores(nc))
            tmp = lambda n, s, d=F32: ph.enter_context(nc.sbuf_tensor(n, s, d))
            keys_clear, keys_in, consts, weights_in = sem("keys_clear"), sem("keys_in"), sem("consts"), sem("weights_in")
            filled, prep = sem("filled"), sem("prep")
            w_moved, w_taken, biases_in = sem("w_moved"), sem("w_taken"), sem("biases_in")
            bn_var_eps, edges_made = sem("bn_var_eps"), sem("edges_made")
            viol, viol_ready, prev_hi_ready = tmp("viol", [P, 2]), sem("viol_ready"), sem("prev_hi_ready")
            bias_left, bias_part = tmp("bias_left", [P, 3, D]), tmp("bias_part", [P, 3, D], BF16)
            no_edges = tmp("no_edges", [S_TILES - E_COLS, 2, P])
            raw_w = tmp("raw_w", [P, 4, D])
            raw_eb = tmp("raw_eb", [HEADS, D])
            bn_std = tmp("bn_std", [D, 1])
            block = ph.enter_context(nc.Block())
            CONSTS = 20
            whole_rows = 96

            @block.sync
            def _(sp):
                sp.wait_ge(keys_clear, 2)
                for keys, flat in ((dst_i, dst), (src_i, src)):
                    rows = flat[0:(P - 1) * E_COLS].rearrange("(p c) -> p c", c=E_COLS)
                    sp.dma_start(keys[0:whole_rows, :], rows[0:whole_rows, :]).then_inc(keys_in, 16)
                    sp.dma_start(keys[whole_rows:P - 1, :], rows[whole_rows:P - 1, :]).then_inc(keys_in, 16)
                    sp.dma_start(keys[P - 1:P, 0:LAST_COLS],
                                 flat[(P - 1) * E_COLS:N_EDGES].rearrange("(a c) -> a c", a=1)).then_inc(keys_in, 16)
                for n, w in enumerate((q_w, k_w, v_w, out_w)):
                    sp.dma_start(raw_w[:, n, :], w).then_inc(weights_in, 16)
                sp.dma_start(raw_eb[:, :], eb_w).then_inc(weights_in, 16)
                sp.dma_start(w1_sb[:, :], w1).then_inc(biases_in, 16)
                sp.dma_start(w2_sb[:, :], w2).then_inc(biases_in, 16)
                row = lambda b: b.rearrange("(a d) -> a d", a=1).to_broadcast([P, D])
                for n, b in enumerate((b1, b2, out_b)):
                    sp.dma_start(bias_left[:, n, :], row(b)).then_inc(biases_in, 16)
                for n, b in enumerate((q_b, k_b, v_b)):
                    sp.dma_start(qkv_bc[:, n * D:(n + 1) * D], row(b)).then_inc(biases_in, 16)
                for k in range(HALF):
                    sp.dma_start(ebb_bc[:, k, :],
                                 eb_b.rearrange("(a d) -> a d", a=1).to_broadcast([P, HEADS])).then_inc(biases_in, 16)
                for n, b in enumerate((gamma, beta, bn_mean, bn_var)):
                    sp.dma_start(bn_cols[:, n:n + 1], column(b)).then_inc(biases_in, 16)
                sp.wait_ge(biases_in, 16 * 20)

            @block.scalar
            def _(act):
                act.wait_ge(edges_made, 4)
                for m, (keys, table) in enumerate(((tmp_a, edge_src), (tmp_b, edge_key))):
                    act.dma_start(table[0:E_COLS, :].rearrange("a d -> (a d)").rearrange("(p c) -> p c", p=P), keys).then_inc(filled, 16)
                    act.dma_start(table[E_COLS:S_TILES, :], no_edges[:, m, :]).then_inc(filled, 16)
                act.wait_ge(biases_in, 16 * 20)
                act.wait_ge(consts, 1)
                act.activation(bn_std[:, :], bn_cols[:, 3:4], ACT.Sqrt, bias=eps_col[:, 0:1]).then_inc(bn_var_eps, 1)
                act.wait_ge(filled, 16 * 4)

            @block.gpsimd
            def _(pool):
                g = nc.gpsimd
                made, order = [0], consts

                def done(ins):
                    ins.then_inc(order, 1)
                    made[0] += 1
                    return made[0]

                done(g.memset(eps_col[:, :], LN_EPS))
                done(g.iota(iota_bf[:, :], pattern=[[1, P]], base=0, channel_multiplier=0,
                            allow_small_or_imprecise_dtypes=True))
                half = done(g.iota(iota_half[:, :], pattern=[[1, P]], base=0, channel_multiplier=0,
                                   allow_small_or_imprecise_dtypes=True))
                pool.wait_ge(order, half)
                done(g.tensor_scalar(iota_half[:, :], iota_half[:, :], 0.5, None, ALU.add))
                done(g.iota(iota_p[:, :], pattern=[[0, 1]], base=0, channel_multiplier=1,
                            allow_small_or_imprecise_dtypes=True))
                for m in (ident, ident_bf, next_row, wrap_row, zeros_bf):
                    done(g.memset(m[:, :], 0.0))
                for m in (ones, ones_bf, before, before_bf):
                    last = done(g.memset(m[:, :], 1.0))
                pool.wait_ge(order, last)
                for m in (ident, ident_bf):
                    done(g.affine_select(out=m[:, :], in_=m[:, :], compare_op=ALU.not_equal, fill=1.0, base=0,
                                         pattern=[[-1, P]], channel_multiplier=1))
                for m in (before, before_bf):
                    done(g.affine_select(out=m[:, :], in_=m[:, :], compare_op=ALU.is_gt, fill=0.0, base=0,
                                         pattern=[[1, P]], channel_multiplier=-1))
                done(g.affine_select(out=next_row[:, :], in_=next_row[:, :], compare_op=ALU.not_equal, fill=1.0,
                                     base=-1, pattern=[[1, P]], channel_multiplier=-1))
                done(g.affine_select(out=wrap_row[:, :], in_=wrap_row[:, :], compare_op=ALU.not_equal, fill=1.0,
                                     base=-(P - 1), pattern=[[-1, P]], channel_multiplier=1))
                pool.wait_ge(order, made[0])
                assert made[0] == CONSTS

            @block.vector
            def _(dve):
                v = nc.vector
                link = Chain(dve, prep)
                v.memset(dst_i, PAD_NODE).then_inc(keys_clear, 1)
                v.memset(src_i, PAD_NODE).then_inc(keys_clear, 1)
                link(v.memset(nodes[:, NT - 1, :], 0.0))
                link(v.memset(d_fill[:, :, :], 0.0))
                link(v.memset(d_fill[:, :, 1:2], EMPTY_KEY))
                link(v.memset(s_fill[:, :, :], 0.0))
                link(v.memset(s_fill[:, :, 1:2], EMPTY_KEY))
                dve.wait_ge(keys_in, 16 * 6)
                src_f, dst_f = tmp_a, tmp_b
                link(v.tensor_copy(src_f, src_i))
                link(v.tensor_copy(dst_f, dst_i))
                cut = slice(0, E_COLS)
                for a in (s_hi, s_lo, d_hi, d_lo, d_lo_kept):
                    v.memset(a[:, E_COLS:], 0.0)
                v.memset(s_hi_bf[:, E_COLS:], 0.0)
                link(v.memset(d_hi_bf[:, E_COLS:], 0.0))
                v.memset(no_edges[:, 0, :], 0.0).then_inc(edges_made, 1)
                v.memset(no_edges[:, 1, :], NO_KEY).then_inc(edges_made, 1)
                for key, hi, lo, hi_bf in ((src_f, s_hi, s_lo, s_hi_bf), (dst_f, d_hi, d_lo, d_hi_bf)):
                    as_int = lo[:, cut].bitcast(I32)
                    link(v.tensor_copy(as_int, key))
                    link(v.tensor_single_scalar(as_int, as_int, P.bit_length() - 1, ALU.arith_shift_right))
                    link(v.tensor_copy(hi[:, cut], as_int))
                    link(v.tensor_copy(hi_bf[:, cut], hi[:, cut]))
                    link(v.scalar_tensor_tensor(lo[:, cut], hi[:, cut], -float(P), key, ALU.mult, ALU.add))
                kept = d_lo_kept[:, cut]
                link(v.tensor_tensor(kept, src_f, dst_f, ALU.is_equal))
                link(v.scalar_tensor_tensor(kept, dst_f, -NO_KEY, kept, ALU.add, ALU.mult))
                v.tensor_tensor(dst_f, dst_f, kept, ALU.subtract).then_inc(edges_made, 2)
                dve.wait_ge(edges_made, 4)
                later = d_lo_kept[:, 0:E_COLS - 1]
                link(v.tensor_tensor(later, d_hi[:, 1:E_COLS], d_hi[:, 0:E_COLS - 1], ALU.is_lt))
                link(v.tensor_reduce(viol[:, 0:1], later, AX.X, ALU.add))
                link(v.scalar_tensor_tensor(kept, d_hi[:, cut], -float(P), dst_f, ALU.mult, ALU.add))
                dve.wait_ge(prev_hi_ready, 1)
                link(v.tensor_tensor(viol[:, 1:2], d_hi[:, 0:1], bank[2][:, 0:1], ALU.is_lt))
                v.tensor_tensor(viol[:, 0:1], viol[:, 0:1], viol[:, 1:2], ALU.add).then_inc(viol_ready, 1)
                dve.wait_ge(prev_hi_ready, 2)
                link(v.tensor_scalar(unsorted[:, :], bank[3][0:1, 0:1], 1.0, None, ALU.min))
                dve.wait_ge(w_moved, 5)
                link(v.tensor_copy(qkv_t[:, :], bank[0][:, 0:3 * D]))
                link(v.tensor_copy(out_t[:, :], bank[0][:, 3 * D:4 * D]))
                link(v.tensor_copy(eb_t[:, :], bank[1][:, 0:HEADS]))
                dve.wait_ge(biases_in, 16 * 20)
                dve.wait_ge(bn_var_eps, 1)
                link(v.reciprocal(bn_std[:, :], bn_std[:, :]))
                link(v.tensor_tensor(bn_scale[:, :], bn_cols[:, 0:1], bn_std[:, :], ALU.mult))
                link(v.tensor_tensor(bn_shift[:, :], bn_cols[:, 2:3], bn_scale[:, :], ALU.mult))
                link(v.tensor_tensor(bn_shift[:, :], bn_cols[:, 1:2], bn_shift[:, :], ALU.subtract))
                link(v.tensor_scalar(qkv_bc[:, 0:D], qkv_bc[:, 0:D], HEAD_DIM ** -0.5, None, ALU.mult))
                link(v.memset(bias_parts[:, :, :], 0.0))
                for at in (0, 32, 64):
                    link(v.tensor_copy(bias_part[:, :, :], bias_left[:, :, :]))
                    link(v.tensor_copy(bias_parts[at:at + 1, :, :], bias_part[at:at + 1, :, :]))
                    link(v.tensor_tensor(bias_left[:, :, :], bias_left[:, :, :], bias_part[:, :, :], ALU.subtract))

            @block.tensor
            def _(pe):
                pe.wait_ge(consts, CONSTS)
                pe.wait_ge(weights_in, 16 * 5)
                for n in range(4):
                    nc.tensor.transpose(bank[0][:, n * D:(n + 1) * D], raw_w[:, n, :], ident[:, :]).then_inc(w_moved, 1)
                nc.tensor.transpose(bank[1][:, 0:HEADS], raw_eb[:, :], ident[0:HEADS, 0:HEADS]).then_inc(w_moved, 1)
                pe.wait_ge(edges_made, 4)
                nc.tensor.matmul(bank[2][:, 0:1], next_row[:, :], d_hi[:, E_COLS - 1:E_COLS], start=True, stop=True).then_inc(prev_hi_ready, 1)
                pe.wait_ge(viol_ready, 1)
                nc.tensor.matmul(bank[3][:, 0:1], ones[:, :], viol[:, 0:1], start=True, stop=True).then_inc(prev_hi_ready, 1)

        class Count:
            RING = TURN
            scatters = False

            def __init__(self, sem, tmp, hi, lo, lo_kept=None, lead=0):
                self.lead = lead
                self.hi, self.lo, self.lo_kept = hi, lo, lo_kept
                self.hot_ready, self.signs_ready, self.used = sem("hot_ready"), sem("signs_ready"), sem("hot_used")
                self.hot = tmp("hot_hi", [P, self.RING, NT], BF16)
                self.sign = tmp("sign", [P, self.RING, P], BF16)
                if lo_kept is not None:
                    self.kept = tmp("hot_kept", [P, self.RING, P], BF16)
                    self.keys, self.keys_ready = tmp("keys", [P, 3, TURN]), sem("keys_ready")
                    self.shared, self.share_go = sem("shared"), sem("share_go")

            def stage(self, pool, i, h):
                need(pool, self.used, (i - 1) * TURN + (h + 1) * HALF)
                for n, keys in enumerate((self.hi, self.lo, self.lo_kept)):
                    nc.gpsimd.tensor_copy(self.keys[:, n, h * HALF:(h + 1) * HALF], keys[:, bass.ds(i * TURN + h * HALF, HALF)]).then_inc(self.keys_ready, 1)

            def share(self, pool, i, h):
                for k in range(h * HALF + 3, (h + 1) * HALF, 4):
                    pool.wait_ge(self.keys_ready, (2 * i + h + 1) * 3)
                    pool.sem_inc(self.share_go, 1)
                    nc.gpsimd.tensor_scalar(self.kept[:, k, :], iota_bf[:, :], self.key(2, None, k), None, ALU.is_equal).then_inc(self.shared, 1)

            def key(self, n, c, k):
                if self.lo_kept is not None:
                    return self.keys[:, n, k:k + 1]
                return (self.hi, self.lo)[n][:, bass.ds(c, 1)]

            def ready(self, eng, i, c, k):
                if k % HALF == 0:
                    need(eng, self.used, c + HALF - self.RING)
                    if self.lo_kept is not None:
                        eng.wait_ge(self.keys_ready, (2 * i + k // HALF % 2 + 1) * 3)

            def one_hots(self, dve, i, k):
                c, slot = i * TURN + k, k % self.RING
                self.ready(dve, i, c, k)
                last = nc.vector.tensor_scalar(self.hot[:, slot, :], iota_bf[:, 0:NT], self.key(0, c, k), None, ALU.is_equal)
                if self.lo_kept is not None and k % 4 != 3:
                    last = nc.vector.tensor_scalar(self.kept[:, slot, :], iota_bf[:, :], self.key(2, c, k), None, ALU.is_equal)
                last.then_inc(self.hot_ready, 1)

            def vector_start(self, dve):
                for k in range(self.lead):
                    self.one_hots(dve, 0, k)

            def vector_step(self, dve, i, k):
                self.one_hots(dve, i, k + self.lead)

            def vector_end_step(self, dve, i, k):
                pass

            def scalar_step(self, act, i, k):
                c, slot = i * TURN + k, k % self.RING
                self.ready(act, i, c, k)
                nc.scalar.activation(self.sign[:, slot, :], iota_half[:, :], ACT.Sign, bias=self.key(1, c, k), scale=-1.0).then_inc(self.signs_ready, 1)

            def zeros(self, **at):
                for n in range(1 if self.lo_kept is None else 2):
                    nc.tensor.matmul(bank[n][0:NT, 0:P], zeros_bf[:, 0:NT], zeros_bf[:, :], **at)

            def tensor_start(self, pe):
                self.zeros(start=True, stop=False)

            def tensor_step(self, pe, i, k):
                c, slot = i * TURN + k, k % self.RING
                pe.wait_ge(self.hot_ready, c + 1)
                pe.wait_ge(self.signs_ready, c + 1)
                if self.lo_kept is not None and k % 4 == 3:
                    pe.wait_ge(self.shared, i * (TURN // 4) + k // 4 + 1)
                last = nc.tensor.matmul(bank[0][0:NT, 0:P], self.hot[:, slot, :], self.sign[:, slot, :], start=False, stop=False)
                if self.lo_kept is not None:
                    last = nc.tensor.matmul(bank[1][0:NT, 0:P], self.hot[:, slot, :], self.kept[:, slot, :], start=False, stop=False)
                last.then_inc(self.used, 1)

            def tensor_end_step(self, pe, i, k):
                pass

            def tensor_end(self, pe):
                self.zeros(start=False, stop=True)

            def sync(self, sp):
                pass

        class Sort:
            RING = 4
            scatters = True
            CHAINED = 2 * 4

            def __init__(self, sem, tmp, hi, lo, hi_bf, lo_kept, base, index, table, fields, with_bias):
                self.hi, self.lo, self.hi_bf, self.lo_kept, self.base = hi, lo, hi_bf, lo_kept, base
                self.index, self.table, self.with_bias = index, table, with_bias
                (self.hot_ready, self.tile_row_ready, self.masks_ready, self.counted, self.next_ready, self.found, self.picked,
                 self.slot_step, self.payload_ready, self.go, self.slots_in) = (sem(n) for n in (
                     "hot_ready", "tile_row_ready", "masks_ready", "counted", "next_ready", "found", "picked",
                     "slot_step", "payload_ready", "go", "slots_in"))
                self.scattered = [sem(f"scattered{h}") for h in range(2)]
                self.hot_hi, self.hot_lo = tmp("hot_hi", [P, self.RING, NT], BF16), tmp("hot_lo", [P, self.RING, P], BF16)
                self.earlier = tmp("earlier", [P, self.RING, P], BF16)
                self.hi_t = tmp("hi_t", [NT, self.RING, P])
                self.next_slot = tmp("next_slot", [NT, 2, P])
                self.junk = tmp("junk", [P, P])
                self.slot = tmp("slot", [P, 2, HALF])
                self.slot_i, self.row_i, self.tile_i = (tmp(n, [P, HALF], I32) for n in ("slot_i", "row_i", "tile_i"))
                self.where = tmp("where", [P, 2, HALF], I32)
                self.payload = tmp("payload", [P, 2, HALF, fields])
                self.tile_row, self.found_in, self.running = bank[0], [bank[1], bank[2]], bank[3]
                if with_bias:
                    self.attr_in = [sem(f"attr_in{h}") for h in range(2)]
                    self.attr_moved, self.attr_kept, self.bias_ready = sem("attr_moved"), sem("attr_kept"), sem("bias_ready")
                    self.attr_sb = tmp("attr_sb", [P, 2, HALF, D])
                    self.attr_t = tmp("attr_t", [D, 2, 4 * P])
                    self.attr_bank, self.bias_out = bank[4], bank[5]

            def one_hots(self, c, k):
                s = k % self.RING
                need(self.dve, self.found, c + 1 - self.RING)
                nc.vector.tensor_scalar(self.hot_hi[:, s, :], iota_bf[:, 0:NT], self.hi[:, bass.ds(c, 1)], None, ALU.is_equal)
                nc.vector.tensor_scalar(self.hot_lo[:, s, :], iota_bf[:, :], self.lo[:, bass.ds(c, 1)], None, ALU.is_equal).then_inc(self.hot_ready, 1)

            def masks(self, c, k):
                s = k % self.RING
                need(self.dve, self.tile_row_ready, c + 1)
                nc.vector.tensor_scalar(self.hi_t[:, s, :], self.tile_row[0:NT, 0:P], iota_p[0:NT, 0:1], None, ALU.is_equal)
                nc.vector.scalar_tensor_tensor(self.earlier[:, s, :], self.tile_row[:, 0:P], self.hi[:, bass.ds(c, 1)], before_bf[:, :],
                                               ALU.is_equal, ALU.mult).then_inc(self.masks_ready, 1)

            def vector_start(self, dve):
                self.dve, self.link = dve, Chain(dve, self.slot_step)
                for c in range(2):
                    self.one_hots(c, c)
                self.masks(0, 0)

            def vector_step(self, dve, i, k):
                c = i * TURN + k
                self.one_hots(c + 2, k + 2)
                self.masks(c + 1, k + 1)

            def vector_end_step(self, dve, i, k):
                v, link = nc.vector, self.link
                c, h = i * TURN + k, k // HALF
                if k == 0:
                    link.turn(i * self.CHAINED)
                dve.wait_ge(self.found, c + 1)
                need(dve, self.picked, c)
                v.tensor_tensor_reduce(out=self.junk[:, :], in0=self.found_in[k % 2][:, 0:P], in1=self.hot_lo[:, k % self.RING, :],
                                       scale=1.0, scalar=0.0, op0=ALU.mult, op1=ALU.add,
                                       accum_out=self.slot[:, h, k % HALF:k % HALF + 1]).then_inc(self.picked, 1)
                if k % HALF < HALF - 1:
                    return
                cols = bass.ds(i * TURN + h * HALF, HALF)
                dve.wait_ge(self.picked, c + 1)
                link(v.tensor_copy(self.slot_i[:, :], self.slot[:, h, :]))
                link(v.tensor_single_scalar(self.tile_i[:, :], self.slot_i[:, :], P.bit_length() - 1, ALU.arith_shift_right))
                link(v.tensor_single_scalar(self.row_i[:, :], self.slot_i[:, :], P - 1, ALU.bitwise_and))
                need(dve, self.scattered[h], i * HALF * 16)
                link(v.scalar_tensor_tensor(self.where[:, h, :], self.row_i[:, :], float(S_TILES), self.tile_i[:, :], ALU.mult, ALU.add))
                v.tensor_copy(self.payload[:, h, :, 0:1].bitcast(I32).rearrange("p k a -> p (k a)"), self.index[:, cols])
                if self.with_bias:
                    dve.wait_ge(self.bias_ready, 2 * i + h + 1)
                    v.tensor_tensor(self.payload[:, h, :, 2:S_FIELDS],
                                    self.bias_out[:, h * HALF * HEADS:(h + 1) * HALF * HEADS].rearrange("p (k a) -> p k a", a=HEADS),
                                    ebb_bc[:, :, :], ALU.add)
                v.tensor_copy(self.payload[:, h, :, 1:2].rearrange("p k a -> p (k a)"), self.lo_kept[:, cols]).then_inc(self.payload_ready, 1)

            def spread_tiles(self, pe, c):
                need(pe, self.masks_ready, c)
                nc.tensor.matmul(self.tile_row[:, 0:P], self.hi_bf[:, bass.ds(c, 1)].to_broadcast([P, P]), ident_bf[:, :],
                                 start=True, stop=True).then_inc(self.tile_row_ready, 1)

            def tensor_start(self, pe):
                nc.tensor.matmul(self.running[0:NT, 0:P], ident[0:NT, 0:NT], self.base[:, :], start=True, stop=True).then_inc(self.counted, 1)
                for c in range(2):
                    self.spread_tiles(pe, c)

            def tensor_step(self, pe, i, k):
                t = nc.tensor
                c, s = i * TURN + k, k % self.RING
                pe.wait_ge(self.hot_ready, c + 1)
                pe.wait_ge(self.next_ready, c + 1)
                t.matmul(self.running[0:NT, 0:P], self.hot_hi[:, s, :], self.hot_lo[:, s, :], start=False, stop=True,
                         skip_group_check=True).then_inc(self.counted, 1)
                pe.wait_ge(self.masks_ready, c + 1)
                need(pe, self.picked, c - 1)
                t.matmul(self.found_in[k % 2][:, 0:P], self.hi_t[:, s, :], self.next_slot[:, k % 2, :], start=True, stop=False)
                t.matmul(self.found_in[k % 2][:, 0:P], self.earlier[:, s, :], self.hot_lo[:, s, :], start=False, stop=True).then_inc(self.found, 1)
                if not self.with_bias:
                    return
                q, h, j = 2 * i + k // HALF, k // HALF, k % HALF
                if j in (1, 3):
                    g = j // 2
                    if g == 0:
                        pe.wait_ge(self.attr_in[h], (i + 1) * (16 * 3))
                    need(pe, self.attr_kept, q * 2 + g)
                    for m in range(4):
                        last = t.transpose(self.attr_bank[:, m * P:(m + 1) * P], self.attr_sb[:, h, g * 4 + m, :], ident[:, :])
                    last.then_inc(self.attr_moved, 1)
                if j in (4, 6):
                    g = (j - 4) // 2
                    pe.wait_ge(self.attr_kept, q * 2 + g + 1)
                    need(pe, self.payload_ready, q)
                    for m in range(4):
                        at_col = (h * HALF + g * 4 + m) * HEADS
                        last = t.matmul(self.bias_out[:, at_col:at_col + HEADS], self.attr_t[:, g, m * P:(m + 1) * P], eb_t[:, :],
                                        start=True, stop=True)
                    if g == 1:
                        last.then_inc(self.bias_ready, 1)

            def tensor_end_step(self, pe, i, k):
                self.spread_tiles(pe, i * TURN + k + 2)

            def tensor_end(self, pe):
                pass

            def scalar_step(self, act, i, k):
                c = i * TURN + k
                act.wait_ge(self.counted, c + 1)
                need(act, self.found, c - 1)
                nc.scalar.copy(self.next_slot[:, k % 2, :], self.running[0:NT, 0:P]).then_inc(self.next_ready, 1)
                if self.with_bias and k % HALF in (2, 4):
                    q, g = 2 * i + k // HALF, k % HALF // 2 - 1
                    act.wait_ge(self.attr_moved, q * 2 + g + 1)
                    need(act, self.bias_ready, q)
                    nc.scalar.copy(self.attr_t[:, g, :], self.attr_bank[:, :]).then_inc(self.attr_kept, 1)

            def scatter(self, pool, i, h):
                pool.wait_ge(self.payload_ready, 2 * i + h + 1)
                pool.sem_inc(self.go, 1)
                for k in range(HALF):
                    nc.gpsimd.indirect_dma_start(self.table, bass.IndirectOffsetOnAxis(ap=self.where[:, h, k:k + 1], axis=0),
                                                 self.payload[:, h, k, :], None).then_inc(self.scattered[h], 16)

            def scatter_end(self, pool):
                for h in range(2):
                    pool.wait_ge(self.scattered[h], E_TURNS * HALF * 16)

            def sync(self, sp):
                if not self.with_bias:
                    return
                attr_rows = attr[0:(P - 1) * E_COLS, :].rearrange("(p c) d -> p c d", c=E_COLS)
                attr_last = attr[(P - 1) * E_COLS:N_EDGES, :].rearrange("(p c) d -> p c d", p=1)
                whole_rows = 96

                def load(i, h, last_too):
                    need(sp, self.attr_moved, (2 * (i - 1) + h) * 2 + 2)
                    cols = bass.ds(i * TURN + h * HALF, HALF)
                    sp.dma_start(self.attr_sb[0:whole_rows, h, :, :], attr_rows[0:whole_rows, cols, :]).then_inc(self.attr_in[h], 16)
                    sp.dma_start(self.attr_sb[whole_rows:P - 1, h, :, :], attr_rows[whole_rows:P - 1, cols, :]).then_inc(self.attr_in[h], 16)
                    again = cols if last_too else bass.ds(h * HALF, HALF)
                    sp.dma_start(self.attr_sb[P - 1:P, h, :, :], attr_last[:, again, :]).then_inc(self.attr_in[h], 16)

                for h in range(2):
                    load(0, h, True)
                with sp.Fori(1, FULL_TURNS) as i:
                    for h in range(2):
                        load(i, h, True)
                with sp.Fori(FULL_TURNS, E_TURNS) as i:
                    for h in range(2):
                        load(i, h, False)

        def count_destinations():
            with ExitStack() as ph:
                own = ph.enter_context(phase_semaphores(nc))
                work = Count(lambda n: own(f"count_d_{n}"),
                             lambda n, s, d=F32: ph.enter_context(nc.sbuf_tensor(f"count_d_{n}", s, d)), d_hi, d_lo, d_lo_kept)
                rows_in, filled = own("x_rows_in"), own("slots_filled")
                block = ph.enter_context(nc.Block())

                @block.sync
                def _(sp):
                    sp.dma_start(nodes[:, 0:NT - 1, :], x[0:(NT - 1) * P, :].rearrange("(n p) d -> p n d", p=P)).then_inc(rows_in, 16)
                    sp.dma_start(nodes[0:LAST_ROWS, NT - 1, :], x[(NT - 1) * P:N_NODES, :]).then_inc(rows_in, 16)
                    quarter = S_TILES // 4
                    for n in range(4):
                        sp.dma_start(d_slots.rearrange("(p t) f -> p t f", p=P)[:, n * quarter:(n + 1) * quarter, :],
                                     d_fill[:, :, :]).then_inc(filled, 16)
                    for n in range(CHUNKS):
                        sp.dma_start(s_slots.rearrange("(p t) f -> p t f", p=P)[:, n * CHUNK_TILES:(n + 1) * CHUNK_TILES, :],
                                     s_fill[:, :, :]).then_inc(filled, 16)
                    sp.wait_ge(rows_in, 16 * 2)
                    sp.wait_ge(filled, 16 * (4 + CHUNKS))

                @block.gpsimd
                def _(pool):
                    def turn(i):
                        for h in range(2):
                            work.stage(pool, i, h)
                            work.share(pool, i, h)

                    turn(0)
                    with pool.Fori(1, E_TURNS) as i:
                        turn(i)

                @block.vector
                def _(dve):
                    def turn(i):
                        for k in range(TURN):
                            work.vector_step(dve, i, k)

                    turn(0)
                    with dve.Fori(1, E_TURNS) as i:
                        turn(i)

                @block.scalar
                def _(act):
                    def turn(i):
                        for k in range(TURN):
                            work.scalar_step(act, i, k)

                    turn(0)
                    with act.Fori(1, E_TURNS) as i:
                        turn(i)

                @block.tensor
                def _(pe):
                    work.tensor_start(pe)
                    with pe.Fori(0, E_TURNS) as i:
                        for k in range(TURN):
                            work.tensor_step(pe, i, k)
                    work.tensor_end(pe)

        def find_bases(name, base, node, row, by_dst):
            with ExitStack() as ph:
                own = ph.enter_context(phase_semaphores(nc))
                sem = lambda n: own(f"{name}_{n}")
                tmp = lambda n, s, d=F32: ph.enter_context(nc.sbuf_tensor(f"{name}_{n}", s, d))
                step, edges_ready, first_ready, tiles_ready, starts_ready, mask_ready, nodes_ready, iota_made = (
                    sem(n) for n in ("step", "edges_ready", "first_ready", "tiles_ready", "starts_ready", "mask_ready", "nodes_ready", "iota_made"))
                deg_ready, deg_moved, deg_root, map_ready, rows_ready = (
                    sem(n) for n in ("deg_ready", "deg_moved", "deg_root", "map_ready", "rows_ready"))
                upto = tmp("upto", [NT, P])
                edges, first, n_tiles, start_tile, end_tile, start_slot, some = (
                    tmp(n, [NT, 1]) for n in ("edges", "first", "n_tiles", "start_tile", "end_tile", "start_slot", "some"))
                bounds, bounds_i = tmp("bounds", [NT, 2]), tmp("bounds_i", [NT, 2], I32)
                tile_map = tmp("tile_map", [NT, 2])
                passed, iota_t = tmp("passed", [NT, S_TILES]), tmp("iota_t", [NT, S_TILES])
                if by_dst:
                    deg, deg_t = tmp("deg", [NT, P]), tmp("deg_t", [P, NT])
                    inside, tile_no = tmp("inside", [NT, S_TILES]), tmp("tile_no", [P, W_BLOCKS])
                QUARTER = S_TILES // 4
                SHIFT = P.bit_length() - 1
                block = ph.enter_context(nc.Block())

                @block.vector
                def _(dve):
                    v = nc.vector
                    link = Chain(dve, step)
                    if by_dst:
                        v.tensor_scalar(deg[:, :], bank[1][0:NT, 0:P], 1.0, None, ALU.add).then_inc(deg_ready, 1)
                    link(v.tensor_copy(upto[:, :], bank[0][0:NT, 0:P]))
                    link(v.tensor_scalar(edges[:, :], upto[:, P - 1:P], -1.0, None, ALU.mult))
                    link(v.tensor_scalar(upto[:, :], upto[:, :], edges[:, :], -0.5, ALU.subtract, ALU.mult))
                    if by_dst:
                        v.tensor_copy(first[:, :], edges[:, :]).then_inc(edges_ready, 1)
                        dve.wait_ge(first_ready, 1)
                        link(v.tensor_copy(bounds[:, 0:1], bank[3][0:NT, 0:1]))
                        link(v.tensor_scalar(bounds[:, 1:2], bounds[:, 0:1], edges[:, :], -1.0, ALU.add, ALU.add))
                        link(v.tensor_copy(bounds_i[:, :], bounds[:, :]))
                        link(v.tensor_single_scalar(bounds_i[:, :], bounds_i[:, :], SHIFT, ALU.arith_shift_right))
                        link(v.tensor_copy(bounds[:, :], bounds_i[:, :]))
                        link(v.tensor_scalar(n_tiles[:, :], bounds[:, 1:2], bounds[:, 0:1], 1.0, ALU.subtract, ALU.add))
                        link(v.tensor_scalar(some[:, :], edges[:, :], 1.0, None, ALU.min))
                        v.tensor_tensor(n_tiles[:, :], n_tiles[:, :], some[:, :], ALU.mult).then_inc(tiles_ready, 1)
                    else:
                        link(v.tensor_scalar(bounds[:, 0:1], edges[:, :], float(P - 1), None, ALU.add))
                        link(v.tensor_copy(bounds_i[:, 0:1], bounds[:, 0:1]))
                        link(v.tensor_single_scalar(bounds_i[:, 0:1], bounds_i[:, 0:1], SHIFT, ALU.arith_shift_right))
                        v.tensor_copy(n_tiles[:, :], bounds_i[:, 0:1]).then_inc(tiles_ready, 1)
                    dve.wait_ge(tiles_ready, 1)
                    dve.wait_ge(starts_ready, 1)
                    link(v.tensor_copy(start_tile[:, :], bank[4][0:NT, 0:1]))
                    link(v.tensor_tensor(end_tile[:, :], start_tile[:, :], n_tiles[:, :], ALU.add))
                    link(v.tensor_scalar(start_slot[:, :], start_tile[:, :], float(P), None, ALU.mult))
                    link(v.tensor_copy(base[:, 0:1], start_slot[:, :]))
                    link(v.tensor_scalar(base[:, 1:], upto[:, 0:P - 1], start_slot[:, :], None, ALU.add))
                    if by_dst:
                        link(v.tensor_tensor(tile_map[:, 0:1], bounds[:, 0:1], start_tile[:, :], ALU.subtract))
                        link(v.tensor_scalar(tile_map[:, 1:2], iota_p[0:NT, :], float(P), None, ALU.mult))
                    dve.wait_ge(iota_made, 2 if by_dst else 1)
                    v.tensor_scalar(passed[:, :], iota_t[0:NT, :], end_tile[:, :], None, ALU.is_ge).then_inc(mask_ready, 1)
                    if by_dst:
                        dve.wait_ge(mask_ready, 1)
                        v.scalar_tensor_tensor(inside[:, :], iota_t[0:NT, :], start_tile[:, :], passed[:, :], ALU.is_ge, ALU.subtract).then_inc(map_ready, 1)
                    dve.wait_ge(nodes_ready, 1)
                    for j in range(4):
                        part_of = slice(j * QUARTER, (j + 1) * QUARTER)
                        if not by_dst:
                            link(v.tensor_scalar(node_s_bc[:, part_of], bank[4 + j][:, 0:QUARTER], float(NT - 1), None, ALU.min))
                        link(v.tensor_scalar(node[:, part_of], bank[4 + j][row:row + 1, 0:QUARTER], float(NT - 1), None, ALU.min))
                    if by_dst:
                        dve.wait_ge(rows_ready, 1)
                        mapped = bank[1][0:WINDOWS, 0:2 * W_BLOCKS].rearrange("p (b a) -> p a b", a=2)
                        link(v.tensor_tensor(window_row[0:WINDOWS, :], mapped[:, 0, :], tile_no[0:WINDOWS, :], ALU.add))
                        link(v.tensor_copy(window_node[0:WINDOWS, :], mapped[:, 1, :]))
                        dve.wait_ge(deg_root, 1)
                        link(v.reciprocal(dinv[:, :], deg_t[:, :]))

                @block.tensor
                def _(pe):
                    if by_dst:
                        pe.wait_ge(deg_ready, 1)
                        nc.tensor.transpose(bank[5][:, 0:NT], deg[:, :], ident[0:NT, 0:NT]).then_inc(deg_moved, 1)
                        pe.wait_ge(edges_ready, 1)
                        nc.tensor.matmul(bank[3][0:NT, 0:1], before[0:NT, 0:NT], first[:, :], start=True, stop=True).then_inc(first_ready, 1)
                    pe.wait_ge(tiles_ready, 1)
                    nc.tensor.matmul(bank[4][0:NT, 0:1], before[0:NT, 0:NT], n_tiles[:, :], start=True, stop=True).then_inc(starts_ready, 1)
                    if by_dst:
                        pe.wait_ge(deg_root, 1)
                    pe.wait_ge(mask_ready, 1)
                    for j in range(4):
                        last = nc.tensor.matmul(bank[4 + j][:, 0:QUARTER], ones[0:NT, :], passed[:, j * QUARTER:(j + 1) * QUARTER],
                                                start=True, stop=True)
                    last.then_inc(nodes_ready, 1)
                    if by_dst:
                        pe.wait_ge(map_ready, 1)
                        for b in range(W_BLOCKS):
                            last = nc.tensor.matmul(bank[1][0:WINDOWS, 2 * b:2 * b + 2], inside[:, b * WINDOWS:(b + 1) * WINDOWS],
                                                    tile_map[:, :], start=True, stop=True)
                        last.then_inc(rows_ready, 1)

                @block.gpsimd
                def _(pool):
                    nc.gpsimd.iota(iota_t[:, :], pattern=[[1, S_TILES]], base=0, channel_multiplier=0,
                                   allow_small_or_imprecise_dtypes=True).then_inc(iota_made, 1)
                    if by_dst:
                        nc.gpsimd.iota(tile_no[:, :], pattern=[[WINDOWS, W_BLOCKS]], base=0, channel_multiplier=1,
                                       allow_small_or_imprecise_dtypes=True).then_inc(iota_made, 1)

                if by_dst:
                    @block.scalar
                    def _(act):
                        act.wait_ge(deg_moved, 1)
                        act.activation(deg_t[:, :], bank[5][:, 0:NT], ACT.Sqrt).then_inc(deg_root, 1)

        def window_slots():
            with ExitStack() as ph:
                own = ph.enter_context(phase_semaphores(nc))
                sem = lambda n: own(f"window_{n}")
                tmp = lambda n, s, d=F32: ph.enter_context(nc.sbuf_tensor(f"window_{n}", s, d))
                rows_in, local, moved, kept = [sem(f"rows_in{m}") for m in range(2)], sem("local"), sem("moved"), sem("kept")
                edge_rows = [tmp(n, [WINDOWS, W_BLOCKS, P]) for n in ("src_rows", "key_rows")]
                PER_BANK = 4
                W_BANKS = -(-W_BLOCKS // PER_BANK)
                blocks_of = lambda n: range(n * PER_BANK, min(W_BLOCKS, (n + 1) * PER_BANK))
                block = ph.enter_context(nc.Block())

                @block.gpsimd
                def _(pool):
                    for m, table in enumerate((edge_src, edge_key)):
                        for b in range(W_BLOCKS):
                            nc.gpsimd.indirect_dma_start(edge_rows[m][:, b, :], None, table,
                                                         bass.IndirectOffsetOnAxis(ap=window_row[0:WINDOWS, b:b + 1], axis=0)).then_inc(rows_in[m], 16)

                @block.tensor
                def _(pe):
                    for m in range(2):
                        if m == 0:
                            pe.wait_ge(rows_in[0], 16 * W_BLOCKS)
                        else:
                            pe.wait_ge(local, 1)
                        for n in range(W_BANKS):
                            for b in blocks_of(n):
                                last = nc.tensor.transpose(bank[m * W_BANKS + n][:, (b % PER_BANK) * P:(b % PER_BANK) * P + WINDOWS],
                                                           edge_rows[m][:, b, :], ident[0:WINDOWS, 0:WINDOWS])
                            last.then_inc(moved, 1)

                @block.vector
                def _(dve):
                    def keep(m):
                        for n in range(W_BANKS):
                            dve.wait_ge(moved, m * W_BANKS + n + 1)
                            held = len(blocks_of(n))
                            field = d_slot[:, n * PER_BANK * WINDOWS:(n * PER_BANK + held) * WINDOWS, m:m + 1]
                            nc.vector.tensor_copy((field.bitcast(I32) if m == 0 else field).rearrange("p (b t) a -> p b (t a)", t=WINDOWS),
                                                  bank[m * W_BANKS + n][:, 0:held * P].rearrange("p (b t) -> p b t", t=P)[:, :, 0:WINDOWS]).then_inc(kept, 1)

                    keep(0)
                    dve.wait_ge(rows_in[1], 16 * W_BLOCKS)
                    nc.vector.tensor_tensor(edge_rows[1][:, :, :], edge_rows[1][:, :, :],
                                            window_node[0:WINDOWS, :].unsqueeze(2).to_broadcast([WINDOWS, W_BLOCKS, P]), ALU.subtract).then_inc(local, 1)
                    keep(1)

        def sort_destinations():
            @contextmanager
            def when_unsorted(eng):
                with eng.If(eng.value_load(unsorted[0:1, 0:1]) != 0):
                    yield

            with ExitStack() as ph:
                own = ph.enter_context(phase_semaphores(nc))
                work = Sort(lambda n: own(f"sort_d_{n}"),
                            lambda n, s, d=F32: ph.enter_context(nc.sbuf_tensor(f"sort_d_{n}", s, d)),
                            d_hi, d_lo, d_hi_bf, d_lo_kept, base_d, src_i, d_slots, D_FIELDS, False)
                block = ph.enter_context(nc.Block())

                @block.vector
                def _(dve):
                    def turn(i):
                        for k in range(TURN):
                            work.vector_step(dve, i, k)
                            work.vector_end_step(dve, i, k)

                    with when_unsorted(dve):
                        work.vector_start(dve)
                        turn(0)
                        with dve.Fori(1, E_TURNS) as i:
                            turn(i)

                @block.tensor
                def _(pe):
                    def turn(i):
                        for k in range(TURN):
                            work.tensor_step(pe, i, k)
                            work.tensor_end_step(pe, i, k)

                    with when_unsorted(pe):
                        work.tensor_start(pe)
                        turn(0)
                        with pe.Fori(1, E_TURNS) as i:
                            turn(i)

                @block.scalar
                def _(act):
                    def turn(i):
                        for k in range(TURN):
                            work.scalar_step(act, i, k)

                    with when_unsorted(act):
                        turn(0)
                        with act.Fori(1, E_TURNS) as i:
                            turn(i)

                @block.gpsimd
                def _(pool):
                    with when_unsorted(pool):
                        with pool.Fori(0, E_TURNS) as i:
                            for h in range(2):
                                work.scatter(pool, i, h)
                        work.scatter_end(pool)
                        pool.dma_start(d_slot, d_slots.rearrange("(p t) f -> p t f", p=P)).then_inc(work.slots_in, 16)
                        pool.wait_ge(work.slots_in, 16)

        NODE_RING = 4

        def by_ring(eng, body):
            whole_turns = NT // NODE_RING

            def turn(i):
                for b in range(NODE_RING):
                    if in_range(i * NODE_RING + b):
                        body(i * NODE_RING + b, b)

            turn(0)
            with eng.Fori(1, whole_turns - 1) as i:
                turn(i)
            for i in range(whole_turns - 1, -(-NT // NODE_RING)):
                turn(i)

        def in_range(n):
            return not isinstance(n, int) or n < NT

        def tile_of(rows, n):
            return rows[:, bass.ds(n, 1), :].rearrange("p a d -> p (a d)")

        def linear(name, w_sb, b_parts, table, normed):
            with ExitStack() as ph:
                own = ph.enter_context(phase_semaphores(nc))
                sem = lambda n: own(f"{name}_{n}")
                tmp = lambda n, s, d=F32: ph.enter_context(nc.sbuf_tensor(f"{name}_{n}", s, d))
                staged, moved, kept, made, scaled, stored, go = (sem(n) for n in ("staged", "moved", "kept", "made", "scaled", "stored", "go"))
                rows, rows_t = tmp("rows", [P, NODE_RING, D]), tmp("rows_t", [D, NODE_RING, P])
                block = ph.enter_context(nc.Block())

                @block.gpsimd
                def _(pool):
                    def stage(n, b):
                        need(pool, moved, n + 1 - NODE_RING)
                        pool.sem_inc(go, 1)
                        if normed:
                            nc.gpsimd.tensor_tensor(rows[:, b, :], tile_of(nodes, n), dinv[:, bass.ds(n, 1)].to_broadcast([P, D]), ALU.mult).then_inc(staged, 1)
                        else:
                            nc.gpsimd.tensor_copy(rows[:, b, :], tile_of(nodes, n)).then_inc(staged, 1)

                    by_ring(pool, stage)

                @block.vector
                def _(dve):
                    def step(n, b):
                        dve.wait_ge(made, n + 1)
                        nc.vector.tensor_scalar(tile_of(nodes, n), bank[4 + b][:, 0:D], dinv[:, bass.ds(n, 1)], None, ALU.mult).then_inc(scaled, 1)

                    by_ring(dve, step)

                @block.tensor
                def _(pe):
                    def transpose(n, b):
                        pe.wait_ge(staged, n + 1)
                        need(pe, kept, n + 1 - NODE_RING)
                        nc.tensor.transpose(bank[b][:, 0:P], rows[:, b, :], ident[:, :]).then_inc(moved, 1)

                    def step(n, b):
                        if in_range(n + 2):
                            transpose(n + 2, (b + 2) % NODE_RING)
                        pe.wait_ge(kept, n + 1)
                        need(pe, scaled, n + 1 - NODE_RING)
                        nc.tensor.matmul(bank[4 + b][:, 0:D], rows_t[:, b, :], w_sb[:, :], start=True, stop=False)
                        nc.tensor.matmul(bank[4 + b][:, 0:D], ones_bf[:, :], b_parts, start=False, stop=True).then_inc(made, 1)

                    for n in range(2):
                        transpose(n, n)
                    by_ring(pe, step)

                @block.scalar
                def _(act):
                    def step(n, b):
                        act.wait_ge(moved, n + 1)
                        need(act, made, n + 1 - NODE_RING)
                        if normed:
                            act.activation(rows_t[:, b, :], bank[b][:, 0:P], ACT.Relu, bias=bn_shift[:, 0:1],
                                           scale=bn_scale[:, 0:1]).then_inc(kept, 1)
                        else:
                            act.copy(rows_t[:, b, :], bank[b][:, 0:P]).then_inc(kept, 1)

                    by_ring(act, step)

                @block.sync
                def _(sp):
                    by_chunk = table.rearrange("(n p) d -> p n d", p=P)
                    with sp.Fori(0, N_CHUNKS) as j:
                        sp.wait_ge(scaled, j * CHUNK + CHUNK)
                        sp.dma_start(by_chunk[:, bass.ds(j * CHUNK, CHUNK), :], nodes[:, bass.ds(j * CHUNK, CHUNK), :]).then_inc(stored, 16)
                    sp.wait_ge(stored, 16 * N_CHUNKS)

        def sparse_product(name, table, nth, beside):
            with ExitStack() as ph:
                own = ph.enter_context(phase_semaphores(nc))
                sem = lambda n: own(f"{name}_{n}")
                tmp = lambda n, s, d=F32: ph.enter_context(nc.sbuf_tensor(f"{name}_{n}", s, d))
                work = beside(lambda n: own(f"{name}_beside_{n}"),
                              lambda n, s, d=F32: ph.enter_context(nc.sbuf_tensor(f"{name}_beside_{n}", s, d)))
                local_ready, index_ready, row_go = sem("local_ready"), sem("index_ready"), sem("row_go")
                row_hot_ready, summed, added = sem("row_hot_ready"), sem("summed"), sem("added")
                HOTS = 4
                sum_bank = [bank[6], bank[7]]
                index_ring = tmp("index_ring", [P, TURN], I32)
                fetched_rows = tmp("fetched_rows", [P, TURN, D])
                hot = tmp("hot", [P, HOTS, P])
                block = ph.enter_context(nc.Block())

                @block.scalar
                def _(act):
                    act.copy(lo_slots[:, 0:S_TILES], d_slot[:, :, 1:2].rearrange("p t a -> p (t a)")).then_inc(local_ready, 1)

                    def indices(i, h):
                        need(act, summed, i * TURN + (h - 1) * HALF)
                        act.copy(index_ring[:, h * HALF:(h + 1) * HALF],
                                 d_slot[:, bass.ds(i * TURN + h * HALF, HALF), 0:1].bitcast(I32).rearrange("p t a -> p (t a)")).then_inc(index_ready, 1)

                    def turn(i):
                        for k in range(TURN):
                            work.scalar_step(act, i, k)
                            if k == 1:
                                indices(i, 1)
                            if k == HALF + 1:
                                indices(i + 1, 0)

                    indices(0, 0)
                    turn(0)
                    with act.Fori(1, E_TURNS) as i:
                        turn(i)
                    with act.Fori(E_TURNS, S_TURNS - 1) as i:
                        indices(i, 1)
                        indices(i + 1, 0)

                @block.gpsimd
                def _(pool):
                    nc.gpsimd.memset(lo_slots[:, S_TILES:], EMPTY_KEY).then_inc(local_ready, 1)

                    def fetch(i, h, tiles=HALF):
                        pool.wait_ge(index_ready, 2 * i + h + 1)
                        pool.sem_inc(row_go, 1)
                        for k in range(h * HALF, h * HALF + tiles):
                            nc.gpsimd.indirect_dma_start(
                                fetched_rows[:, k, :], None, table,
                                bass.IndirectOffsetOnAxis(ap=index_ring[:, k:k + 1], axis=0)).then_inc(fetched[k], 16)

                    fetch(0, 0)
                    with pool.Fori(0, E_TURNS) as i:
                        fetch(i, 1)
                        if work.scatters:
                            work.scatter(pool, i, 0)
                        fetch(i + 1, 0)
                        if work.scatters:
                            work.scatter(pool, i, 1)
                    with pool.Fori(E_TURNS, S_TURNS - 2) as i:
                        fetch(i, 1)
                        fetch(i + 1, 0)
                    fetch(S_TURNS - 2, 1)
                    fetch(S_TURNS - 1, 0, LAST_TILES)
                    if work.scatters:
                        work.scatter_end(pool)

                @block.vector
                def _(dve):
                    dve.wait_ge(local_ready, 2)

                    def one_hot(t, k):
                        need(dve, summed, t + 1 - HOTS)
                        nc.vector.tensor_scalar(hot[:, k % HOTS, :], iota_bf[:, :], lo_slots[:, bass.ds(t, 1)], None,
                                                ALU.is_equal).then_inc(row_hot_ready, 1)

                    def turn(i, edges=True, tiles=TURN):
                        for h in range(-(-tiles // HALF)):
                            _, node = nc.values_load_multi_w_load_instructions(
                                node_d[0:1, bass.ds(i * TURN + h * HALF, HALF)], engines=[mybir.EngineType.DVE],
                                min_val=0, max_val=NT - 1, skip_runtime_bounds_check_because=CLAMPED)
                            for k in range(h * HALF, min(tiles, (h + 1) * HALF)):
                                t = i * TURN + k
                                if edges:
                                    work.vector_step(dve, i, k)
                                one_hot(t + 2, k + 2)
                                if edges:
                                    work.vector_end_step(dve, i, k)
                                dve.wait_ge(summed, t + 1)
                                need(dve, added, t)
                                here = tile_of(nodes, node[k % HALF])
                                nc.vector.tensor_tensor(here, here, sum_bank[k % 2][:, 0:D], ALU.add).then_inc(added, 1)

                    work.vector_start(dve)
                    for t in range(2):
                        one_hot(t, t)
                    turn(0)
                    with dve.Fori(1, E_TURNS) as i:
                        turn(i)
                    with dve.Fori(E_TURNS, S_TURNS - 1) as i:
                        turn(i, edges=False)
                    turn(S_TURNS - 1, edges=False, tiles=LAST_TILES)

                @block.tensor
                def _(pe):
                    def turn(i, edges=True, tiles=TURN):
                        for k in range(tiles):
                            t = i * TURN + k
                            if edges:
                                work.tensor_step(pe, i, k)
                            pe.wait_ge(row_hot_ready, t + 1)
                            need(pe, added, t - 1)
                            pe.wait_ge(fetched[k], (fetched_before(nth, k) + i + 1) * 16)
                            nc.tensor.matmul(sum_bank[k % 2][:, 0:D], hot[:, k % HOTS, :], fetched_rows[:, k, :],
                                             start=True, stop=True).then_inc(summed, 1)
                            if edges:
                                work.tensor_end_step(pe, i, k)

                    work.tensor_start(pe)
                    turn(0)
                    with pe.Fori(1, E_TURNS) as i:
                        turn(i)
                    work.tensor_end(pe)
                    with pe.Fori(E_TURNS, S_TURNS - 1) as i:
                        turn(i, edges=False)
                    turn(S_TURNS - 1, edges=False, tiles=LAST_TILES)

                @block.sync
                def _(sp):
                    work.sync(sp)

        count_destinations()
        early.close()
        find_bases("base_d", base_d, node_d, 0, True)
        window_slots()
        sort_destinations()
        linear("lin1", w1_sb, b1_parts, h_table[0], False)
        sparse_product("spmm1", h_table[0], 0, lambda sem, tmp: Count(sem, tmp, s_hi, s_lo, lead=2))
        find_bases("base_s", base_s, node_s, S_ROW, False)
        linear("lin2", w2_sb, b2_parts, h_table[1], True)
        sparse_product("spmm2", h_table[1], 1, lambda sem, tmp: Sort(
            sem, tmp, s_hi, s_lo, s_hi_bf, s_lo, base_s, dst_i, s_slots, S_FIELDS, True))

        class Norm:

            def __init__(self, name, sem, tmp, rows):
                self.rows = rows
                self.res_in = [sem(f"res_in{b}") for b in range(2)]
                self.summed, self.centred, self.squared, self.var_ready, self.rooted, self.normed, self.step, self.go = (
                    sem(n) for n in ("res_summed", "centred", "squared", "var_ready", "rooted", "normed", "norm_step", "norm_go"))
                self.res, self.sq = tmp("res", [P, 2, CHUNK, D]), tmp("sq", [P, 2, CHUNK, D])
                self.mean, self.rstd = tmp("mean", [P, 2, CHUNK]), tmp("rstd", [P, 2, CHUNK])

            def chunk(self, j):
                return self.rows[:, bass.ds(j * CHUNK, CHUNK), :]

            def load(self, sp, j, b, source):
                need(sp, self.centred, j - 1)
                sp.dma_start(self.res[:, b, :, :], source[:, bass.ds(j * CHUNK, CHUNK), :]).then_inc(self.res_in[b], 16)

            def gpsimd(self, pool, rows_ready):
                def add(j, b, loads):
                    rows_ready(j)
                    pool.wait_ge(self.res_in[b], loads * 16)
                    pool.sem_inc(self.go, 1)
                    nc.gpsimd.tensor_tensor(self.res[:, b, :, :], self.chunk(j), self.res[:, b, :, :], ALU.add).then_inc(self.summed, 1)

                turns = N_CHUNKS // 2
                with pool.Fori(0, turns - 1) as i:
                    for b in range(2):
                        add(i * 2 + b, b, i + 1)
                for b in range(2):
                    add((turns - 1) * 2 + b, b, turns)

            def vector(self, dve):
                v = nc.vector
                link = Chain(dve, self.step)
                over = lambda a: a.unsqueeze(2).to_broadcast([P, CHUNK, D])

                def centre(j, b):
                    here = self.chunk(j)
                    dve.wait_ge(self.summed, j + 1)
                    link(v.tensor_reduce(self.mean[:, b, :], self.res[:, b, :, :], AX.X, ALU.add))
                    link(v.tensor_scalar(self.mean[:, b, :], self.mean[:, b, :], 1.0 / D, None, ALU.mult))
                    v.tensor_tensor(here, self.res[:, b, :, :], over(self.mean[:, b, :]), ALU.subtract).then_inc(self.centred, 1)

                def scale(j, b):
                    here = self.chunk(j)
                    dve.wait_ge(self.squared, j + 1)
                    v.tensor_reduce(self.rstd[:, b, :], self.sq[:, b, :, :], AX.X, ALU.add).then_inc(self.var_ready, 1)
                    dve.wait_ge(self.rooted, j + 1)
                    link(v.reciprocal(self.rstd[:, b, :], self.rstd[:, b, :]))
                    v.tensor_tensor(here, here, over(self.rstd[:, b, :]), ALU.mult).then_inc(self.normed, 1)

                PER_TURN = 2 * 3
                turns = N_CHUNKS // 2

                def turn(i):
                    link.turn(2 + i * PER_TURN)
                    centre(i * 2 + 1, 1)
                    scale(i * 2, 0)
                    if not isinstance(i, int) or i < turns - 1:
                        centre(i * 2 + 2, 0)
                    scale(i * 2 + 1, 1)

                centre(0, 0)
                turn(0)
                with dve.Fori(1, turns - 1) as i:
                    turn(i)
                turn(turns - 1)

            def scalar(self, act):
                with act.Fori(0, N_CHUNKS // 2) as i:
                    for b in range(2):
                        j = i * 2 + b
                        act.wait_ge(self.centred, j + 1)
                        act.activation(self.sq[:, b, :, :], self.chunk(j), ACT.Square).then_inc(self.squared, 1)
                        act.wait_ge(self.var_ready, j + 1)
                        act.activation(self.rstd[:, b, :], self.rstd[:, b, :], ACT.Sqrt, bias=eps_col[:, 0:1], scale=1.0 / D).then_inc(self.rooted, 1)

        with ExitStack() as ph:
            own = ph.enter_context(phase_semaphores(nc))
            sem = lambda n: own(f"qkv_{n}")
            tmp = lambda n, s, d=F32: ph.enter_context(nc.sbuf_tensor(f"qkv_{n}", s, d))
            norm = Norm("qkv", sem, tmp, nodes)
            x1_out, tail_in = sem("x1_out"), sem("tail_in")
            kv_out = [sem(f"kv_out{b}") for b in range(NODE_RING)]
            weighed, staged, moved, kept, made, q_done, kv_done = (
                sem(n) for n in ("weighed", "staged", "moved", "kept", "made", "q_done", "kv_done"))
            rows, rows_t = tmp("rows", [P, NODE_RING, D]), tmp("rows_t", [D, NODE_RING, P])
            kv_rows = tmp("kv_rows", [P, NODE_RING, 2 * D])
            block = ph.enter_context(nc.Block())

            @block.sync
            def _(sp):
                x_tiles = x[0:(NT - 1) * P, :].rearrange("(n p) d -> p n d", p=P)
                for b in range(2):
                    norm.load(sp, b, b, x_tiles)
                with sp.Fori(1, N_CHUNKS // 2 - 1) as i:
                    for b in range(2):
                        norm.load(sp, i * 2 + b, b, x_tiles)
                norm.load(sp, N_CHUNKS - 2, 0, x_tiles)
                last = (N_CHUNKS - 1) * CHUNK
                sp.wait_ge(norm.centred, N_CHUNKS - 2)
                sp.dma_start(norm.res[:, 1, 0:CHUNK - 1, :], x_tiles[:, last:NT - 1, :]).then_inc(norm.res_in[1], 16)
                sp.dma_start(norm.res[0:LAST_ROWS, 1, CHUNK - 1, :], x[(NT - 1) * P:N_NODES, :]).then_inc(tail_in, 16)

                def store(n, b):
                    sp.wait_ge(kv_done, n + 1)
                    sp.dma_start(kv_table[bass.ds(n * P, P), :], kv_rows[:, b, :]).then_inc(kv_out[b], 16)

                by_ring(sp, store)
                for b in range(NODE_RING):
                    sp.wait_ge(kv_out[b], 16 * len(range(b, NT, NODE_RING)))

            @block.gpsimd
            def _(pool):
                def rows_ready(j):
                    nc.gpsimd.tensor_tensor(norm.chunk(j), norm.chunk(j),
                                            dinv[:, bass.ds(j * CHUNK, CHUNK)].unsqueeze(2).to_broadcast([P, CHUNK, D]), ALU.mult).then_inc(weighed, 1)
                    pool.wait_ge(weighed, j + 1)
                    if isinstance(j, int) and j == N_CHUNKS - 1:
                        pool.wait_ge(tail_in, 16)

                norm.gpsimd(pool, rows_ready)

                def stage(n, b):
                    need(pool, moved, n + 1 - NODE_RING)
                    nc.gpsimd.tensor_copy(rows[:, b, :], tile_of(nodes, n)).then_inc(staged, 1)

                with pool.Fori(0, N_CHUNKS) as j:
                    pool.wait_ge(norm.normed, j + 1)
                    pool.dma_start(x1_dram.rearrange("(n p) d -> p n d", p=P)[:, bass.ds(j * CHUNK, CHUNK), :], norm.chunk(j)).then_inc(x1_out, 16)
                by_ring(pool, stage)

            @block.vector
            def _(dve):
                v = nc.vector

                norm.vector(dve)

                def step(n, b):
                    dve.wait_ge(made, n + 1)
                    v.scalar_tensor_tensor(tile_of(nodes, n), bank[4 + b][:, 0:D], HEAD_DIM ** -0.5, qkv_bc[:, 0:D], ALU.mult, ALU.add).then_inc(q_done, 1)
                    need(dve, kv_out[b], (n - b) * (16 // NODE_RING))
                    v.tensor_tensor(kv_rows[:, b, :], bank[4 + b][:, D:3 * D], qkv_bc[:, D:3 * D], ALU.add).then_inc(kv_done, 1)

                dve.wait_ge(x1_out, 16 * N_CHUNKS)
                by_ring(dve, step)

            @block.scalar
            def _(act):
                norm.scalar(act)

                def keep(n, b):
                    act.wait_ge(moved, n + 1)
                    need(act, made, n + 1 - NODE_RING)
                    act.copy(rows_t[:, b, :], bank[b][:, 0:P]).then_inc(kept, 1)

                by_ring(act, keep)

            @block.tensor
            def _(pe):
                def transpose(n, b):
                    pe.wait_ge(staged, n + 1)
                    need(pe, kept, n + 1 - NODE_RING)
                    nc.tensor.transpose(bank[b][:, 0:P], rows[:, b, :], ident[:, :]).then_inc(moved, 1)

                def step(n, b):
                    if in_range(n + 2):
                        transpose(n + 2, (b + 2) % NODE_RING)
                    pe.wait_ge(kept, n + 1)
                    need(pe, kv_done, n + 1 - NODE_RING)
                    nc.tensor.matmul(bank[4 + b][:, 0:3 * D], rows_t[:, b, :], qkv_t[:, :], start=True, stop=True).then_inc(made, 1)

                for n in range(2):
                    transpose(n, n)
                by_ring(pe, step)

        GROUP = 4
        GROUPS = TURN // GROUP
        with ExitStack() as ph:
            own = ph.enter_context(phase_semaphores(nc))
            sem = lambda n: own(f"score_{n}")
            tmp = lambda n, s, d=F32: ph.enter_context(nc.sbuf_tensor(f"score_{n}", s, d))
            PIECES = 4
            slots_in = [sem("first_slots_in"), sem("other_slots_in")]
            local_ready, index_ready, go = sem("local_ready"), sem("index_ready"), sem("go")
            spread, hot_ready, q_ready, product, reduced, scored = (
                sem(n) for n in ("spread", "hot_ready", "q_ready", "product", "reduced", "scored"))
            v_out = [sem(f"v_out{h}") for h in range(2)]
            index_ring = tmp("index_ring", [P, TURN], I32)
            kv_rows = tmp("kv_rows", [P, TURN, 2 * D])
            hot_t = tmp("hot_t", [P, 2, GROUP * P])
            qk = tmp("qk", [P, GROUP * D])
            part_scores = tmp("part_scores", [P, GROUP, HEADS])
            block = ph.enter_context(nc.Block())

            @block.sync
            def _(sp):
                for n in range(PIECES):
                    some = slice(n * S_TILES // PIECES, (n + 1) * S_TILES // PIECES)
                    sp.dma_start(s_slot[:, some, :], s_slots.rearrange("(p t) f -> p t f", p=P)[:, some, :]).then_inc(slots_in[min(n, 1)], 16)
                with sp.Fori(0, S_TURNS) as i:
                    for h in range(2):
                        for k in range(h * HALF, (h + 1) * HALF):
                            sp.wait_ge(fetched[k], (fetched_before(2, k) + i + 1) * 16)
                        sp.dma_start(v_sorted[:, bass.ds(i * TURN + h * HALF, HALF), :],
                                     kv_rows[:, h * HALF:(h + 1) * HALF, D:2 * D]).then_inc(v_out[h], 16)
                for h in range(2):
                    sp.wait_ge(v_out[h], 16 * S_TURNS)

            @block.scalar
            def _(act):
                def turn(i):
                    for h in range(2):
                        need(act, product, (i - 1) * GROUPS + (h + 1) * (GROUPS // 2))
                        need(act, v_out[h], i * 16)
                        act.copy(index_ring[:, h * HALF:(h + 1) * HALF],
                                 s_slot[:, bass.ds(i * TURN + h * HALF, HALF), 0:1].bitcast(I32).rearrange("p t a -> p (t a)")).then_inc(index_ready, 1)

                act.wait_ge(slots_in[0], 16)
                turn(0)
                act.wait_ge(slots_in[1], 16 * (PIECES - 1))
                lo = s_slot[:, :, 1:2].rearrange("p t a -> p (t a)")
                act.copy(lo_slots_bf[:, 0:S_TILES], lo).then_inc(local_ready, 1)
                act.copy(lo_slots[:, 0:S_TILES], lo).then_inc(local_ready, 1)
                with act.Fori(1, S_TURNS) as i:
                    turn(i)

            @block.gpsimd
            def _(pool):
                nc.gpsimd.memset(lo_slots_bf[:, S_TILES:], EMPTY_KEY).then_inc(local_ready, 1)
                with pool.Fori(0, S_TURNS) as i:
                    for h in range(2):
                        pool.wait_ge(index_ready, 2 * i + h + 1)
                        pool.sem_inc(go, 1)
                        for k in range(h * HALF, (h + 1) * HALF):
                            nc.gpsimd.indirect_dma_start(
                                kv_rows[:, k, :], None, kv_table,
                                bass.IndirectOffsetOnAxis(ap=index_ring[:, k:k + 1], axis=0)).then_inc(fetched[k], 16)

            @block.tensor
            def _(pe):
                pe.wait_ge(local_ready, 3)

                def spread_keys(g, b, t0):
                    need(pe, hot_ready, g - 1)
                    for m in range(GROUP):
                        last = nc.tensor.matmul(bank[b][:, m * P:(m + 1) * P], lo_slots_bf[:, bass.ds(t0 + m, 1)].to_broadcast([P, P]),
                                                ident_bf[:, :], start=True, stop=True)
                    last.then_inc(spread, 1)

                def turn(i):
                    for j in range(GROUPS):
                        g = i * GROUPS + j
                        spread_keys(g + 1, (j + 1) % 2, i * TURN + (j + 1) * GROUP)
                        _, node = nc.values_load_multi_w_load_instructions(
                            node_s[0:1, bass.ds(i * TURN + j * GROUP, GROUP)], engines=[mybir.EngineType.PE],
                            min_val=0, max_val=NT - 1, skip_runtime_bounds_check_because=CLAMPED)
                        pe.wait_ge(hot_ready, g + 1)
                        need(pe, product, g - 1)
                        for m in range(GROUP):
                            last = nc.tensor.matmul(bank[2 + j % 2][:, m * D:(m + 1) * D], hot_t[:, j % 2, m * P:(m + 1) * P],
                                                    nodes[:, bass.ds(node[m], 1), :].rearrange("p a d -> p (a d)"), start=True, stop=True)
                        last.then_inc(q_ready, 1)

                spread_keys(0, 0, 0)
                turn(0)
                with pe.Fori(1, S_TURNS) as i:
                    turn(i)

            @block.vector
            def _(dve):
                v = nc.vector

                def one_hots(g, b):
                    dve.wait_ge(spread, g + 1)
                    need(dve, q_ready, g - 1)
                    v.tensor_scalar(hot_t[:, b, :], bank[b][:, :], iota_p[:, 0:1], None, ALU.is_equal).then_inc(hot_ready, 1)

                def turn(i):
                    for j in range(GROUPS):
                        g = i * GROUPS + j
                        one_hots(g + 1, (j + 1) % 2)
                        for k in range(j * GROUP, (j + 1) * GROUP):
                            dve.wait_ge(fetched[k], (fetched_before(2, k) + i + 1) * 16)
                        dve.wait_ge(q_ready, g + 1)
                        need(dve, reduced, g)
                        v.tensor_tensor(qk[:, :].rearrange("p (m d) -> p m d", d=D), bank[2 + j % 2][:, :].rearrange("p (m d) -> p m d", d=D),
                                        kv_rows[:, j * GROUP:(j + 1) * GROUP, 0:D], ALU.mult).then_inc(product, 1)
                        dve.wait_ge(product, g + 1)
                        need(dve, scored, g)
                        v.tensor_reduce(part_scores[:, :, :].rearrange("p m h -> p (m h)"),
                                        qk[:, :].rearrange("p (m d) -> p m d", d=HEAD_DIM), AX.X, ALU.add).then_inc(reduced, 1)
                        dve.wait_ge(reduced, g + 1)
                        biased = s_slot[:, bass.ds(i * TURN + j * GROUP, GROUP), 2:S_FIELDS]
                        v.tensor_tensor(biased, biased, part_scores[:, :, :], ALU.add).then_inc(scored, 1)

                dve.wait_ge(slots_in[0], 16)
                dve.wait_ge(slots_in[1], 16 * (PIECES - 1))
                one_hots(0, 0)
                turn(0)
                with dve.Fori(1, S_TURNS) as i:
                    turn(i)

        with ExitStack() as ph:
            own = ph.enter_context(phase_semaphores(nc))
            sem = lambda n: own(f"soft_{n}")
            tmp = lambda n, s, d=F32: ph.enter_context(nc.sbuf_tensor(f"soft_{n}", s, d))
            step, key_ready, prev_ready = sem("step"), sem("key_ready"), sem("prev_ready")
            staged, moved, kept_s, kept_b = sem("staged"), sem("moved"), sem("kept_s"), sem("kept_b")
            b_staged, ends_ready, rows_ready, carry_ready, carried = (
                sem(n) for n in ("b_staged", "ends_ready", "rows_ready", "carry_ready", "carried"))
            shifted, exped, w_moved, w_kept = sem("shifted"), sem("exped"), sem("w_moved"), sem("w_kept")
            QUARTER = S_TILES // 4
            key = tmp("key", [P, S_TILES + 1])
            new_seg = tmp("new_seg", [P, S_TILES])
            TRIO = 3
            TRIOS = CHUNK_TILES // TRIO
            T3 = TRIO * P
            assert TRIOS * TRIO == CHUNK_TILES and TRIOS % 2 == 1
            s_stage, b_stage = tmp("s_stage", [P, 2, T3]), tmp("b_stage", [P, 2, T3])
            as_tch = lambda rows: rows.rearrange("p (t c h) -> p t c h", t=TRIO, h=HEADS)

            def by_trios(eng, body):
                def turn(i):
                    for b in range(2):
                        body(i * 2 + b, b)

                turn(0)
                with eng.Fori(1, TRIOS // 2) as i:
                    turn(i)
                body(TRIOS - 1, 0)

            ends = tmp("ends", [P, 6])
            carry_row = tmp("carry_row", [1, 6, P])
            carry_out = tmp("carry_out", [1, 2, P + HEADS])
            carry = tmp("carry", [P, 2])
            chunk_key = new_seg[:, :].rearrange("p (c t) -> p c t", c=CHUNKS)
            chunk_scores = s_slot.rearrange("p (c t) f -> p c t f", c=CHUNKS)
            QUARTERS = 4
            PIECE = CHUNK_LEN // QUARTERS
            block = ph.enter_context(nc.Block())

            @block.vector
            def _(dve):
                v = nc.vector
                link = Chain(dve, step)
                link(v.memset(key[:, 0:1], -float(P)))
                v.scalar_tensor_tensor(key[:, 1:], node_s_bc[:, :], float(P), lo_slots[:, 0:S_TILES], ALU.mult, ALU.add).then_inc(key_ready, 1)
                dve.wait_ge(key_ready, 1)
                dve.wait_ge(prev_ready, 1)
                for j in range(4):
                    cut = slice(j * QUARTER, (j + 1) * QUARTER)
                    link(v.tensor_tensor(new_seg[:, cut], bank[4 + j][:, 0:QUARTER], key[:, 1 + j * QUARTER:1 + (j + 1) * QUARTER], ALU.not_equal))
                link(v.tensor_scalar(new_seg[:, :], new_seg[:, :], BREAK, None, ALU.mult))

                def stage(g, b):
                    need(dve, moved, g - 1)
                    v.tensor_copy(as_tch(b_stage[:, b, :]), chunk_key[:, :, bass.ds(g * TRIO, TRIO)].rearrange("p c t -> p t c").unsqueeze(3)
                                  .to_broadcast([P, TRIO, CHUNKS, HEADS])).then_inc(b_staged, 1)

                def keep(g, b):
                    if not (isinstance(g, int) and g == TRIOS - 1):
                        stage(g + 1, 1 - b)
                    dve.wait_ge(moved, g + 1)
                    v.tensor_copy(breaks[:, bass.ds(g * T3, T3)], bank[2 + b][:, 0:T3]).then_inc(kept_b, 1)

                stage(0, 0)
                by_trios(dve, keep)
                dve.wait_ge(kept_b, TRIOS)
                dve.wait_ge(kept_s, TRIOS)
                link(v.memset(breaks[:, CHUNK_LEN:], 0.0))
                body, back = breaks[:, 0:CHUNK_LEN], breaks[:, 1:CHUNK_LEN + 1]
                link(v.tensor_reduce(ends[:, 0:1], body, AX.X, ALU.add))
                link(v.tensor_copy(ends[:, 2:3], breaks[:, 0:1]))
                link(v.tensor_tensor(ends[:, 1:2], ends[:, 0:1], ends[:, 2:3], ALU.subtract))
                link(v.tensor_tensor_scan(seg_max, body, scores_t, BREAK, ALU.add, ALU.max))
                link(v.tensor_copy(ends[:, 3:4], seg_max[:, CHUNK_LEN - 1:CHUNK_LEN]))
                link(v.tensor_tensor_scan(seg_max[:, ::-1], back[:, ::-1], scores_t[:, ::-1], BREAK, ALU.add, ALU.max))
                v.tensor_copy(ends[:, 4:5], seg_max[:, 0:1]).then_inc(ends_ready, 1)
                dve.wait_ge(rows_ready, 1)
                dve.wait_ge(ends_ready, 1)
                link(v.tensor_copy(carry_row[:, 0:4, :].rearrange("p a b -> p (a b)"), bank[0][0:1, 0:4 * P]))
                link(v.tensor_copy(carry_row[:, 4, :], bank[1][0:1, 0:P]))
                link(v.memset(carry_out[:, :, :], BREAK))
                by_head = carry_row[:, :, :].rearrange("p a (c h) -> p a h c", h=HEADS)
                into = carry_out[:, :, :].rearrange("p a (c h) -> p a h c", h=HEADS)
                link(v.tensor_tensor(carry_row[:, 1, :], carry_row[:, 1, :], carry_row[:, 2, :], ALU.add))
                link(v.tensor_tensor(carry_row[:, 4, :], carry_row[:, 4, :], carry_row[:, 2, :], ALU.add))
                for h in range(HEADS):
                    v.tensor_tensor_scan(into[:, 0, h, 1:], by_head[:, 0, h, :], by_head[:, 3, h, :], BREAK, ALU.add, ALU.max)
                    link(v.tensor_tensor_scan(into[:, 1, h, 0:CHUNKS][:, ::-1], by_head[:, 1, h, ::-1], by_head[:, 4, h, ::-1],
                                              BREAK, ALU.add, ALU.max))
                v.tensor_copy(carry_row[:, 5, :], carry_row[:, 4, :]).then_inc(carry_ready, 1)
                dve.wait_ge(carried, 1)
                link(v.tensor_copy(carry[:, :], bank[2][:, 0:2]))
                link(v.tensor_tensor_scan(seg_max, body, scores_t, carry[:, 0:1], ALU.add, ALU.max))
                link(v.tensor_tensor_scan(seg_max[:, ::-1], back[:, ::-1], seg_max[:, ::-1], carry[:, 1:2], ALU.add, ALU.max))
                for j in range(QUARTERS):
                    cut = slice(j * PIECE, (j + 1) * PIECE)
                    v.tensor_tensor(scores_t[:, cut], scores_t[:, cut], seg_max[:, cut], ALU.subtract).then_inc(shifted, 1)

                dve.wait_ge(shifted, QUARTERS)

                def keep_weights(g, b):
                    dve.wait_ge(w_moved, g + 1)
                    v.tensor_copy(weights.rearrange("p (c t) h -> p t c h", c=CHUNKS)[:, bass.ds(g * TRIO, TRIO), :, :],
                                  as_tch(bank[4 + b][:, 0:T3])).then_inc(w_kept, 1)

                by_trios(dve, keep_weights)

            @block.tensor
            def _(pe):
                t = nc.tensor
                pe.wait_ge(key_ready, 1)
                for j in range(4):
                    t.matmul(bank[4 + j][:, 0:QUARTER], next_row[:, :], key[:, 1 + j * QUARTER:1 + (j + 1) * QUARTER], start=True, stop=False)
                    last = t.matmul(bank[4 + j][:, 0:QUARTER], wrap_row[:, :], key[:, j * QUARTER:(j + 1) * QUARTER], start=False, stop=True)
                last.then_inc(prev_ready, 1)

                def move(g, b):
                    need(pe, kept_s, g - 1)
                    pe.wait_ge(staged, g + 1)
                    for m in range(TRIO):
                        t.transpose(bank[b][:, m * P:(m + 1) * P], s_stage[:, b, m * P:(m + 1) * P], ident[:, :])
                    need(pe, kept_b, g - 1)
                    pe.wait_ge(b_staged, g + 1)
                    for m in range(TRIO):
                        last = t.transpose(bank[2 + b][:, m * P:(m + 1) * P], b_stage[:, b, m * P:(m + 1) * P], ident[:, :])
                    last.then_inc(moved, 1)

                by_trios(pe, move)
                pe.wait_ge(ends_ready, 1)
                for n in range(5):
                    last = t.matmul(bank[n // 4][0:1, (n % 4) * P:(n % 4 + 1) * P], ends[:, n:n + 1], ident[:, :], start=True, stop=True)
                last.then_inc(rows_ready, 1)
                pe.wait_ge(carry_ready, 1)
                t.matmul(bank[2][:, 0:1], carry_out[0:1, 0, 0:P], ones[0:1, 0:1], start=True, stop=True)
                t.matmul(bank[2][:, 1:2], carry_out[0:1, 1, HEADS:P + HEADS], ones[0:1, 0:1], start=True, stop=True).then_inc(carried, 1)

                def move_back(g, b):
                    pe.wait_ge(exped, g + 1)
                    need(pe, w_kept, g - 1)
                    for m in range(TRIO):
                        last = t.transpose(bank[4 + b][:, m * P:(m + 1) * P], s_stage[:, b, m * P:(m + 1) * P], ident[:, :])
                    last.then_inc(w_moved, 1)

                by_trios(pe, move_back)

            @block.scalar
            def _(act):
                def stage(g, b):
                    need(act, moved, g - 1)
                    act.copy(as_tch(s_stage[:, b, :]),
                             chunk_scores[:, :, bass.ds(g * TRIO, TRIO), 2:S_FIELDS].rearrange("p c t h -> p t c h")).then_inc(staged, 1)

                def keep(g, b):
                    if not (isinstance(g, int) and g == TRIOS - 1):
                        stage(g + 1, 1 - b)
                    act.wait_ge(moved, g + 1)
                    act.copy(scores_t[:, bass.ds(g * T3, T3)], bank[b][:, 0:T3]).then_inc(kept_s, 1)

                stage(0, 0)
                by_trios(act, keep)
                act.wait_ge(shifted, QUARTERS)

                def exps(g, b):
                    need(act, w_moved, g - 1)
                    act.activation(s_stage[:, b, :], scores_t[:, bass.ds(g * T3, T3)], ACT.Exp).then_inc(exped, 1)

                by_trios(act, exps)

        STREAM = S_TILES // 2
        with ExitStack() as ph:
            own = ph.enter_context(phase_semaphores(nc))
            sem = lambda n: own(f"mix_{n}")
            tmp = lambda n, s, d=F32: ph.enter_context(nc.sbuf_tensor(f"mix_{n}", s, d))
            cleared, hot_ready, apart, near_ready, weighted, joined, summed, added, step = (
                sem(n) for n in ("cleared", "hot_ready", "apart", "near_ready", "weighted", "joined", "summed", "added", "step"))
            v_in = [sem(f"v_in{j}") for j in range(GROUPS)]
            RING = 8
            SHARE = 3
            W = D + HEADS
            v_rows = tmp("v_rows", [P, GROUPS, GROUP, D])
            mixed = tmp("mixed", [P, GROUPS, GROUP, W])
            hot = tmp("hot", [P, GROUPS, GROUP, P])
            ends = tmp("ends", [P, 2])
            places = tmp("places", [1, S_TURNS, 2, GROUP, 2], I32)
            block = ph.enter_context(nc.Block())

            def tiles_of(i, j):
                return bass.ds(i * HALF + j // 2 * GROUP + j % 2 * STREAM, GROUP)

            def half_summed(i, j):
                return (i - 1) * TURN + (j // 2 + 1) * HALF

            @block.sync
            def _(sp):
                def turn(i):
                    for j in range(GROUPS):
                        need(sp, weighted, (i - 1) * GROUPS + j + 1)
                        sp.dma_start(v_rows[:, j, :, :], v_sorted[:, tiles_of(i, j), :]).then_inc(v_in[j], 16)

                turn(0)
                with sp.Fori(1, S_TURNS) as i:
                    turn(i)

            @block.gpsimd
            def _(pool):
                def turn(i):
                    for j in range(GROUPS):
                        pool.wait_ge(v_in[j], i * 16 + 16)
                        need(pool, summed, half_summed(i, j))
                        nc.gpsimd.tensor_tensor(
                            mixed[:, j, :, 0:D].rearrange("p m (h d) -> p m h d", d=HEAD_DIM),
                            v_rows[:, j, :, :].rearrange("p m (h d) -> p m h d", d=HEAD_DIM),
                            weights[:, tiles_of(i, j), :].unsqueeze(3).to_broadcast([P, GROUP, HEADS, HEAD_DIM]), ALU.mult).then_inc(weighted, 1)

                turn(0)
                with pool.Fori(1, S_TURNS) as i:
                    turn(i)

            @block.scalar
            def _(act):
                def turn(i):
                    for j in range(GROUPS):
                        need(act, summed, half_summed(i, j))
                        for m in range(0 if j % 2 else SHARE, GROUP):
                            act.activation(hot[:, j, m, :], iota_bf[:, :], ACT.Abs,
                                           bias=lo_slots[:, bass.ds(i * HALF + j // 2 * GROUP + j % 2 * STREAM + m, 1)], scale=-1.0).then_inc(apart, 1)
                        per_pair = GROUP - SHARE + GROUP
                        act.wait_ge(apart, (i * 2 + j // 2) * per_pair + (per_pair if j % 2 else GROUP - SHARE))
                        mine = hot[:, j, (0 if j % 2 else SHARE):GROUP, :]
                        act.activation(mine, mine, ACT.Relu, bias=ones[:, 0:1], scale=-1.0).then_inc(near_ready, 1)
                        act.copy(mixed[:, j, :, D:W], weights[:, tiles_of(i, j), :]).then_inc(joined, 1)

                turn(0)
                with act.Fori(1, S_TURNS) as i:
                    turn(i)

            @block.vector
            def _(dve):
                v = nc.vector
                link = Chain(dve, step)
                v.memset(sums, 0.0).then_inc(cleared, 1)
                for stream in range(2):
                    link(v.tensor_scalar(places[:, :, :, :, stream],
                                         node_s[0:1, stream * STREAM:(stream + 1) * STREAM].rearrange("p (i h m) -> p i h m", h=2, m=GROUP),
                                         float(stream), None, ALU.add))
                dve.wait_ge(cleared, 1)

                def one_hots(i, j):
                    need(dve, summed, half_summed(i, j))
                    v.tensor_tensor(hot[:, j, 0:SHARE, :], iota_bf[:, :].unsqueeze(1).to_broadcast([P, SHARE, P]),
                                    lo_slots[:, bass.ds(i * HALF + j // 2 * GROUP, SHARE)].unsqueeze(2).to_broadcast([P, SHARE, P]),
                                    ALU.is_equal).then_inc(hot_ready, 1)

                def turn(i, last=False):
                    _, place = nc.values_load_multi_w_load_instructions(
                        places[:, bass.ds(i, 1), :, :, :].rearrange("p i h m s -> p (i h m s)"), engines=[mybir.EngineType.DVE],
                        min_val=0, max_val=NT, skip_runtime_bounds_check_because=CLAMPED)
                    for h in range(2):
                        for k in range(HALF):
                            done = i * TURN + h * HALF + k
                            if k == 0 and not (last and h == 1):
                                one_hots(i + h, 2 * (1 - h))
                            dve.wait_ge(summed, done + 1)
                            need(dve, added, done - 1)
                            here = tile_of(sums, place[h * HALF + k])
                            v.tensor_tensor(here, here, bank[k][:, 0:W], ALU.add).then_inc(added, 1)

                one_hots(0, 0)
                turn(0)
                with dve.Fori(1, S_TURNS - 1) as i:
                    turn(i)
                turn(S_TURNS - 1, last=True)
                _, meet = nc.values_load_multi_w_load_instructions(
                    node_s[0:1, STREAM - 1:STREAM + 1], engines=[mybir.EngineType.DVE],
                    min_val=0, max_val=NT - 1, skip_runtime_bounds_check_because=CLAMPED)
                link(v.tensor_copy(ends[:, :], node_s_bc[:, STREAM - 1:STREAM + 1]))
                link(v.tensor_tensor(ends[:, 1:2], ends[:, 0:1], ends[:, 1:2], ALU.is_equal))
                dve.wait_ge(added, S_TILES)
                here = tile_of(sums, meet[0])
                link(v.scalar_tensor_tensor(here, tile_of(sums, meet[1] + 1), ends[:, 1:2], here, ALU.mult, ALU.add))
                link(v.tensor_scalar(sum_place[:, :], iota_bf[0:1, 0:NT], ends[0:1, 0:1], None, ALU.is_gt))
                link(v.tensor_tensor(sum_place[:, :], sum_place[:, :], iota_bf[0:1, 0:NT], ALU.add))

            @block.tensor
            def _(pe):
                def turn(i):
                    for k in range(TURN):
                        t, j, m = i * TURN + k, k // HALF * 2 + k % 2, k % HALF // 2
                        if m == 0:
                            pe.wait_ge(weighted, i * GROUPS + j + 1)
                            pe.wait_ge(joined, i * GROUPS + j + 1)
                            pe.wait_ge(near_ready, i * GROUPS + j + 1)
                            if j % 2 == 0:
                                pe.wait_ge(hot_ready, i * 2 + j // 2 + 1)
                        need(pe, added, t + 1 - RING)
                        nc.tensor.matmul(bank[k % RING][:, 0:W], hot[:, j, m, :], mixed[:, j, m, :], start=True, stop=True).then_inc(summed, 1)

                turn(0)
                with pe.Fori(1, S_TURNS) as i:
                    turn(i)

        with ExitStack() as ph:
            own = ph.enter_context(phase_semaphores(nc))
            sem = lambda n: own(f"fin_{n}")
            tmp = lambda n, s, d=F32: ph.enter_context(nc.sbuf_tensor(f"fin_{n}", s, d))
            rec_step, staged, moved, kept, made, projected, stored = (
                sem(n) for n in ("rec_step", "staged", "moved", "kept", "made", "projected", "stored"))
            rec = tmp("rec", [P, NT + 1, HEADS])
            rows, rows_t = tmp("rows", [P, NODE_RING, D]), tmp("rows_t", [D, NODE_RING, P])
            final = sums[:, 0:NT, 0:D]
            norm = Norm("fin", sem, tmp, final)
            block = ph.enter_context(nc.Block())

            @block.sync
            def _(sp):
                x1_tiles = x1_dram.rearrange("(n p) d -> p n d", p=P)
                for b in range(2):
                    norm.load(sp, b, b, x1_tiles)
                with sp.Fori(1, N_CHUNKS // 2) as i:
                    for b in range(2):
                        norm.load(sp, i * 2 + b, b, x1_tiles)

            @block.scalar
            def _(act):
                def keep(n, b):
                    act.wait_ge(moved, n + 1)
                    need(act, made, n + 1 - NODE_RING)
                    act.copy(rows_t[:, b, :], bank[b][:, 0:P]).then_inc(kept, 1)

                by_ring(act, keep)
                norm.scalar(act)

            @block.gpsimd
            def _(pool):
                def stage(n, b):
                    if b == 0:
                        count = NODE_RING if not isinstance(n, int) else min(NODE_RING, NT - n)
                        _, place[:] = nc.values_load_multi_w_load_instructions(
                            sum_place[0:1, bass.ds(n, count)], engines=[mybir.EngineType.Pool],
                            min_val=0, max_val=NT, skip_runtime_bounds_check_because="a node tile's number, or one more")
                    need(pool, moved, n + 1 - NODE_RING)
                    nc.gpsimd.tensor_tensor(rows[:, b, :].rearrange("p (h d) -> p h d", d=HEAD_DIM),
                                            tile_of(sums, place[b])[:, 0:D].rearrange("p (h d) -> p h d", d=HEAD_DIM),
                                            tile_of(rec, place[b]).unsqueeze(2).to_broadcast([P, HEADS, HEAD_DIM]), ALU.mult).then_inc(staged, 1)

                place = []
                pool.wait_ge(rec_step, 2)
                by_ring(pool, stage)
                norm.gpsimd(pool, lambda j: pool.wait_ge(projected, j * CHUNK + CHUNK))
                out_tiles = out[0:(NT - 1) * P, :].rearrange("(n p) d -> p n d", p=P)
                with pool.Fori(0, N_CHUNKS - 1) as j:
                    pool.wait_ge(norm.normed, j + 1)
                    pool.dma_start(out_tiles[:, bass.ds(j * CHUNK, CHUNK), :], norm.chunk(j)).then_inc(stored, 16)
                pool.wait_ge(norm.normed, N_CHUNKS)
                pool.dma_start(out_tiles[:, (N_CHUNKS - 1) * CHUNK:NT - 1, :], final[:, (N_CHUNKS - 1) * CHUNK:NT - 1, :]).then_inc(stored, 16)
                pool.dma_start(out[(NT - 1) * P:N_NODES, :], final[0:LAST_ROWS, NT - 1, :]).then_inc(stored, 16)
                pool.wait_ge(stored, 16 * (N_CHUNKS + 1))

            @block.vector
            def _(dve):
                v = nc.vector
                v.tensor_scalar(rec[:, :, :], sums[:, :, D:D + HEADS], SUM_EPS, None, ALU.add).then_inc(rec_step, 1)
                dve.wait_ge(rec_step, 1)
                v.reciprocal(rec[:, :, :], rec[:, :, :]).then_inc(rec_step, 1)

                def keep(n, b):
                    dve.wait_ge(made, n + 1)
                    v.tensor_copy(tile_of(final, n), bank[4 + b][:, 0:D]).then_inc(projected, 1)

                by_ring(dve, keep)
                norm.vector(dve)

            @block.tensor
            def _(pe):
                def transpose(n, b):
                    pe.wait_ge(staged, n + 1)
                    need(pe, kept, n + 1 - NODE_RING)
                    nc.tensor.transpose(bank[b][:, 0:P], rows[:, b, :], ident[:, :]).then_inc(moved, 1)

                def step(n, b):
                    if in_range(n + 2):
                        transpose(n + 2, (b + 2) % NODE_RING)
                    pe.wait_ge(kept, n + 1)
                    need(pe, projected, n + 1 - NODE_RING)
                    nc.tensor.matmul(bank[4 + b][:, 0:D], rows_t[:, b, :], out_t[:, :], start=True, stop=False)
                    nc.tensor.matmul(bank[4 + b][:, 0:D], ones_bf[:, :], out_parts, start=False, stop=True).then_inc(made, 1)

                for n in range(2):
                    transpose(n, n)
                by_ring(pe, step)


_INS = ["x", "src", "dst", "edge_attr_128",
        "L0_gnn_W1", "L0_gnn_b1", "L0_gnn_W2", "L0_gnn_b2", "L0_gnn_bn_gamma", "L0_gnn_bn_beta", "L0_gnn_bn_mean", "L0_gnn_bn_var",
        "L1_gnn_q_w", "L1_gnn_q_b", "L1_gnn_k_w", "L1_gnn_k_b", "L1_gnn_v_w", "L1_gnn_v_b", "L1_gnn_out_w", "L1_gnn_out_b",
        "L1_gnn_eb_w", "L1_gnn_eb_b"]


def kernel(**inputs):
    import numpy as _np
    import concourse.bacc as _bacc
    from concourse import mybir as _mybir
    from concourse.bass_utils import run_bass_kernel_spmd as _run

    nc = _bacc.Bacc("TRN2", target_bir_lowering=False, num_devices=1)
    arrays, args = {}, []
    for name in _INS:
        a = _np.ascontiguousarray(inputs[name])
        arrays[f"in_{name}_dram"] = a
        args.append(nc.dram_tensor(f"in_{name}_dram", a.shape, _mybir.dt.from_np(a.dtype), kind="ExternalInput").ap())
    args.append(nc.dram_tensor("out_0_dram", (N_NODES, D), F32, kind="ExternalOutput").ap())
    gnn(nc, *args)
    r = _run(nc, [arrays], core_ids=[0])
    return r.results[0]["out_0_dram"]
```
